# Optimizing a Trainium2 kernel written in Bass

```python
import numpy as np
import jax
import jax.numpy as jnp

def _softmax(x, axis=-1):
    return jax.nn.softmax(x, axis=axis)

def _gelu(x):
    return jax.nn.gelu(x, approximate=True)

def _silu(x):
    return jax.nn.silu(x)

def _sigmoid(x):
    return jax.nn.sigmoid(x)

def _layernorm(x, axis=-1, eps=1e-05):
    m = jnp.mean(x, axis=axis, keepdims=True)
    v = jnp.var(x, axis=axis, keepdims=True)
    return (x - m) / jnp.sqrt(v + eps)

def _scatter_add(tgt, idx, src, axis=0):
    return tgt.at[idx].add(src)

def _segment_sum(src, seg, n):
    return jax.ops.segment_sum(src, seg, n)
kernel_name = 'mk_decoder_postln_d2_seqx_r4_e28c3f'

def setup_inputs(seed: int=0):
    np.random.seed(seed)
    _w = jnp.asarray

    def _rec_inputs():
        import jax
        import jax.numpy as jnp
        _rk = jax.random.key(seed)
        x = -0.0002928 + 1 * jax.random.normal(jax.random.fold_in(_rk, 1), (4, 512, 256), jnp.float32)
        _lenS = 512 - jax.random.randint(jax.random.fold_in(_rk, 7), (4,), 0, max(1, 512 // 4) + 1, jnp.int32)
        _lenS2 = 512 - jax.random.randint(jax.random.fold_in(_rk, 8), (4,), 0, max(1, 512 // 4) + 1, jnp.int32)
        _ctx_1024P = jax.random.normal(jax.random.fold_in(_rk, 11), (4, 16, 256), jnp.float32)
        _ctx_1024c = jax.random.dirichlet(jax.random.fold_in(_rk, 511), 0.3 * jnp.ones((16,), jnp.float32), (4, 512))
        _ctx_1024t = jnp.einsum('bsk,bkd->bsd', _ctx_1024c, _ctx_1024P)
        _ctx_1024t = _ctx_1024t * jax.lax.rsqrt(jnp.mean(jnp.square(_ctx_1024t)) + 1e-12) * 0.953939
        ctx_1024 = -1.39393e-06 + 0.999914 * (_ctx_1024t + 0.3 * jax.random.normal(jax.random.fold_in(_rk, 611), (4, 512, 256), jnp.float32))
        return (x, ctx_1024)
    x, ctx_1024 = _rec_inputs()

    def _L0_attn_setup():
        import math
        import jax, jax.numpy as jnp
        import numpy as np
        B, S, D, H = (2, 512, 256, 16)
        HD = D // H
        LAMBDA_MAX = 0.5
        AMP_EPS = 1e-06

        def _amp_norm(t):
            a = jax.nn.softplus(t)
            return a / jnp.sqrt(jnp.mean(a * a, axis=-1, keepdims=True) + AMP_EPS)
        key = jax.random.key(seed)
        ks = jax.random.split(key, 8)
        x = jax.random.normal(ks[0], (B, S, D), jnp.float32)
        w = lambda k, std: std * jax.random.normal(k, (D, D), jnp.float32)
        return {'x': x, 'Wq': w(ks[1], 0.02), 'Wk': w(ks[2], 0.02), 'Wv': w(ks[3], 0.02), 'Wo': w(ks[4], 0.02), 'Wqp': w(ks[5], 0.005), 'Wkp': w(ks[6], 0.005), 'lambda_raw': jnp.full((H,), float(np.arctanh(0.5)), jnp.float32)}
    _L0_attn_all = _L0_attn_setup()
    _L0_attn_in = {k: v for k, v in _L0_attn_all.items() if k in ('Wq', 'Wk', 'Wv', 'Wo', 'Wqp', 'Wkp', 'lambda_raw')}
    del _L0_attn_all

    def _L0_xattn_setup():
        import jax, jax.numpy as jnp
        import numpy as np
        EPS_BACKEND = 1e-06
        NORM_EPS = 1e-06
        NUM_HEADS = 4

        def _mlstm_forward(q, k, v, ig_kernel, ig_bias, fg_kernel, fg_bias, outnorm_weight):
            B, S, E = q.shape
            NH = ig_bias.shape[0]
            DH = E // NH
            gate_input = jnp.concatenate([q, k, v], axis=-1)
            igate = gate_input @ ig_kernel + ig_bias
            fgate = gate_input @ fg_kernel + fg_bias
            qh = q.reshape(B, S, NH, DH).transpose(0, 2, 1, 3)
            kh = k.reshape(B, S, NH, DH).transpose(0, 2, 1, 3)
            vh = v.reshape(B, S, NH, DH).transpose(0, 2, 1, 3)
            ig = igate.transpose(0, 2, 1)
            fg = fgate.transpose(0, 2, 1)
            log_fg = jax.nn.log_sigmoid(fg)
            cums = jnp.concatenate([jnp.zeros((B, NH, 1), log_fg.dtype), jnp.cumsum(log_fg, axis=-1)], axis=-1)
            fg_mat = cums[..., :, None] - cums[..., None, :]
            mask = jnp.tril(jnp.ones((S + 1, S + 1), bool))
            fg_mat = jnp.where(mask, fg_mat, -jnp.inf)[..., 1:, 1:]
            log_D = fg_mat + ig[..., None, :]
            max_log_D = jnp.max(log_D, axis=-1, keepdims=True)
            D = jnp.exp(log_D - max_log_D)
            qk = jnp.einsum('bnsd,bntd->bnst', qh, kh) / jnp.sqrt(jnp.float32(DH))
            C = qk * D
            normalizer = jnp.maximum(jnp.abs(C.sum(-1, keepdims=True)), jnp.exp(-max_log_D))
            h = jnp.einsum('bnst,bntd->bnsd', C / (normalizer + EPS_BACKEND), vh)
            h = h.transpose(0, 2, 1, 3)
            mean = h.mean(-1, keepdims=True)
            var = h.var(-1, keepdims=True)
            hn = (h - mean) * jax.lax.rsqrt(var + NORM_EPS) * outnorm_weight
            return hn.reshape(B, S, E)
        key = jax.random.key(seed)
        ks = jax.random.split(key, 8)
        B, S, E, NH = (2, 512, 256, NUM_HEADS)
        DH = E // NH
        q = jax.random.normal(ks[0], (B, S, E), jnp.float32)
        k = jax.random.normal(ks[1], (B, S, E), jnp.float32)
        v = jax.random.normal(ks[2], (B, S, E), jnp.float32)
        ig_kernel = jax.random.normal(ks[3], (3 * E, NH), jnp.float32) * 0.02
        fg_kernel = jax.random.normal(ks[4], (3 * E, NH), jnp.float32) * 0.02
        ig_bias = jax.random.normal(ks[5], (NH,), jnp.float32) * 0.1
        fg_bias = jnp.linspace(3.0, 6.0, NH, dtype=jnp.float32)
        outnorm_weight = jnp.ones((NH, DH), jnp.float32)
        return {'q': q, 'k': k, 'v': v, 'ig_kernel': ig_kernel, 'ig_bias': ig_bias, 'fg_kernel': fg_kernel, 'fg_bias': fg_bias, 'outnorm_weight': outnorm_weight}
    _L0_xattn_all = _L0_xattn_setup()
    _L0_xattn_in = {k: v for k, v in _L0_xattn_all.items() if k in ('ig_kernel', 'ig_bias', 'fg_kernel', 'fg_bias', 'outnorm_weight')}
    del _L0_xattn_all

    def _L0_ffn_setup():
        import jax, jax.numpy as jnp
        import numpy as np
        DIM = 256
        INTER = 256
        E = 8
        TOPK = 2
        ROUTE_SCALE = 1.0
        SHARED_INTER = 512
        B, S = (4, 512)

        def _moe_forward(x, gate_w, gate_b, w1, b1, w3, b3, w2, b2, ws1, bs1, ws3, bs3, ws2, bs2):
            Bq, Sq, D = x.shape
            xt = x.reshape(-1, D)
            logits = (xt @ gate_w.T + gate_b).astype(jnp.float32)
            scores = jax.nn.softmax(logits, axis=-1)
            top_w, top_i = jax.lax.top_k(scores, TOPK)
            weights = (top_w * ROUTE_SCALE).astype(x.dtype)
            gate_dense = jnp.sum(jax.nn.one_hot(top_i, E, dtype=x.dtype) * weights[..., None], axis=1)

            def expert(w1e, b1e, w3e, b3e, w2e, b2e):
                h = jax.nn.silu(xt @ w1e.T + b1e) * (xt @ w3e.T + b3e)
                return h @ w2e.T + b2e
            outs = jax.vmap(expert)(w1, b1, w3, b3, w2, b2)
            y = jnp.einsum('etd,te->td', outs, gate_dense)
            z = jax.nn.silu(xt @ ws1.T + bs1) * (xt @ ws3.T + bs3) @ ws2.T + bs2
            return (y + z).reshape(Bq, Sq, D)
        key = jax.random.key(seed)
        ks = jax.random.split(key, 10)

        def w(k, shape, scale=0.02):
            return jax.random.normal(k, shape, jnp.float32) * scale
        return {'x': jax.random.normal(ks[0], (B, S, DIM), jnp.float32), 'gate_w': w(ks[1], (E, DIM)), 'gate_b': jnp.zeros((E,), jnp.float32), 'w1': w(ks[2], (E, INTER, DIM)), 'b1': jnp.zeros((E, INTER), jnp.float32), 'w3': w(ks[3], (E, INTER, DIM)), 'b3': jnp.zeros((E, INTER), jnp.float32), 'w2': w(ks[4], (E, DIM, INTER)), 'b2': jnp.zeros((E, DIM), jnp.float32), 'ws1': w(ks[5], (SHARED_INTER, DIM)), 'bs1': jnp.zeros((SHARED_INTER,), jnp.float32), 'ws3': w(ks[6], (SHARED_INTER, DIM)), 'bs3': jnp.zeros((SHARED_INTER,), jnp.float32), 'ws2': w(ks[7], (DIM, SHARED_INTER)), 'bs2': jnp.zeros((DIM,), jnp.float32)}
    _L0_ffn_all = _L0_ffn_setup()
    _L0_ffn_in = {k: v for k, v in _L0_ffn_all.items() if k in ('gate_w', 'gate_b', 'w1', 'b1', 'w3', 'b3', 'w2', 'b2', 'ws1', 'bs1', 'ws3', 'bs3', 'ws2', 'bs2')}
    del _L0_ffn_all

    def _L1_attn_setup():
        import jax, jax.numpy as jnp
        import numpy as np
        import math
        B, L, H, D, HID = (2, 256, 16, 64, 256)

        def _rope_tables(seq_len, dim):
            inv_freq = 1.0 / 10000.0 ** (jnp.arange(0, dim, 2, dtype=jnp.float32) / dim)
            t = jnp.arange(seq_len, dtype=jnp.float32)
            freqs = jnp.outer(t, inv_freq)
            emb = jnp.concatenate([freqs, freqs], -1)
            return (jnp.cos(emb), jnp.sin(emb))

        def _rotate_half(x):
            x1, x2 = jnp.split(x, 2, axis=-1)
            return jnp.concatenate([-x2, x1], axis=-1)

        def _apply_rope(x, cos, sin):
            return x * cos + _rotate_half(x) * sin

        def _forward(x, w_qkv, w_o, log_p, log_a, w1, b1, w2, b2):
            Bx, Lx, _ = x.shape
            qkv = jnp.dot(x, w_qkv).reshape(Bx, Lx, 3, H, D)
            qkv = jnp.transpose(qkv, (2, 0, 3, 1, 4))
            q, k, v = (qkv[0], qkv[1], qkv[2])
            cos, sin = _rope_tables(Lx, D)
            cos, sin = (cos[None, None], sin[None, None])
            q = _apply_rope(q, cos, sin)
            k = _apply_rope(k, cos, sin)
            scale = 1.0 / math.sqrt(D)
            scores = jnp.einsum('bhid,bhjd->bhij', q, k) * scale
            pos = jnp.arange(Lx, dtype=jnp.float32)
            dist = jnp.abs(pos[None, :] - pos[:, None])
            p = jax.nn.softplus(log_p)
            a = jax.nn.softplus(log_a)
            kerple = -p * jnp.log1p(a * dist[None])
            attn_t = jnp.transpose(scores, (0, 2, 3, 1))
            kerple_t = jnp.broadcast_to(jnp.transpose(kerple, (1, 2, 0))[None], attn_t.shape)
            combined = jnp.concatenate([attn_t, kerple_t], axis=-1)
            hdn = jax.nn.gelu(jnp.dot(combined, w1) + b1, approximate=False)
            refined = jnp.dot(hdn, w2) + b2
            refined = jnp.transpose(refined, (0, 3, 1, 2))
            scores = scores + kerple[None] + refined
            causal = jnp.tril(jnp.ones((Lx, Lx), dtype=bool))
            scores = jnp.where(causal[None, None], scores, -jnp.inf)
            weights = jax.nn.softmax(scores, axis=-1)
            out = jnp.einsum('bhij,bhjd->bhid', weights, v)
            out = jnp.transpose(out, (0, 2, 1, 3)).reshape(Bx, Lx, H * D)
            return jnp.dot(out, w_o)
        key = jax.random.key(seed)
        ks = jax.random.split(key, 8)
        s = 0.02
        return {'x': jax.random.normal(ks[0], (B, L, HID), jnp.float32), 'w_qkv': jax.random.normal(ks[1], (HID, 3 * H * D), jnp.float32) * s, 'w_o': jax.random.normal(ks[2], (H * D, HID), jnp.float32) * s, 'log_p': jax.random.normal(ks[3], (H, 1, 1), jnp.float32) * 0.02, 'log_a': jax.random.normal(ks[4], (H, 1, 1), jnp.float32) * 0.02, 'w1': jax.random.normal(ks[5], (2 * H, 2 * H), jnp.float32) * s, 'b1': jnp.zeros((2 * H,), jnp.float32), 'w2': jax.random.normal(ks[6], (2 * H, H), jnp.float32) * s, 'b2': jnp.zeros((H,), jnp.float32)}
    _L1_attn_all = _L1_attn_setup()
    _L1_attn_in = {k: v for k, v in _L1_attn_all.items() if k in ('w_qkv', 'w_o', 'log_p', 'log_a', 'w1', 'b1', 'w2', 'b2')}
    del _L1_attn_all

    def _L1_xattn_setup():
        import math
        import jax, jax.numpy as jnp
        import numpy as np
        B, S, H, NH = (2, 512, 256, 4)
        DH = H // NH

        def _mlstm_parallel(qh, kh, vh, ig, fg, eps=1e-06):
            b, nh, s, dh = qh.shape
            log_f = jax.nn.log_sigmoid(fg)
            pcs = jnp.pad(jnp.cumsum(log_f, axis=-1), ((0, 0), (0, 0), (1, 0)))
            mat = pcs[..., :, None] - pcs[..., None, :]
            ltr = jnp.tril(jnp.ones((s, s), dtype=bool))
            log_fg_matrix = jnp.where(ltr, mat[..., 1:, 1:], -jnp.inf)
            log_D = log_fg_matrix + ig[..., None, :]
            max_log_D = jnp.max(log_D, axis=-1, keepdims=True)
            D = jnp.exp(log_D - max_log_D)
            qk = jnp.einsum('bhsd,bhtd->bhst', qh, kh) / math.sqrt(dh)
            C = qk * D
            normalizer = jnp.maximum(jnp.abs(C.sum(axis=-1, keepdims=True)), jnp.exp(-max_log_D))
            Cn = C / (normalizer + eps)
            return jnp.einsum('bhst,bhtd->bhsd', Cn, vh)
        key = jax.random.key(seed)
        ks = jax.random.split(key, 8)
        gate_std = 1.0 / math.sqrt(3 * H)
        return {'q': jax.random.normal(ks[0], (B, S, H), jnp.float32), 'k': jax.random.normal(ks[1], (B, S, H), jnp.float32), 'v': jax.random.normal(ks[2], (B, S, H), jnp.float32), 'w_igate': jax.random.normal(ks[3], (NH, 3 * H), jnp.float32) * gate_std, 'b_igate': jax.random.normal(ks[4], (NH,), jnp.float32) * 0.1, 'w_fgate': jax.random.normal(ks[5], (NH, 3 * H), jnp.float32) * gate_std, 'b_fgate': jnp.linspace(3.4, 6.0, NH, dtype=jnp.float32), 'ln_weight': jnp.zeros((H,), jnp.float32)}
    _L1_xattn_all = _L1_xattn_setup()
    _L1_xattn_in = {k: v for k, v in _L1_xattn_all.items() if k in ('w_igate', 'b_igate', 'w_fgate', 'b_fgate', 'ln_weight')}
    del _L1_xattn_all

    def _L1_ffn_setup():
        import jax, jax.numpy as jnp
        import numpy as np
        B, S, H, E, F = (2, 512, 256, 8, 1024)
        key = jax.random.key(seed)
        k1, k2, k3, k4 = jax.random.split(key, 4)
        h = jax.random.normal(k1, (B, S, H), dtype=jnp.float32)
        Wr = jax.random.normal(k2, (H, E), dtype=jnp.float32) / np.sqrt(H)
        W1 = jax.random.normal(k3, (E, H, F), dtype=jnp.float32) / np.sqrt(H)
        W2 = jax.random.normal(k4, (E, F, H), dtype=jnp.float32) / np.sqrt(F)
        return {'h': h, 'Wr': Wr, 'W1': W1, 'W2': W2}
    _L1_ffn_all = _L1_ffn_setup()
    _L1_ffn_in = {k: v for k, v in _L1_ffn_all.items() if k in ('Wr', 'W1', 'W2')}
    del _L1_ffn_all
    return {'x': x, 'ctx_1024': ctx_1024, 'L0_attn_Wq': _L0_attn_in['Wq'], 'L0_attn_Wk': _L0_attn_in['Wk'], 'L0_attn_Wv': _L0_attn_in['Wv'], 'L0_attn_Wo': _L0_attn_in['Wo'], 'L0_attn_Wqp': _L0_attn_in['Wqp'], 'L0_attn_Wkp': _L0_attn_in['Wkp'], 'L0_attn_lambda_raw': _L0_attn_in['lambda_raw'], 'L0_xattn_ig_kernel': _L0_xattn_in['ig_kernel'], 'L0_xattn_ig_bias': _L0_xattn_in['ig_bias'], 'L0_xattn_fg_kernel': _L0_xattn_in['fg_kernel'], 'L0_xattn_fg_bias': _L0_xattn_in['fg_bias'], 'L0_xattn_outnorm_weight': _L0_xattn_in['outnorm_weight'], 'L0_ffn_gate_w': _L0_ffn_in['gate_w'], 'L0_ffn_gate_b': _L0_ffn_in['gate_b'], 'L0_ffn_w1': _L0_ffn_in['w1'], 'L0_ffn_b1': _L0_ffn_in['b1'], 'L0_ffn_w3': _L0_ffn_in['w3'], 'L0_ffn_b3': _L0_ffn_in['b3'], 'L0_ffn_w2': _L0_ffn_in['w2'], 'L0_ffn_b2': _L0_ffn_in['b2'], 'L0_ffn_ws1': _L0_ffn_in['ws1'], 'L0_ffn_bs1': _L0_ffn_in['bs1'], 'L0_ffn_ws3': _L0_ffn_in['ws3'], 'L0_ffn_bs3': _L0_ffn_in['bs3'], 'L0_ffn_ws2': _L0_ffn_in['ws2'], 'L0_ffn_bs2': _L0_ffn_in['bs2'], 'L1_attn_w_qkv': _L1_attn_in['w_qkv'], 'L1_attn_w_o': _L1_attn_in['w_o'], 'L1_attn_log_p': _L1_attn_in['log_p'], 'L1_attn_log_a': _L1_attn_in['log_a'], 'L1_attn_w1': _L1_attn_in['w1'], 'L1_attn_b1': _L1_attn_in['b1'], 'L1_attn_w2': _L1_attn_in['w2'], 'L1_attn_b2': _L1_attn_in['b2'], 'L1_xattn_w_igate': _L1_xattn_in['w_igate'], 'L1_xattn_b_igate': _L1_xattn_in['b_igate'], 'L1_xattn_w_fgate': _L1_xattn_in['w_fgate'], 'L1_xattn_b_fgate': _L1_xattn_in['b_fgate'], 'L1_xattn_ln_weight': _L1_xattn_in['ln_weight'], 'L1_ffn_Wr': _L1_ffn_in['Wr'], 'L1_ffn_W1': _L1_ffn_in['W1'], 'L1_ffn_W2': _L1_ffn_in['W2']}

def reference(x, ctx_1024, L0_attn_Wq, L0_attn_Wk, L0_attn_Wv, L0_attn_Wo, L0_attn_Wqp, L0_attn_Wkp, L0_attn_lambda_raw, L0_xattn_ig_kernel, L0_xattn_ig_bias, L0_xattn_fg_kernel, L0_xattn_fg_bias, L0_xattn_outnorm_weight, L0_ffn_gate_w, L0_ffn_gate_b, L0_ffn_w1, L0_ffn_b1, L0_ffn_w3, L0_ffn_b3, L0_ffn_w2, L0_ffn_b2, L0_ffn_ws1, L0_ffn_bs1, L0_ffn_ws3, L0_ffn_bs3, L0_ffn_ws2, L0_ffn_bs2, L1_attn_w_qkv, L1_attn_w_o, L1_attn_log_p, L1_attn_log_a, L1_attn_w1, L1_attn_b1, L1_attn_w2, L1_attn_b2, L1_xattn_w_igate, L1_xattn_b_igate, L1_xattn_w_fgate, L1_xattn_b_fgate, L1_xattn_ln_weight, L1_ffn_Wr, L1_ffn_W1, L1_ffn_W2):
    import jax
    import jax.numpy as jnp

    def _L0_attn_ref(x, Wq, Wk, Wv, Wo, Wqp, Wkp, lambda_raw):
        import math
        import jax, jax.numpy as jnp
        import numpy as np
        B, S, D, H = (2, 512, 256, 16)
        HD = D // H
        LAMBDA_MAX = 0.5
        AMP_EPS = 1e-06

        def _amp_norm(t):
            a = jax.nn.softplus(t)
            return a / jnp.sqrt(jnp.mean(a * a, axis=-1, keepdims=True) + AMP_EPS)
        b, s, d = x.shape
        split = lambda t: t.reshape(b, s, H, HD)
        q = split(x @ Wq)
        k = split(x @ Wk)
        v = split(x @ Wv)
        scale = 1.0 / math.sqrt(HD)
        scores_dot = jnp.einsum('bihd,bjhd->bhij', q, k) * scale
        q_amp = _amp_norm(q)
        k_amp = _amp_norm(k)
        q_phi = math.pi * jnp.tanh(split(x @ Wqp))
        k_phi = math.pi * jnp.tanh(split(x @ Wkp))
        q_cos = q_amp * jnp.cos(q_phi)
        q_sin = q_amp * jnp.sin(q_phi)
        k_cos = k_amp * jnp.cos(k_phi)
        k_sin = k_amp * jnp.sin(k_phi)
        scores_phase = (jnp.einsum('bihd,bjhd->bhij', q_cos, k_cos) + jnp.einsum('bihd,bjhd->bhij', q_sin, k_sin)) * scale
        lam = (LAMBDA_MAX * jnp.tanh(lambda_raw))[None, :, None, None]
        scores = scores_dot + lam * scores_phase
        causal = jnp.tril(jnp.ones((s, s), bool))
        scores = jnp.where(causal[None, None], scores, -jnp.inf)
        attn = jax.nn.softmax(scores, axis=-1)
        out = jnp.einsum('bhij,bjhd->bihd', attn, v).reshape(b, s, d)
        return out @ Wo

    def _L0_xattn_ref(q, k, v, ig_kernel, ig_bias, fg_kernel, fg_bias, outnorm_weight):
        import jax, jax.numpy as jnp
        import numpy as np
        EPS_BACKEND = 1e-06
        NORM_EPS = 1e-06
        NUM_HEADS = 4

        def _mlstm_forward(q, k, v, ig_kernel, ig_bias, fg_kernel, fg_bias, outnorm_weight):
            B, S, E = q.shape
            NH = ig_bias.shape[0]
            DH = E // NH
            gate_input = jnp.concatenate([q, k, v], axis=-1)
            igate = gate_input @ ig_kernel + ig_bias
            fgate = gate_input @ fg_kernel + fg_bias
            qh = q.reshape(B, S, NH, DH).transpose(0, 2, 1, 3)
            kh = k.reshape(B, S, NH, DH).transpose(0, 2, 1, 3)
            vh = v.reshape(B, S, NH, DH).transpose(0, 2, 1, 3)
            ig = igate.transpose(0, 2, 1)
            fg = fgate.transpose(0, 2, 1)
            log_fg = jax.nn.log_sigmoid(fg)
            cums = jnp.concatenate([jnp.zeros((B, NH, 1), log_fg.dtype), jnp.cumsum(log_fg, axis=-1)], axis=-1)
            fg_mat = cums[..., :, None] - cums[..., None, :]
            mask = jnp.tril(jnp.ones((S + 1, S + 1), bool))
            fg_mat = jnp.where(mask, fg_mat, -jnp.inf)[..., 1:, 1:]
            log_D = fg_mat + ig[..., None, :]
            max_log_D = jnp.max(log_D, axis=-1, keepdims=True)
            D = jnp.exp(log_D - max_log_D)
            qk = jnp.einsum('bnsd,bntd->bnst', qh, kh) / jnp.sqrt(jnp.float32(DH))
            C = qk * D
            normalizer = jnp.maximum(jnp.abs(C.sum(-1, keepdims=True)), jnp.exp(-max_log_D))
            h = jnp.einsum('bnst,bntd->bnsd', C / (normalizer + EPS_BACKEND), vh)
            h = h.transpose(0, 2, 1, 3)
            mean = h.mean(-1, keepdims=True)
            var = h.var(-1, keepdims=True)
            hn = (h - mean) * jax.lax.rsqrt(var + NORM_EPS) * outnorm_weight
            return hn.reshape(B, S, E)
        return _mlstm_forward(q, k, v, ig_kernel, ig_bias, fg_kernel, fg_bias, outnorm_weight)

    def _L0_ffn_ref(x, gate_w, gate_b, w1, b1, w3, b3, w2, b2, ws1, bs1, ws3, bs3, ws2, bs2):
        import jax, jax.numpy as jnp
        import numpy as np
        DIM = 256
        INTER = 256
        E = 8
        TOPK = 2
        ROUTE_SCALE = 1.0
        SHARED_INTER = 512
        B, S = (4, 512)

        def _moe_forward(x, gate_w, gate_b, w1, b1, w3, b3, w2, b2, ws1, bs1, ws3, bs3, ws2, bs2):
            Bq, Sq, D = x.shape
            xt = x.reshape(-1, D)
            logits = (xt @ gate_w.T + gate_b).astype(jnp.float32)
            scores = jax.nn.softmax(logits, axis=-1)
            top_w, top_i = jax.lax.top_k(scores, TOPK)
            weights = (top_w * ROUTE_SCALE).astype(x.dtype)
            gate_dense = jnp.sum(jax.nn.one_hot(top_i, E, dtype=x.dtype) * weights[..., None], axis=1)

            def expert(w1e, b1e, w3e, b3e, w2e, b2e):
                h = jax.nn.silu(xt @ w1e.T + b1e) * (xt @ w3e.T + b3e)
                return h @ w2e.T + b2e
            outs = jax.vmap(expert)(w1, b1, w3, b3, w2, b2)
            y = jnp.einsum('etd,te->td', outs, gate_dense)
            z = jax.nn.silu(xt @ ws1.T + bs1) * (xt @ ws3.T + bs3) @ ws2.T + bs2
            return (y + z).reshape(Bq, Sq, D)
        return _moe_forward(x, gate_w, gate_b, w1, b1, w3, b3, w2, b2, ws1, bs1, ws3, bs3, ws2, bs2)

    def _L1_attn_ref(x, w_qkv, w_o, log_p, log_a, w1, b1, w2, b2):
        import jax, jax.numpy as jnp
        import numpy as np
        import math
        B, L, H, D, HID = (2, 256, 16, 64, 256)

        def _rope_tables(seq_len, dim):
            inv_freq = 1.0 / 10000.0 ** (jnp.arange(0, dim, 2, dtype=jnp.float32) / dim)
            t = jnp.arange(seq_len, dtype=jnp.float32)
            freqs = jnp.outer(t, inv_freq)
            emb = jnp.concatenate([freqs, freqs], -1)
            return (jnp.cos(emb), jnp.sin(emb))

        def _rotate_half(x):
            x1, x2 = jnp.split(x, 2, axis=-1)
            return jnp.concatenate([-x2, x1], axis=-1)

        def _apply_rope(x, cos, sin):
            return x * cos + _rotate_half(x) * sin

        def _forward(x, w_qkv, w_o, log_p, log_a, w1, b1, w2, b2):
            Bx, Lx, _ = x.shape
            qkv = jnp.dot(x, w_qkv).reshape(Bx, Lx, 3, H, D)
            qkv = jnp.transpose(qkv, (2, 0, 3, 1, 4))
            q, k, v = (qkv[0], qkv[1], qkv[2])
            cos, sin = _rope_tables(Lx, D)
            cos, sin = (cos[None, None], sin[None, None])
            q = _apply_rope(q, cos, sin)
            k = _apply_rope(k, cos, sin)
            scale = 1.0 / math.sqrt(D)
            scores = jnp.einsum('bhid,bhjd->bhij', q, k) * scale
            pos = jnp.arange(Lx, dtype=jnp.float32)
            dist = jnp.abs(pos[None, :] - pos[:, None])
            p = jax.nn.softplus(log_p)
            a = jax.nn.softplus(log_a)
            kerple = -p * jnp.log1p(a * dist[None])
            attn_t = jnp.transpose(scores, (0, 2, 3, 1))
            kerple_t = jnp.broadcast_to(jnp.transpose(kerple, (1, 2, 0))[None], attn_t.shape)
            combined = jnp.concatenate([attn_t, kerple_t], axis=-1)
            hdn = jax.nn.gelu(jnp.dot(combined, w1) + b1, approximate=False)
            refined = jnp.dot(hdn, w2) + b2
            refined = jnp.transpose(refined, (0, 3, 1, 2))
            scores = scores + kerple[None] + refined
            causal = jnp.tril(jnp.ones((Lx, Lx), dtype=bool))
            scores = jnp.where(causal[None, None], scores, -jnp.inf)
            weights = jax.nn.softmax(scores, axis=-1)
            out = jnp.einsum('bhij,bhjd->bhid', weights, v)
            out = jnp.transpose(out, (0, 2, 1, 3)).reshape(Bx, Lx, H * D)
            return jnp.dot(out, w_o)
        return _forward(x, w_qkv, w_o, log_p, log_a, w1, b1, w2, b2)

    def _L1_xattn_ref(q, k, v, w_igate, b_igate, w_fgate, b_fgate, ln_weight):
        import math
        import jax, jax.numpy as jnp
        import numpy as np
        B, S, H, NH = (2, 512, 256, 4)
        DH = H // NH

        def _mlstm_parallel(qh, kh, vh, ig, fg, eps=1e-06):
            b, nh, s, dh = qh.shape
            log_f = jax.nn.log_sigmoid(fg)
            pcs = jnp.pad(jnp.cumsum(log_f, axis=-1), ((0, 0), (0, 0), (1, 0)))
            mat = pcs[..., :, None] - pcs[..., None, :]
            ltr = jnp.tril(jnp.ones((s, s), dtype=bool))
            log_fg_matrix = jnp.where(ltr, mat[..., 1:, 1:], -jnp.inf)
            log_D = log_fg_matrix + ig[..., None, :]
            max_log_D = jnp.max(log_D, axis=-1, keepdims=True)
            D = jnp.exp(log_D - max_log_D)
            qk = jnp.einsum('bhsd,bhtd->bhst', qh, kh) / math.sqrt(dh)
            C = qk * D
            normalizer = jnp.maximum(jnp.abs(C.sum(axis=-1, keepdims=True)), jnp.exp(-max_log_D))
            Cn = C / (normalizer + eps)
            return jnp.einsum('bhst,bhtd->bhsd', Cn, vh)
        b, s, h = q.shape
        nh = b_igate.shape[0]
        dh = h // nh
        gin = jnp.concatenate([q, k, v], axis=-1)
        ig = jnp.einsum('bsd,hd->bhs', gin, w_igate) + b_igate[None, :, None]
        fg = jnp.einsum('bsd,hd->bhs', gin, w_fgate) + b_fgate[None, :, None]
        qh = q.reshape(b, s, nh, dh).transpose(0, 2, 1, 3)
        kh = k.reshape(b, s, nh, dh).transpose(0, 2, 1, 3)
        vh = v.reshape(b, s, nh, dh).transpose(0, 2, 1, 3)
        hst = _mlstm_parallel(qh, kh, vh, ig, fg)
        mean = hst.mean(axis=-1, keepdims=True)
        var = hst.var(axis=-1, keepdims=True)
        hn = (hst - mean) / jnp.sqrt(var + 1e-05)
        scale = (1.0 + ln_weight).reshape(nh, dh)
        hn = hn * scale[None, :, None, :]
        return hn.transpose(0, 2, 1, 3).reshape(b, s, h)

    def _L1_ffn_ref(h, Wr, W1, W2):
        import jax, jax.numpy as jnp
        import numpy as np
        B, S, H, E, F = (2, 512, 256, 8, 1024)
        g = jax.nn.softmax(h @ Wr, axis=-1)
        top2_w, top2_idx = jax.lax.top_k(g, 2)
        top2_w = top2_w / jnp.sum(top2_w, axis=-1, keepdims=True)
        hid = jax.nn.relu(jnp.einsum('bsh,ehf->bsef', h, W1))
        expert_out = jnp.einsum('bsef,efh->bseh', hid, W2)
        top2_out = jnp.take_along_axis(expert_out, top2_idx[..., None], axis=2)
        return jnp.sum(top2_out * top2_w[..., None], axis=2)
    x = _layernorm(x + _L0_attn_ref(x, L0_attn_Wq, L0_attn_Wk, L0_attn_Wv, L0_attn_Wo, L0_attn_Wqp, L0_attn_Wkp, L0_attn_lambda_raw), axis=-1)
    x = _layernorm(x + _L0_xattn_ref(x, ctx_1024, ctx_1024, L0_xattn_ig_kernel, L0_xattn_ig_bias, L0_xattn_fg_kernel, L0_xattn_fg_bias, L0_xattn_outnorm_weight), axis=-1)
    x = _layernorm(x + _L0_ffn_ref(x, L0_ffn_gate_w, L0_ffn_gate_b, L0_ffn_w1, L0_ffn_b1, L0_ffn_w3, L0_ffn_b3, L0_ffn_w2, L0_ffn_b2, L0_ffn_ws1, L0_ffn_bs1, L0_ffn_ws3, L0_ffn_bs3, L0_ffn_ws2, L0_ffn_bs2), axis=-1)
    x = _layernorm(x + _L1_attn_ref(x, L1_attn_w_qkv, L1_attn_w_o, L1_attn_log_p, L1_attn_log_a, L1_attn_w1, L1_attn_b1, L1_attn_w2, L1_attn_b2), axis=-1)
    x = _layernorm(x + _L1_xattn_ref(x, ctx_1024, ctx_1024, L1_xattn_w_igate, L1_xattn_b_igate, L1_xattn_w_fgate, L1_xattn_b_fgate, L1_xattn_ln_weight), axis=-1)
    x = _layernorm(x + _L1_ffn_ref(x, L1_ffn_Wr, L1_ffn_W1, L1_ffn_W2), axis=-1)
    return x

_drawn_inputs = setup_inputs


def setup_inputs(seed=0):
    import zlib

    import numpy as np

    out = dict(_drawn_inputs(seed))
    spreads = {'L0_attn_lambda_raw': (0.5493061542510986, 0.6),
     'L0_xattn_outnorm_weight': (1.0, 0.2),
     'L0_ffn_gate_b': (0.0, 0.1),
     'L0_ffn_b1': (0.0, 0.532),
     'L0_ffn_b3': (0.0, 0.475),
     'L0_ffn_b2': (0.0, 0.1),
     'L0_ffn_bs1': (0.0, 0.349),
     'L0_ffn_bs3': (0.0, 0.274),
     'L0_ffn_bs2': (0.0, 0.1),
     'L1_attn_b1': (0.0, 2.0),
     'L1_attn_b2': (0.0, 2.0),
     'L1_xattn_ln_weight': (0.0, 0.1)}
    factors = {'L0_attn_Wq': 4.257,
     'L0_attn_Wk': 4.299,
     'L0_attn_Wqp': 8.0,
     'L0_attn_Wkp': 8.0,
     'L0_xattn_ig_bias': 64.0,
     'L0_ffn_w1': 2.697,
     'L0_ffn_w3': 3.33,
     'L0_ffn_w2': 3.039,
     'L1_attn_log_p': 22.936,
     'L1_attn_log_a': 38.009,
     'L1_attn_w1': 6.847,
     'L1_attn_w2': 8.0,
     'L1_xattn_b_igate': 64.0}
    for name, (base, spread) in spreads.items():
        noise = np.random.default_rng([zlib.crc32(name.encode()), seed]).standard_normal(out[name].shape)
        drawn = base * np.exp(spread * noise) if base else spread * noise
        out[name] = jnp.asarray(drawn.astype(out[name].dtype))
    for name, factor in factors.items():
        out[name] = (out[name] * factor).astype(out[name].dtype)
    return out
```

```python
import math
from contextlib import ExitStack, contextmanager

import numpy as np
import concourse.bass as bass
from concourse import mybir

F32 = mybir.dt.float32
BF16 = mybir.dt.bfloat16
ALU = mybir.AluOpType
ACT = mybir.ActivationFunctionType
AX = mybir.AxisListType

P = 128
B, S, D = 4, 512, 256
TT = S // P
DC = D // P
NEG = -1e30

H0, HD0 = 16, 16
HS0 = 64
NH, DH = 4, 64
E0, I0 = 8, 256
E0A = 10
H1, HD1 = 16, 64
E1, F1 = 8, 1024
JG = 32

FIRST_SEM = 120

LAYERS = 6


def free(ap, *dims):
    return bass.AP(ap.tensor, ap.offset, [list(ap.ap[0])] + [list(d) for d in dims])


def absolute(dve, out, x):
    return dve.scalar_tensor_tensor(out=out, in0=x, scalar=-1.0, in1=x, op0=ALU.mult, op1=ALU.max)


class Own:

    def __init__(self, sem):
        self.sem, self.n = sem, 0

    def __call__(self, eng, ins):
        self.n += 1
        ins.then_inc(self.sem, 1)
        eng.wait_ge(self.sem, self.n)


class Arena:

    def __init__(self, base, size):
        self.base, self.size, self.at = base, size, 0

    def take(self, *dims):
        n = int(np.prod(dims))
        a = self.base[:, self.at:self.at + n]
        self.at += n
        assert self.at <= self.size, (self.at, self.size)
        if len(dims) == 2:
            return a.rearrange("p (a b) -> p a b", a=dims[0])
        if len(dims) == 3:
            return a.rearrange("p (a b c) -> p a b c", a=dims[0], b=dims[1])
        if len(dims) == 4:
            return a.rearrange("p (a b c d) -> p a b c d", a=dims[0], b=dims[1], c=dims[2])
        return a


class Core:

    def __init__(self, nc, ctx, dram):
        self.nc, self.ctx, self.dram = nc, ctx, dram
        sb = self.sb
        self.ident = sb("ident", [P, P])
        self.ident_bf = sb("ident_bf", [P, P], BF16)
        self.mask_bf = sb("mask_bf", [P, P], BF16)
        self.maskT_bf = sb("maskT_bf", [P, P], BF16)
        self.X = sb("X", [P, TT, D])
        self.XT = sb("XT", [P, DC, S])
        self.CV = sb("CV", [P, TT, NH, DH + 1])
        self.CX = sb("CX", [P, TT, D])
        self.CT = sb("CT", [P, DC, S])
        self.R = sb("R", [P, TT, D])
        self.stats = sb("stats", [P, TT, 6])
        self.mv = sb("mv", [P, TT, 2])
        self.rstd = sb("rstd", [P, TT])
        self.mhalf = sb("mhalf", [P, 16])
        self.halfpi = sb("halfpi", [P, 1])
        self.ones = sb("ones", [NH, S])
        self.zero_bf = sb("zero_bf", [P, S], BF16)
        self.WA = sb("WA", [P, DC, 5 * D])
        self.WOA = sb("WOA", [P, DC, D])
        self.lam = sb("lam", [P, H0])
        self.gate = [sb(f"gate{i}", [P, 6, 2 * NH]) for i in range(2)]
        self.gate_bias = [sb(f"gate_bias{i}", [NH, 2]) for i in range(2)]
        self.norm_w = [sb(f"norm_w{i}", [P, D]) for i in range(2)]
        self.sel = sb("sel", [NH, NH, P])
        self.WR0 = sb("WR0", [P, DC, E0])
        self.rb0 = sb("rb0", [P, E0])
        self.WR1 = sb("WR1", [P, DC, E1])
        self.B2 = sb("B2", [E0A, D])
        self.tri = sb("tri", [P, E0, E0])
        self.rope = sb("rope", [P, TT, 2, HD1])
        self.W1S = sb("W1S", [P, 2, P])
        self.W2B = sb("W2B", [P, 64])
        self.TB = sb("TB", [P, 640])
        self.KF = sb("KF", [P, S, H1])
        self.WO1 = sb("WO1", [P, 8, D])
        size = 28600
        self.work = sb("work", [P, size])
        self.size = size
        self.ps = [ctx.enter_context(nc.psum_tensor(f"ps{i}", [P, 512], F32)) for i in range(8)]

    def sb(self, name, shape, dt=F32):
        return self.ctx.enter_context(self.nc.sbuf_tensor(name, shape, dt))

    def sem(self, name):
        s = self.sem_ctx.enter_context(self.nc.semaphore(name, num=FIRST_SEM + len(self.sems)))
        self.sems.append(s)
        return s

    @contextmanager
    def semaphores(self):
        with ExitStack() as self.sem_ctx:
            self.sems = []
            self.own_dve = Own(self.sem("dve_own"))
            self.own_act = Own(self.sem("act_own"))
            self.own_pool = Own(self.sem("pool_own"))
            yield
            self.nc.all_engine_barrier(sems_to_clear=range(FIRST_SEM, FIRST_SEM + len(self.sems)))

    def arena(self):
        return Arena(self.work, self.size)



class Norm:

    def __init__(self, core, name, eps=1e-5):
        self.c, self.eps = core, eps
        self.var_ready = core.sem(f"{name}_var_ready")
        self.rstd_ready = core.sem(f"{name}_rstd_ready")
        self.x_ready = core.sem(f"{name}_x_normed")

    def stats(self, dve, t, y):
        c = self.c
        c.own_dve(dve, dve.tensor_tensor(c.R[:, t, :], y, c.X[:, t, :], ALU.add))
        c.own_dve(dve, dve.bn_stats(c.stats[:, t, :], c.R[:, t, :]))
        dve.bn_aggr(c.mv[:, t, :], c.stats[:, t, :]).then_inc(self.var_ready, 1)

    def pool(self, pool, t):
        c = self.c
        pool.wait_ge(self.var_ready, t + 1)
        c.own_pool(pool, pool.tensor_scalar(c.rstd[:, t:t + 1], c.mv[:, t, 1:2], self.eps, None, ALU.add))
        pool.tensor_tensor(c.rstd[:, t:t + 1], c.rstd[:, t:t + 1], c.mhalf[:, 0:1],
                           ALU.pow).then_inc(self.rstd_ready, 1)

    def apply(self, dve, t):
        c = self.c
        dve.wait_ge(self.rstd_ready, t + 1)
        dve.tensor_scalar(c.X[:, t, :], c.R[:, t, :], c.mv[:, t, 0:1], c.rstd[:, t:t + 1],
                          ALU.subtract, ALU.mult).then_inc(self.x_ready, 1)


class Turn:

    def __init__(self, core, name, src, dst, banks=(0, 1)):
        self.c, self.src, self.dst, self.banks = core, src, dst, banks
        self.turned = core.sem(f"{name}_x_turned")
        self.ready = core.sem(f"{name}_feature_major")

    def pe(self, pe):
        c = self.c
        for k in range(DC):
            for t in range(TT):
                last = pe.transpose(c.ps[self.banks[k]][:, t * P:(t + 1) * P], self.src(t, k), c.ident[:, :])
            last.then_inc(self.turned, 1)

    def dve(self, dve):
        dve.wait_ge(self.turned, 1)
        dve.tensor_copy(self.dst[:, 0, :], self.c.ps[self.banks[0]][:, :]).then_inc(self.ready, 1)

    def act(self, act):
        act.wait_ge(self.turned, 2)
        act.copy(self.dst[:, 1, :], self.c.ps[self.banks[1]][:, :]).then_inc(self.ready, 1)


def turn_x(core, name):
    return Turn(core, name, lambda t, k: core.X[:, t, k * P:(k + 1) * P], core.XT)



def setup(core):
    nc, d = core.nc, core.dram
    a = core.arena()
    par = a.take(3, H1)
    sp = a.take(6, H1)
    col = a.take(4)
    spc = a.take(8)
    dist_c = a.take(640)
    dist_r = a.take(S)
    maskf, maskTf = a.take(P), a.take(P)
    w1k = a.take(P)
    lamr = a.take(H0)
    lam1 = a.take(H0)
    loaded = core.sem("constants_loaded")
    p_ready = core.sem("softplus_ready")
    kerple_ready = core.sem("kerple_ready")
    kcol_ready = core.sem("kerple_column_ready")
    tb_ready = core.sem("table_product_ready")
    lam_t = core.sem("lambda_tanh")
    loads = [
        (core.ident[:, :], d["ident"]), (maskTf, d["maskT"]), (core.WA[:, :, :], d["wa"].rearrange("(c p) n -> p c n", p=P)),
        (core.WOA[:, :, :], d["woa"].rearrange("(c p) n -> p c n", p=P)), (lamr, d["lambda"].partition_broadcast(P)),
        (core.sel[:, :, :], d["sel"]), (core.tri[:, :, :], d["tri"]), (core.rope[:, :, :, :], d["rope"]),
        (core.WR0[:, :, :], d["wr0"].rearrange("(c p) n -> p c n", p=P)), (core.rb0[:, :], d["rb0"].partition_broadcast(P)),
        (core.WR1[:, :, :], d["wr1"].rearrange("(c p) n -> p c n", p=P)), (core.B2[:, :], d["b2"]),
        (core.W1S[:, :, :], d["w1s"]), (w1k[0:64, :], d["w1k"]), (core.W2B[:, :], d["w2b"]),
        (core.WO1[:, :, :], d["wo1"].rearrange("(c p) n -> p c n", p=P)),
        (par[:, 0, :], d["log_p"].partition_broadcast(P)), (par[:, 1, :], d["log_a"].partition_broadcast(P)),
        (par[:, 2, :], d["b2a"].partition_broadcast(P)), (col[0:64, 0:2], d["pa_col"]), (col[:, 2:3], d["b1_col"]),
        (dist_c[0:64, :], d["dist_c"]), (dist_r, d["dist_r"]), (maskf, d["mask"]),
    ]
    for i in range(2):
        loads += [(core.gate[i][:, :, :], d[f"gate{i}"].rearrange("(c p) n -> p c n", p=P)),
                  (core.gate_bias[i][:, :], d[f"gate_bias{i}"]),
                  (core.norm_w[i][:, :], d[f"norm_w{i}"].partition_broadcast(P))]
    n_loads = 16 * len(loads)

    with nc.Block() as block:
        @block.sync
        def _(sp_):
            for dst, src in loads:
                sp_.dma_start(dst, src).then_inc(loaded, 16)
            sp_.wait_ge(loaded, n_loads)

        @block.scalar
        def _(act):
            own = core.own_act
            act.wait_ge(loaded, n_loads)
            act.activation(lam1, lamr, ACT.Tanh).then_inc(lam_t, 1)
            act.wait_ge(p_ready, 2)
            own(act, act.activation(sp[:, 2:4, :], sp[:, 0:2, :], ACT.Exp, scale=-1.0))
            own(act, act.activation(spc[0:64, 2:4], spc[0:64, 0:2], ACT.Exp, scale=-1.0))
            own(act, act.activation(sp[:, 4:6, :], sp[:, 2:4, :], ACT.Ln, bias=1.0))
            act.activation(spc[0:64, 4:6], spc[0:64, 2:4], ACT.Ln, bias=1.0).then_inc(kcol_ready, 1)
            act.wait_ge(p_ready, 5)
            act.activation(core.KF[:, :, :], core.KF[:, :, :], ACT.Ln, bias=1.0).then_inc(kerple_ready, 1)
            act.activation(dist_c[0:64, :], dist_c[0:64, :], ACT.Ln, bias=1.0,
                           scale=spc[0:64, 7:8]).then_inc(kerple_ready, 1)

        @block.vector
        def _(dve):
            own = core.own_dve
            dve.memset(core.mhalf[:, :], -0.5)
            dve.memset(core.ones[:, :], 1.0)
            dve.memset(core.zero_bf[:, :], 0.0)
            dve.memset(core.halfpi[:, :], math.pi / 2)
            dve.wait_ge(loaded, n_loads)
            dve.tensor_copy(core.ident_bf[:, :], core.ident[:, :])
            dve.tensor_copy(core.mask_bf[:, :], maskf)
            dve.tensor_copy(core.maskT_bf[:, :], maskTf)
            absolute(dve, sp[:, 0:2, :], par[:, 0:2, :]).then_inc(p_ready, 1)
            absolute(dve, spc[0:64, 0:2], col[0:64, 0:2]).then_inc(p_ready, 1)
            dve.tensor_scalar(core.norm_w[1][:, :], core.norm_w[1][:, :], 1.0, None, ALU.add)
            dve.wait_ge(lam_t, 1)
            dve.tensor_scalar(core.lam[:, :], lam1, 0.5 / math.sqrt(HD0), None, ALU.mult)
            dve.wait_ge(kcol_ready, 1)
            own(dve, dve.scalar_tensor_tensor(out=sp[:, 0:2, :], in0=par[:, 0:2, :], scalar=0.0, in1=sp[:, 4:6, :],
                                              op0=ALU.max, op1=ALU.add))
            dve.scalar_tensor_tensor(out=spc[0:64, 6:8], in0=col[0:64, 0:2], scalar=0.0, in1=spc[0:64, 4:6],
                                     op0=ALU.max, op1=ALU.add).then_inc(p_ready, 1)
            dve.wait_ge(p_ready, 3)
            dve.tensor_scalar(spc[0:64, 0:1], spc[0:64, 6:7], -1.0, None, ALU.mult).then_inc(p_ready, 1)
            dve.tensor_tensor(core.KF[:, :, :], free(dist_r, (1, S), (0, H1)), free(sp[:, 1, :], (0, S), (1, H1)),
                              ALU.mult).then_inc(p_ready, 1)
            dve.wait_ge(kerple_ready, 2)
            dve.tensor_scalar(dist_c[0:64, :], dist_c[0:64, :], spc[0:64, 0:1], None, ALU.mult).then_inc(kcol_ready, 1)
            own(dve, dve.tensor_tensor(core.KF[:, :, :], core.KF[:, :, :], free(sp[:, 0, :], (0, S), (1, H1)), ALU.mult))
            own(dve, dve.tensor_tensor(core.KF[:, :, :], free(par[:, 2, :], (0, S), (1, H1)), core.KF[:, :, :],
                                       ALU.subtract))
            dve.tensor_tensor(core.KF[:, S - P:S, :], core.KF[:, S - P:S, :], free(maskf, (1, P), (0, H1)), ALU.add)
            dve.wait_ge(tb_ready, 1)
            dve.tensor_scalar(core.TB[:, 0:512], core.ps[0][:, :], col[:, 2:3], None, ALU.add)
            dve.tensor_scalar(core.TB[:, 512:640], core.ps[1][:, 0:128], col[:, 2:3], None, ALU.add)

        @block.tensor
        def _(pe):
            pe.wait_ge(kcol_ready, 2)
            pe.wait_ge(loaded, n_loads)
            pe.matmul(core.ps[0][:, :], w1k[0:64, :], dist_c[0:64, 0:512], start=True, stop=True)
            pe.matmul(core.ps[1][:, 0:128], w1k[0:64, :], dist_c[0:64, 512:640], start=True,
                      stop=True).then_inc(tb_ready, 1)



def phase_attention(core, b):
    nc, ps = core.nc, core.ps
    a = core.arena()
    QT, KT = a.take(8, S), a.take(8, S)
    RAW, AMP = a.take(TT, 2 * D), a.take(TT, 2 * D)
    TH, SN, CS = a.take(TT, 2 * D), a.take(TT, 2 * D), a.take(TT, 2 * D)
    V = a.take(TT, D)
    Q3 = a.take(2, 2, H0, HS0)
    SQ = a.take(2, 2 * D)
    SS = a.take(TT, 2 * H0)
    RN = a.take(TT, 2 * H0)
    a2 = Arena(core.work, core.size)
    a2.take(16 * S)
    PR, PTS = a2.take(3, S), a2.take(2, S)
    NM, DEN, RD = a2.take(64), a2.take(64), a2.take(64)
    O, OT = a2.take(TT, D), a2.take(DC, S)
    assert a2.at <= 16 * S + 5 * TT * 2 * D

    x_in = core.sem("a_x_loaded")
    ctx_in = core.sem("a_context_loaded")
    turn = turn_x(core, "a")
    proj = core.sem("a_projected")
    raw = core.sem("a_raw_ready")
    tanh = core.sem("a_tanh_ready")
    absph = core.sem("a_abs_phase_ready")
    absraw = core.sem("a_abs_raw_ready")
    sin = core.sem("a_sin_cos_ready")
    lnp = core.sem("a_log1p_ready")
    ssq = core.sem("a_square_sums_ready")
    rn = core.sem("a_amp_norm_ready")
    zeroed = core.sem("a_zeroed")
    q3raw = core.sem("a_q3_raw_ready")
    q3 = core.sem("a_q3_ready")
    tp = core.sem("a_turned")
    ev = (core.sem("a_qk_copied_even"), core.sem("a_qk_copied_odd"))
    sc = core.sem("a_scores_ready")
    mx = core.sem("a_max_ready")
    ex = core.sem("a_probs_ready")
    tr = core.sem("a_probs_turned")
    pt = core.sem("a_probsT_ready")
    pv = core.sem("a_pv_done")
    on = core.sem("a_out_ready")
    ot = core.sem("a_out_turned")
    otr = core.sem("a_outT_ready")
    y = core.sem("a_y_ready")
    norm = Norm(core, "a")
    steps = [(h, it) for h in range(H0) for it in range(TT)]
    N = len(steps)
    PROJ = [2, 5]
    SB, PB = (0, 1, 2), (3, 4)
    OB = lambda it: ps[5 + it // 2][:, (it % 2) * D:(it % 2 + 1) * D]
    YB = lambda t: ps[(2, 3, 4, 7)[t]][:, 0:D]

    with nc.Block() as block:
        @block.sync
        def _(sp):
            sp.dma_start(core.X[:, :, :], core.dram["x"][b].rearrange("(t p) d -> p t d", p=P)).then_inc(x_in, 16)
            sp.dma_start(core.CX[:, :, :], core.dram["ctx"][b].rearrange("(t p) d -> p t d", p=P)).then_inc(ctx_in, 16)
            for t in range(TT):
                sp.dma_start(core.CV[:, t, :, 0:DH], core.dram["ctx"][b, t * P:(t + 1) * P, :].rearrange(
                    "p (h d) -> p h d", h=NH)).then_inc(ctx_in, 16)
            sp.wait_ge(ctx_in, 16 * (TT + 1))

        @block.gpsimd
        def _(pool):
            pool.memset(core.CV[:, :, :, DH:DH + 1], 1.0)
            pool.memset(Q3[:, :, :, :, 48:64], 0.0).then_inc(zeroed, 1)
            for t in range(TT):
                pool.wait_ge(raw, t + 1)
                if t >= 2:
                    pool.wait_ge(tp, 4 * (t - 1))
                src = RAW[:, t, :].rearrange("p (s h d) -> p s h d", s=2, h=H0)
                pool.tensor_copy(Q3[:, t % 2, 0, :, 0:16], src[:, 0])
                pool.tensor_scalar(Q3[:, t % 2, 1, :, 0:16], src[:, 1], 1.0 / math.sqrt(HD0), None,
                                   ALU.mult).then_inc(q3raw, 1)
            for t in range(TT):
                norm.pool(pool, t)

        @block.tensor
        def _(pe):
            pe.wait_ge(x_in, 16)
            turn.pe(pe)
            pe.wait_ge(turn.ready, 2)
            for t in range(TT):
                if t >= 2:
                    pe.wait_ge(raw, t - 1)
                    pe.wait_ge(tanh, t - 1)
                for i, w in enumerate((512, 512, 256)):
                    for k in range(DC):
                        last = pe.matmul(ps[PROJ[t % 2] + i][:, 0:w], core.XT[:, k, t * P:(t + 1) * P],
                                         core.WA[:, k, 512 * i:512 * i + w], start=(k == 0), stop=(k == DC - 1))
                last.then_inc(proj, 1)
            for t in range(TT):
                pe.wait_ge(q3, t + 1)
                for i in range(4):
                    n = 4 * t + i
                    if n >= 4:
                        pe.wait_ge(ev[n % 2], (n - 4) // 2 + 1)
                    for j in range(4):
                        pair = 4 * (i % 2) + j
                        last = pe.transpose(ps[n % 4][:, j * P:(j + 1) * P],
                                            Q3[:, t % 2, i // 2, 2 * pair:2 * pair + 2, :], core.ident[:, :])
                    last.then_inc(tp, 1)

            def scores(n):
                h, it = steps[n]
                if n >= 3:
                    pe.wait_ge(ex, n - 2)
                r = 64 * (h % 2)
                w = (it + 1) * P
                pe.matmul(ps[SB[n % 3]][:, 0:w], QT[r:r + 48, h // 2, it * P:w], KT[r:r + 48, h // 2, 0:w],
                          start=True, stop=False)
                pe.matmul(ps[SB[n % 3]][:, w - P:w], core.ident_bf[:, :], core.mask_bf[:, :],
                          start=False, stop=True).then_inc(sc, 1)

            def turn_probs(n):
                _, it = steps[n]
                pe.wait_ge(ex, n + 1)
                if n >= 2:
                    pe.wait_ge(pt, n - 1)
                for j in range(it + 1):
                    last = pe.transpose(ps[PB[n % 2]][:, j * P:(j + 1) * P], PR[:, n % 3, j * P:(j + 1) * P],
                                        core.ident[:, :])
                last.then_inc(tr, 1)

            def values(n):
                h, it = steps[n]
                pe.wait_ge(pt, n + 1)
                for j in range(it + 1):
                    last = pe.matmul(OB(it)[:, h * HD0:(h + 1) * HD0], PTS[:, n % 2, j * P:(j + 1) * P],
                                     V[:, j, h * HD0:(h + 1) * HD0], start=(j == 0), stop=(j == it))
                last.then_inc(pv, 1)

            for e in range(2):
                pe.wait_ge(ev[e], 8)
            scores(0)
            scores(1)
            for n in range(N + 1):
                if n + 2 < N:
                    scores(n + 2)
                if n < N:
                    turn_probs(n)
                if n >= 1:
                    values(n - 1)
            pe.wait_ge(on, TT)
            for k in range(DC):
                for t in range(TT):
                    last = pe.transpose(ps[k][:, t * P:(t + 1) * P], O[:, t, k * P:(k + 1) * P], core.ident[:, :])
            last.then_inc(ot, 1)
            pe.wait_ge(otr, 1)
            for t in range(TT):
                for k in range(DC):
                    last = pe.matmul(YB(t), OT[:, k, t * P:(t + 1) * P], core.WOA[:, k, :],
                                     start=(k == 0), stop=(k == DC - 1))
                last.then_inc(y, 1)

        @block.scalar
        def _(act):
            turn.act(act)
            for t in range(TT):
                act.wait_ge(proj, t + 1)
                act.activation(TH[:, t, :], ps[PROJ[t % 2] + 1][:, :], ACT.Tanh).then_inc(tanh, 1)
            for t in range(TT):
                act.wait_ge(tanh, t + 1)
                act.activation(SN[:, t, :], TH[:, t, :], ACT.Sin, scale=math.pi)
                act.wait_ge(absph, t + 1)
                act.activation(CS[:, t, :], CS[:, t, :], ACT.Sin, scale=-math.pi,
                               bias=core.halfpi[:, :]).then_inc(sin, 1)
            for t in range(TT):
                act.wait_ge(absraw, t + 1)
                core.own_act(act, act.activation(AMP[:, t, :], AMP[:, t, :], ACT.Exp, scale=-1.0))
                act.activation(AMP[:, t, :], AMP[:, t, :], ACT.Ln, bias=1.0).then_inc(lnp, 1)
            for t in range(TT):
                act.wait_ge(ssq, t + 1)
                core.own_act(act, act.activation(RN[:, t, :], SS[:, t, :], ACT.Ln))
                act.activation(RN[:, t, :], RN[:, t, :], ACT.Exp, scale=-0.5).then_inc(rn, 1)
            for n in range(1, 16, 2):
                act.wait_ge(tp, n + 1)
                t, i = n // 4, n % 4
                dst = (QT if i < 2 else KT)[:, 4 * (i % 2):4 * (i % 2) + 4, t * P:(t + 1) * P]
                act.copy(dst, ps[n % 4][:, :].rearrange("p (a b) -> p a b", a=4)).then_inc(ev[1], 1)
            for n in range(N):
                w = (steps[n][1] + 1) * P
                act.wait_ge(mx, n + 1)
                if n >= 3:
                    act.wait_ge(tr, n - 2)
                act.activation(PR[:, n % 3, 0:w], ps[SB[n % 3]][:, 0:w], ACT.Exp, bias=NM[:, n:n + 1],
                               accum_out=DEN[:, n:n + 1]).then_inc(ex, 1)

        @block.vector
        def _(dve):
            own = core.own_dve
            turn.dve(dve)
            for t in range(TT):
                dve.wait_ge(proj, t + 1)
                dve.tensor_copy(V[:, t, :], ps[PROJ[t % 2] + 2][:, 0:D])
                dve.tensor_copy(RAW[:, t, :], ps[PROJ[t % 2]][:, :]).then_inc(raw, 1)
            for t in range(TT):
                dve.wait_ge(tanh, t + 1)
                absolute(dve, CS[:, t, :], TH[:, t, :]).then_inc(absph, 1)
            dve.wait_ge(raw, TT)
            for t in range(TT):
                absolute(dve, AMP[:, t, :], RAW[:, t, :]).then_inc(absraw, 1)
            for t in range(TT):
                dve.wait_ge(lnp, t + 1)
                own(dve, dve.scalar_tensor_tensor(out=AMP[:, t, :], in0=RAW[:, t, :], scalar=0.0, in1=AMP[:, t, :],
                                                  op0=ALU.max, op1=ALU.add))
                own(dve, dve.tensor_tensor(SQ[:, t % 2, :], AMP[:, t, :], AMP[:, t, :], ALU.mult))
                own(dve, dve.tensor_reduce(SS[:, t, :], SQ[:, t % 2, :].rearrange("p (h d) -> p h d", d=HD0),
                                           AX.X, ALU.add))
                dve.tensor_scalar(SS[:, t, :], SS[:, t, :], 1.0 / HD0, 1e-6, ALU.mult, ALU.add).then_inc(ssq, 1)
            dve.wait_ge(zeroed, 1)
            for t in range(TT):
                dve.wait_ge(rn, t + 1)
                own(dve, dve.tensor_tensor(RN[:, t, H0:], RN[:, t, H0:], core.lam[:, :], ALU.mult))
                amp = AMP[:, t, :].rearrange("p (h d) -> p h d", d=HD0)
                own(dve, dve.tensor_tensor(amp, amp, free(RN[:, t, :], (1, 2 * H0), (0, HD0)), ALU.mult))
                dve.wait_ge(sin, t + 1)
                if t >= 2:
                    dve.wait_ge(tp, 4 * (t - 1))
                dve.wait_ge(q3raw, t + 1)
                q = Q3[:, t % 2].rearrange("p s h d -> p (s h) d")
                dve.tensor_tensor(q[:, :, 16:32], amp, CS[:, t, :].rearrange("p (h d) -> p h d", d=HD0), ALU.mult)
                dve.tensor_tensor(q[:, :, 32:48], amp, SN[:, t, :].rearrange("p (h d) -> p h d", d=HD0),
                                  ALU.mult).then_inc(q3, 1)
                for n in range(4 * t, 4 * t + 4, 2):
                    dve.wait_ge(tp, n + 1)
                    i = n % 4
                    dst = (QT if i < 2 else KT)[:, 4 * (i % 2):4 * (i % 2) + 4, t * P:(t + 1) * P]
                    dve.tensor_copy(dst, ps[n % 4][:, :].rearrange("p (a b) -> p a b", a=4)).then_inc(ev[0], 1)

            for n in range(N + 1):
                if n < N:
                    w = (steps[n][1] + 1) * P
                    dve.wait_ge(sc, n + 1)
                    dve.tensor_reduce(NM[:, n:n + 1], ps[SB[n % 3]][:, 0:w], AX.X, ALU.max,
                                      negate=True).then_inc(mx, 1)
                if n >= 1:
                    m = n - 1
                    w = (steps[m][1] + 1) * P
                    dve.wait_ge(tr, m + 1)
                    if m >= 2:
                        dve.wait_ge(pv, m - 1)
                    dve.tensor_copy(PTS[:, m % 2, 0:w], ps[PB[m % 2]][:, 0:w]).then_inc(pt, 1)
            dve.wait_ge(ex, N)
            own(dve, dve.reciprocal(RD, DEN))
            dve.wait_ge(pv, N)
            for it in range(TT):
                dve.tensor_tensor(O[:, it, :].rearrange("p (h d) -> p h d", h=H0),
                                  OB(it).rearrange("p (h d) -> p h d", h=H0),
                                  free(RD[:, it:it + 1], (TT, H0), (0, HD0)), ALU.mult).then_inc(on, 1)
            dve.wait_ge(ot, 1)
            dve.tensor_copy(OT[:, 0, :], ps[0][:, :])
            dve.tensor_copy(OT[:, 1, :], ps[1][:, :]).then_inc(otr, 1)
            for t in range(TT):
                dve.wait_ge(y, t + 1)
                norm.stats(dve, t, YB(t))
            for t in range(TT):
                norm.apply(dve, t)



def mlstm(core, which, name, head_eps, prefetch):
    nc, ps = core.nc, core.ps
    a = core.arena()
    FG, AF, LF, IG = a.take(S), a.take(S), a.take(S), a.take(S)
    CUM, A, M, NMR, NL = a.take(S), a.take(S), a.take(S), a.take(S), a.take(S)
    AT, EN = a.take(16), a.take(16)
    DD = a.take(2, S)
    CC = a.take(2, 10 * P)
    DN, RD = a.take(16), a.take(16)
    HH = Arena(core.work, core.size).take(TT, NH, DH)
    ST, MV, RS = a.take(16, 6), a.take(16, 2), a.take(16)
    assert a.at <= W0_AT
    offs = [0, 4 * P, 7 * P, 9 * P]

    turn = turn_x(core, name)
    first = which == 0
    if first:
        turn_c = Turn(core, name + "_ctx",
                      lambda t, k: core.CX[:, t, k * P:(k + 1) * P], core.CT, banks=(2, 3))
    gates = core.sem(name + "_gates_ready")
    absf = core.sem(name + "_abs_f_ready")
    lnf = core.sem(name + "_log1p_ready")
    rows = core.sem(name + "_gate_rows_ready")
    cols = core.sem(name + "_gate_columns_turned")
    at = core.sem(name + "_columns_ready")
    en = core.sem(name + "_exp_neg_max_ready")
    nm = core.sem(name + "_neg_max_spread")
    qk = core.sem(name + "_qk_ready")
    dd = core.sem(name + "_decay_ready")
    cc = core.sem(name + "_c_ready")
    pv = core.sem(name + "_values_done")
    hv = core.sem(name + "_head_var_ready")
    hr = core.sem(name + "_head_rstd_ready")
    norm = Norm(core, name)

    with nc.Block() as block:
        @block.sync
        def _(sp):
            prefetch(sp)

        @block.gpsimd
        def _(pool):
            pool.wait_ge(hv, 1)
            core.own_pool(pool, pool.tensor_scalar(RS, MV[:, :, 1], head_eps, None, ALU.add))
            pool.tensor_tensor(RS, RS, core.mhalf[:, 0:16], ALU.pow).then_inc(hr, 1)
            for t in range(TT):
                norm.pool(pool, t)

        @block.tensor
        def _(pe):
            turn.pe(pe)
            if first:
                turn_c.pe(pe)
                pe.wait_ge(turn_c.ready, 2)
            pe.wait_ge(turn.ready, 2)
            for g in range(2):
                for c in range(6):
                    rhs = core.XT[:, c, :] if c < 2 else core.CT[:, c % 2, :]
                    last = pe.matmul(ps[4 + g][0:NH, :], core.gate[which][:, c, NH * g:NH * (g + 1)], rhs,
                                     start=(c == 0), stop=(c == 5))
            last.then_inc(gates, 1)
            pe.wait_ge(rows, 1)
            for i, src in enumerate((A, NL)):
                for t in range(TT):
                    last = pe.transpose(ps[6 + i][:, 4 * t:4 * t + 4], src[0:NH, t * P:(t + 1) * P],
                                        core.ident[0:NH, 0:NH])
            last.then_inc(cols, 1)
            pe.wait_ge(at, 1)
            pe.wait_ge(en, 1)

            def spread(h):
                if h >= 1:
                    pe.wait_ge(dd, 4 * h)
                pe.matmul(ps[4][:, :], core.sel[:, h, :], NMR[0:NH, :], start=True, stop=True)
                pe.matmul(ps[5][:, :], core.sel[:, h, :], NMR[0:NH, :], start=True, stop=False)
                pe.matmul(ps[5][:, :], core.ident_bf[:, :], free(core.maskT_bf[:, :], (0, TT), (1, P)),
                          start=False, stop=True).then_inc(nm, 1)

            def scores(h):
                r = 64 * (h % 2)
                for j in range(TT):
                    m = 4 * h + j
                    if m >= 2:
                        pe.wait_ge(cc, m - 1)
                    pe.matmul(ps[6 + m % 2][:, j * P:S], core.CT[r:r + 64, h // 2, j * P:(j + 1) * P],
                              core.XT[r:r + 64, h // 2, j * P:S], start=True, stop=True).then_inc(qk, 1)

            def values(h):
                pe.wait_ge(cc, 4 * (h + 1))
                for it in range(TT):
                    for j in range(it + 1):
                        o = offs[j] + (it - j) * P
                        last = pe.matmul(ps[it][:, h * (DH + 1):(h + 1) * (DH + 1)], CC[:, h % 2, o:o + P],
                                         core.CV[:, j, h, :], start=(j == 0), stop=(j == it))
                last.then_inc(pv, 1)

            for h in range(NH):
                spread(h)
                scores(h)
                if h >= 1:
                    values(h - 1)
            values(NH - 1)

        @block.scalar
        def _(act):
            turn.act(act)
            if first:
                turn_c.act(act)
            act.wait_ge(absf, 1)
            core.own_act(act, act.activation(AF[0:NH, :], AF[0:NH, :], ACT.Exp, scale=-1.0))
            act.activation(AF[0:NH, :], AF[0:NH, :], ACT.Ln, bias=1.0).then_inc(lnf, 1)
            act.wait_ge(cols, 1)
            act.activation(EN, ps[7][:, 0:16], ACT.Exp).then_inc(en, 1)
            act.wait_ge(at, 1)
            for h in range(NH):
                act.wait_ge(nm, h + 1)
                for j in range(TT):
                    m = 4 * h + j
                    if m >= 2:
                        act.wait_ge(cc, m - 1)
                    bias = AT[:, 4 * j + h:4 * j + h + 1]
                    last = act.activation(DD[:, m % 2, j * P:(j + 1) * P], ps[5][:, j * P:(j + 1) * P], ACT.Exp, bias=bias)
                    if j < TT - 1:
                        last = act.activation(DD[:, m % 2, (j + 1) * P:S], ps[4][:, (j + 1) * P:S], ACT.Exp, bias=bias)
                    last.then_inc(dd, 1)

        @block.vector
        def _(dve):
            own = core.own_dve
            g = slice(0, NH)
            turn.dve(dve)
            if first:
                turn_c.dve(dve)
            dve.wait_ge(gates, 1)
            own(dve, dve.tensor_scalar(FG[g, :], ps[5][g, :], core.gate_bias[which][:, 1:2], None, ALU.add))
            absolute(dve, AF[g, :], FG[g, :]).then_inc(absf, 1)
            dve.tensor_scalar(IG[g, :], ps[4][g, :], core.gate_bias[which][:, 0:1], None, ALU.add)
            dve.wait_ge(lnf, 1)
            own(dve, dve.scalar_tensor_tensor(out=LF[g, :], in0=FG[g, :], scalar=0.0, in1=AF[g, :],
                                              op0=ALU.min, op1=ALU.subtract))
            own(dve, dve.tensor_tensor_scan(CUM[g, :], core.ones[g, :],
                                            LF[g, :], 0.0, ALU.mult, ALU.add))
            own(dve, dve.tensor_tensor(A[g, :], IG[g, :], CUM[g, :], ALU.subtract))
            own(dve, dve.tensor_tensor_scan(M[g, :], A[g, :], A[g, :], -3e38, ALU.max, ALU.max))
            dve.tensor_scalar(NMR[g, :], M[g, :], -1.0, None, ALU.mult)
            dve.scalar_tensor_tensor(out=NL[g, :], in0=CUM[g, :], scalar=-1.0, in1=M[g, :],
                                     op0=ALU.mult, op1=ALU.subtract).then_inc(rows, 1)
            dve.wait_ge(cols, 1)
            dve.tensor_copy(AT, ps[6][:, 0:16]).then_inc(at, 1)
            for m in range(4 * NH):
                h, j = m // 4, m % 4
                dve.wait_ge(qk, m + 1)
                dve.wait_ge(dd, m + 1)
                if j == 0 and h >= 2:
                    dve.wait_ge(pv, h - 1)
                dve.scalar_tensor_tensor(out=CC[:, h % 2, offs[j]:offs[j] + S - j * P], in0=ps[6 + m % 2][:, j * P:S],
                                         scalar=1.0 / math.sqrt(DH), in1=DD[:, m % 2, j * P:S],
                                         op0=ALU.mult, op1=ALU.mult).then_inc(cc, 1)
            dve.wait_ge(pv, NH)
            for t in range(TT):
                o = ps[t][:, 0:NH * (DH + 1)].rearrange("p (h d) -> p h d", h=NH)
                last = dve.tensor_copy(DN[:, 4 * t:4 * t + 4], o[:, :, DH])
            own(dve, last)
            own(dve, absolute(dve, DN, DN))
            dve.wait_ge(en, 1)
            own(dve, dve.tensor_tensor(DN, DN, EN, ALU.max))
            own(dve, dve.tensor_scalar(DN, DN, 1e-6, None, ALU.add))
            own(dve, dve.reciprocal(RD, DN))
            for t in range(TT):
                o = ps[t][:, 0:NH * (DH + 1)].rearrange("p (h d) -> p h d", h=NH)
                last = dve.tensor_tensor(HH[:, t], o[:, :, 0:DH], free(RD[:, 4 * t:4 * t + 1], (1, NH), (0, DH)), ALU.mult)
            own(dve, last)
            for n in range(16):
                last = dve.bn_stats(ST[:, n, :], HH[:, n // 4, n % 4, :])
            own(dve, last)
            for n in range(16):
                last = dve.bn_aggr(MV[:, n, :], ST[:, n, :])
            last.then_inc(hv, 1)
            dve.wait_ge(hr, 1)
            for n in range(16):
                last = dve.tensor_scalar(HH[:, n // 4, n % 4, :], HH[:, n // 4, n % 4, :], MV[:, n, 0:1], RS[:, n:n + 1],
                                         ALU.subtract, ALU.mult)
            own(dve, last)
            hh = HH.rearrange("p t h d -> p t (h d)")
            own(dve, dve.tensor_tensor(hh, hh, free(core.norm_w[which][:, :], (0, TT), (1, D)), ALU.mult))
            for t in range(TT):
                norm.stats(dve, t, hh[:, t, :])
            for t in range(TT):
                norm.apply(dve, t)



class Router:

    def __init__(self, core, a, name, wr, bias, extra, renormalise, gates_dram):
        self.c, self.wr, self.bias, self.extra, self.renorm, self.dram = core, wr, bias, extra, renormalise, gates_dram
        self.n = 8 + extra
        self.L, self.NMX, self.SM = a.take(TT, 8), a.take(TT), a.take(TT)
        self.CMP, self.EQ = a.take(TT, 8, 8), a.take(TT, 8, 8)
        self.RK, self.G, self.GT = a.take(TT, 8), a.take(TT, self.n), a.take(S)
        s = lambda x: core.sem(f"{name}_{x}")
        self.logits, self.shifted, self.exped = s("logits_ready"), s("logits_shifted"), s("exp_logits_ready")
        self.gated, self.turned, self.gt, self.stored = s("gates_ready"), s("gates_turned"), s("gatesT_ready"), s("gates_stored")

    def pe(self, pe):
        c = self.c
        for t in range(TT):
            for k in range(DC):
                last = pe.matmul(c.ps[2][:, 8 * t:8 * t + 8], c.XT[:, k, t * P:(t + 1) * P], self.wr[:, k, :],
                                 start=(k == 0), stop=(k == DC - 1))
        last.then_inc(self.logits, 1)
        pe.wait_ge(self.gated, 1)
        for t in range(TT):
            last = pe.transpose(c.ps[3][0:self.n, t * P:(t + 1) * P], self.G[:, t, :], c.ident[:, :])
        last.then_inc(self.turned, 1)
        pe.wait_ge(self.gt, 1)

    def act(self, act):
        act.wait_ge(self.shifted, 1)
        act.activation(self.L, self.L, ACT.Exp).then_inc(self.exped, 1)

    def dve(self, dve):
        c, own = self.c, self.c.own_dve
        logits = c.ps[2][:, 0:8 * TT].rearrange("p (t e) -> p t e", t=TT)
        dve.wait_ge(self.logits, 1)
        if self.bias is not None:
            own(dve, dve.tensor_tensor(self.L, logits, free(self.bias[:, :], (0, TT), (1, 8)), ALU.add))
        else:
            own(dve, dve.tensor_copy(self.L, logits))
        own(dve, dve.tensor_reduce(self.NMX, self.L, AX.X, ALU.max, negate=True))
        dve.tensor_tensor(self.L, self.L, free(self.NMX, (1, TT), (0, 8)), ALU.add).then_inc(self.shifted, 1)
        dve.wait_ge(self.exped, 1)
        own(dve, dve.tensor_reduce(self.SM, self.L, AX.X, ALU.add))
        own(dve, dve.reciprocal(self.SM, self.SM))
        own(dve, dve.tensor_tensor(self.L, self.L, free(self.SM, (1, TT), (0, 8)), ALU.mult))
        sk, sj = free(self.L, (8, TT), (0, 8), (1, 8)), free(self.L, (8, TT), (1, 8), (0, 8))
        dve.tensor_tensor(self.CMP, sk, sj, ALU.is_gt)
        own(dve, dve.tensor_tensor(self.EQ, sk, sj, ALU.is_equal))
        own(dve, dve.tensor_tensor(self.EQ, self.EQ, free(c.tri[:, :, :], (0, TT), (8, 8), (1, 8)), ALU.mult))
        own(dve, dve.tensor_tensor(self.CMP, self.CMP, self.EQ, ALU.add))
        own(dve, dve.tensor_reduce(self.RK, self.CMP, AX.X, ALU.add))
        last = dve.scalar_tensor_tensor(out=self.G[:, :, 0:8], in0=self.RK, scalar=1.5, in1=self.L,
                                        op0=ALU.is_lt, op1=ALU.mult)
        if self.renorm:
            own(dve, last)
            own(dve, dve.tensor_reduce(self.SM, self.G, AX.X, ALU.add))
            own(dve, dve.reciprocal(self.SM, self.SM))
            last = dve.tensor_tensor(self.G, self.G, free(self.SM, (1, TT), (0, 8)), ALU.mult)
        if self.extra:
            last = dve.memset(self.G[:, :, 8:self.n], 1.0)
        last.then_inc(self.gated, 1)
        dve.wait_ge(self.turned, 1)
        dve.tensor_copy(self.GT[0:self.n, :], c.ps[3][0:self.n, :]).then_inc(self.gt, 1)

    def store(self, sp):
        sp.wait_ge(self.gt, 1)
        sp.dma_start(self.dram, self.GT[0:self.n, :]).then_inc(self.stored, 16)
        sp.wait_ge(self.stored, 16)


class Combine:

    def __init__(self, core, a, name):
        self.c, self.YT = core, a.take(DC, S)
        self.sum = core.sem(name + "_experts_summed")
        self.copied = core.sem(name + "_sum_copied")
        self.turned = core.sem(name + "_sum_turned")
        self.norm = Norm(core, name)

    def pe(self, pe):
        c = self.c
        pe.wait_ge(self.copied, 1)
        for t in range(TT):
            for k in range(DC):
                last = pe.transpose(c.ps[2 + t][:, k * P:(k + 1) * P],
                                    self.YT[:, k, t * P:(t + 1) * P], c.ident[:, :])
            last.then_inc(self.turned, 1)

    def dve(self, dve):
        c = self.c
        dve.wait_ge(self.sum, 1)
        dve.tensor_copy(self.YT[:, 0, :], c.ps[0][:, :])
        dve.tensor_copy(self.YT[:, 1, :], c.ps[1][:, :]).then_inc(self.copied, 1)
        for t in range(TT):
            dve.wait_ge(self.turned, t + 1)
            self.norm.stats(dve, t, c.ps[2 + t][:, 0:D])
        for t in range(TT):
            self.norm.apply(dve, t)


W0 = 3 * DC * I0 + 4
W0_AT = 9000
WQKV_AT = 3 * 4096
W1 = DC * F1 + 8 * D
W1_AT = 19000


def slots0(core):
    return [core.work[:, W0_AT + i * W0:W0_AT + (i + 1) * W0] for i in range(2)]


def slots1(core):
    return [core.work[:, W1_AT + i * W1:W1_AT + (i + 1) * W1] for i in range(2)]


def silu_experts(core, w_in, prefetch):
    nc, ps = core.nc, core.ps
    a = core.arena()
    W = slots0(core)
    GB = a.take(2, S)
    SL = a.take(2, S)
    HG = a.take(4, S)
    router = Router(core, a, "c", core.WR0, core.rb0, 2, False, core.dram["gates0"])
    combine = Combine(core, a, "c")
    assert a.at <= W0_AT and W0_AT + 2 * W0 <= WQKV_AT
    turn = turn_x(core, "c")
    w_used = [core.sem(f"c_weights_used{i}") for i in range(2)]
    g_in = [core.sem(f"c_gate_loaded{i}") for i in range(2)]
    g_used = [core.sem(f"c_gate_used{i}") for i in range(2)]
    up = core.sem("c_up_ready")
    sl = core.sem("c_silu_ready")
    sg = core.sem("c_gated_silu_ready")
    hid = core.sem("c_hidden_ready")
    pairs = E0A // 2

    def chunk(w, kind, k, m):
        o = (kind * DC + k) * I0 + m * P
        return w[:, o:o + P]

    with nc.Block() as block:
        @block.sync
        def _(sp):
            router.store(sp)
            def gates(e, s):
                sp.dma_start(GB[:, s, :], core.dram["gates0"][bass.ds(e, 1), :].partition_broadcast(P) if not isinstance(e, int)
                             else core.dram["gates0"][e, :].partition_broadcast(P)).then_inc(g_in[s], 16)
            for s in range(2):
                gates(s, s)
            with sp.Fori(0, pairs - 1) as i:
                for s in range(2):
                    sp.wait_ge(g_used[s], i + 1)
                    gates(2 * i + (2 + s), s)
                    sp.wait_ge(w_used[s], i + 1)
                    sp.dma_start(W[s], core.dram["w_e0"][2 * i + (2 + s)]).then_inc(w_in[s], 16)
            prefetch(sp)

        @block.tensor
        def _(pe):
            turn.pe(pe)
            pe.wait_ge(turn.ready, 2)
            router.pe(pe)
            for k in range(DC):
                pe.matmul(ps[k][:, :], core.B2[:, k * P:(k + 1) * P], router.GT[0:E0A, :], start=True, stop=False)

            def up_chunk(i, s, m):
                pe.wait_ge(hid, 4 * i + (2 * s + m + 1))
                for kind in range(2):
                    for k in range(DC):
                        last = pe.matmul(ps[2 + 2 * m + kind][:, :], chunk(W[s], kind, k, m), core.XT[:, k, :],
                                         start=(k == 0), stop=(k == DC - 1))
                last.then_inc(up, 1)

            def down_chunk(i, s, m, end=False):
                pe.wait_ge(hid, 4 * i + (2 * s + m + 3))
                for k in range(DC):
                    last = pe.matmul(ps[k][:, :], chunk(W[s], 2, m, k), HG[:, 2 * s + m, :], start=False, stop=end)
                if m == 1:
                    last.then_inc(combine.sum if end else w_used[s], 1)

            def pair(i, end):
                for s in range(2):
                    up_chunk(i, s, 1)
                    down_chunk(i, s, 0)
                    if s == 0:
                        pe.wait_ge(w_in[1], 16 * i + 16)
                        up_chunk(i, 1, 0)
                    elif not end:
                        pe.wait_ge(w_in[0], 16 * i + 32)
                        up_chunk(i + 1, 0, 0)
                    down_chunk(i, s, 1, end and s == 1)

            pe.wait_ge(w_in[0], 16)
            up_chunk(0, 0, 0)
            with pe.Fori(0, pairs - 1) as i:
                pair(i, False)
            pair(pairs - 1, True)
            combine.pe(pe)

        @block.scalar
        def _(act):
            turn.act(act)
            router.act(act)
            with act.Fori(0, pairs) as i:
                for s in range(2):
                    for m in range(2):
                        act.wait_ge(up, 4 * i + (2 * s + m + 1))
                        act.activation(SL[:, m, :], ps[2 + 2 * m][:, :], ACT.Silu,
                                       bias=W[s][:, W0 - 4 + m:W0 - 3 + m]).then_inc(sl, 1)

        @block.gpsimd
        def _(pool):
            with pool.Fori(0, pairs) as i:
                for s in range(2):
                    pool.wait_ge(g_in[s], 16 * i + 16)
                    for m in range(2):
                        pool.wait_ge(sl, 4 * i + (2 * s + m + 1))
                        last = pool.tensor_tensor(SL[:, m, :], SL[:, m, :], GB[:, s, :], ALU.mult)
                        last.then_inc(sg, 1)
                    pool.wait_ge(sg, 4 * i + (2 * s + 2))
                    pool.sem_inc(g_used[s], 1)
            for t in range(TT):
                combine.norm.pool(pool, t)

        @block.vector
        def _(dve):
            turn.dve(dve)
            dve.sem_inc(hid, 2)
            router.dve(dve)
            with dve.Fori(0, pairs) as i:
                for s in range(2):
                    for m in range(2):
                        dve.wait_ge(sg, 4 * i + (2 * s + m + 1))
                        dve.scalar_tensor_tensor(out=HG[:, 2 * s + m, :], in0=ps[3 + 2 * m][:, :],
                                                 scalar=W[s][:, W0 - 2 + m:W0 - 1 + m], in1=SL[:, m, :],
                                                 op0=ALU.add, op1=ALU.mult).then_inc(hid, 1)
            combine.dve(dve)


def relu_experts(core, w_in, b):
    nc, ps = core.nc, core.ps
    a = core.arena()
    W = slots1(core)
    GB = a.take(2, S)
    HG = a.take(4, S)
    router = Router(core, a, "f", core.WR1, None, 0, True, core.dram["gates1"])
    combine = Combine(core, a, "f")
    assert a.at <= W1_AT and W1_AT + 2 * W1 <= core.size
    turn = turn_x(core, "f")
    w_used = [core.sem(f"f_weights_used{i}") for i in range(2)]
    g_in = [core.sem(f"f_gate_loaded{i}") for i in range(2)]
    g_used = [core.sem(f"f_gate_used{i}") for i in range(2)]
    up = core.sem("f_up_ready")
    hid = core.sem("f_hidden_ready")
    stored = core.sem("f_out_stored")
    pairs, MC = E1 // 2, F1 // P

    with nc.Block() as block:
        @block.sync
        def _(sp):
            router.store(sp)
            def gates(e, s):
                sp.dma_start(GB[:, s, :], core.dram["gates1"][bass.ds(e, 1), :].partition_broadcast(P) if not isinstance(e, int)
                             else core.dram["gates1"][e, :].partition_broadcast(P)).then_inc(g_in[s], 16)
            for s in range(2):
                gates(s, s)
            with sp.Fori(0, pairs - 1) as i:
                for s in range(2):
                    sp.wait_ge(g_used[s], i + 1)
                    gates(2 * i + (2 + s), s)
                    sp.wait_ge(w_used[s], i + 1)
                    sp.dma_start(W[s], core.dram["w_e1"][2 * i + (2 + s)]).then_inc(w_in[s], 16)
            for t in range(TT):
                sp.wait_ge(combine.norm.x_ready, t + 1)
                sp.dma_start(core.dram["out"][b, t * P:(t + 1) * P, :], core.X[:, t, :]).then_inc(stored, 16)
            sp.wait_ge(stored, 16 * TT)

        @block.tensor
        def _(pe):
            turn.pe(pe)
            pe.wait_ge(turn.ready, 2)
            router.pe(pe)
            for k in range(DC):
                pe.matmul(ps[k][:, :], core.ident_bf[:, :], core.zero_bf[:, :], start=True, stop=False)

            def up_chunk(i, s, m):
                q = MC * s + m
                pe.wait_ge(hid, 2 * MC * i + (q + 1))
                for k in range(DC):
                    last = pe.matmul(ps[2 + m % 4][:, :], W[s][:, k * F1 + m * P:k * F1 + (m + 1) * P],
                                     core.XT[:, k, :], start=(k == 0), stop=(k == DC - 1))
                last.then_inc(up, 1)

            def down_chunk(i, s, m, end):
                pe.wait_ge(hid, 2 * MC * i + (MC * s + m + 5))
                for k in range(DC):
                    o = DC * F1 + m * D + k * P
                    last = pe.matmul(ps[k][:, :], W[s][:, o:o + P], HG[:, m % 4, :], start=False, stop=end)
                if m == MC - 1:
                    last.then_inc(combine.sum if end else w_used[s], 1)

            def pair(i, end):
                for s in range(2):
                    for m in range(MC):
                        if m < MC - 1:
                            up_chunk(i, s, m + 1)
                        elif s == 0:
                            pe.wait_ge(w_in[1], 16 * i + 16)
                            up_chunk(i, 1, 0)
                        elif not end:
                            pe.wait_ge(w_in[0], 16 * i + 32)
                            up_chunk(i + 1, 0, 0)
                        down_chunk(i, s, m, end and s == 1 and m == MC - 1)

            pe.wait_ge(w_in[0], 16)
            up_chunk(0, 0, 0)
            with pe.Fori(0, pairs - 1) as i:
                pair(i, False)
            pair(pairs - 1, True)
            combine.pe(pe)

        @block.scalar
        def _(act):
            turn.act(act)
            router.act(act)

        @block.gpsimd
        def _(pool):
            for t in range(TT):
                combine.norm.pool(pool, t)

        @block.vector
        def _(dve):
            turn.dve(dve)
            dve.sem_inc(hid, 4)
            router.dve(dve)
            with dve.Fori(0, pairs) as i:
                for s in range(2):
                    dve.wait_ge(g_in[s], 16 * i + 16)
                    for m in range(MC):
                        dve.wait_ge(up, 2 * MC * i + (MC * s + m + 1))
                        dve.scalar_tensor_tensor(out=HG[:, m % 4, :], in0=ps[2 + m % 4][:, :], scalar=0.0,
                                                 in1=GB[:, s, :], op0=ALU.max, op1=ALU.mult).then_inc(hid, 1)
                    dve.wait_ge(hid, 2 * MC * i + (MC * s + MC + 4))
                    dve.sem_inc(g_used[s], 1)
            combine.dve(dve)



def rope_attention(core):
    nc, ps = core.nc, core.ps
    a = core.arena()
    QT, KT, V = a.take(8, S), a.take(8, S), a.take(TT, H1 * HD1)
    assert a.at == WQKV_AT
    SC = a.take(S, H1)
    W = core.work[:, WQKV_AT:WQKV_AT + DC * 3072].rearrange("p (c n) -> p c n", c=DC)
    end = a.at
    M1, M2, RT = a.take(2, S), a.take(2, S), a.take(4, S)
    a.at = end
    TS, HS, HG = a.take(2, S), a.take(2, S), a.take(4, S)
    PR, PTS = a.take(3, S), a.take(2, S)
    O = a.take(H1 * HD1)
    OT = TS.rearrange("p a b -> p (a b)").rearrange("p (c t) -> p c t", c=8)
    NM, DEN, RD = a.take(64), a.take(64), a.take(64)

    turn = turn_x(core, "d")
    s = lambda x: core.sem("d_" + x)
    proj, roped, vcop = s("projected"), s("rope_products_ready"), s("v_ready")
    rot, tq, qk = s("rotated"), s("qk_turned"), s("qkT_ready")
    sc, scc, tt_, tev, kf = s("scores_ready"), s("scores_copied"), s("scores_turned"), s("scoresT_ready"), s("kerple_added")
    h1, hs, gl, l2, fa = s("hidden_product"), s("hidden_biased"), s("gelu_ready"), s("refined_ready"), s("refined_added")
    mx, ex, tr, pt, pv = s("max_ready"), s("probs_ready"), s("probs_turned"), s("probsT_ready"), s("values_done")
    on, ot, otr, y = s("out_ready"), s("out_turned"), s("outT_ready"), s("y_ready")
    norm = Norm(core, "d")
    base = [2 * it * (it + 1) for it in range(TT + 1)]
    last_group = lambda it: 4 * (it + 1) - 1

    def table(it, g, hf):
        o = P * (it + 1) - JG * g - 24 - 4 * hf
        return free(core.TB[:, o:o + 1], (8, 4), (1, P))

    with nc.Block() as block:
        @block.gpsimd
        def _(pool):
            for t in range(TT):
                for i in range(4):
                    n = 4 * t + i
                    pool.wait_ge(roped, n + 1)
                    if t >= 1 and i == 0:
                        pool.wait_ge(tq, 4 * t)
                    pool.tensor_tensor(RT[:, i, :], M1[:, n % 2, :], M2[:, n % 2, :], ALU.add).then_inc(rot, 1)
            for it in range(TT):
                for g in range(last_group(it) + 1):
                    n = base[it] + g
                    pool.wait_ge(tt_, n + 1)
                    v = S - P - it * P + g * JG
                    pool.tensor_tensor(SC[:, g * JG:(g + 1) * JG, :], SC[:, g * JG:(g + 1) * JG, :],
                                       core.KF[:, v:v + JG, :], ALU.add).then_inc(kf, 1)
            for t in range(TT):
                norm.pool(pool, t)

        @block.tensor
        def _(pe):
            turn.pe(pe)
            pe.wait_ge(turn.ready, 2)

            def project(t):
                for i in range(6):
                    if t >= 1:
                        if i < 4:
                            pe.wait_ge(roped, 4 * (t - 1) + i + 1)
                        else:
                            pe.wait_ge(vcop, 2 * (t - 1) + i - 3)
                    for k in range(DC):
                        last = pe.matmul(ps[i][:, :], core.XT[:, k, t * P:(t + 1) * P],
                                         W[:, k, i * 512:(i + 1) * 512], start=(k == 0), stop=(k == DC - 1))
                    last.then_inc(proj, 1)

            def turn_qk(t):
                for i in range(4):
                    n = 4 * t + i
                    pe.wait_ge(rot, n + 1)
                    if n >= 2:
                        pe.wait_ge(qk, n - 1)
                    for j in range(4):
                        last = pe.transpose(ps[6 + n % 2][:, j * P:(j + 1) * P], RT[:, i, j * P:(j + 1) * P],
                                            core.ident[:, :])
                    last.then_inc(tq, 1)

            project(0)
            for t in range(TT):
                if t + 1 < TT:
                    project(t + 1)
                turn_qk(t)
            pe.wait_ge(qk, 4 * TT)
            pe.wait_ge(vcop, 2 * TT)

            def scores(it):
                if it >= 1:
                    pe.wait_ge(pt, H1 * it)
                for h in range(H1):
                    n = H1 * it + h
                    if h >= 2:
                        pe.wait_ge(scc, n - 1)
                    r = HD1 * (h % 2)
                    pe.matmul(ps[n % 2][:, 0:(it + 1) * P], QT[r:r + HD1, h // 2, it * P:(it + 1) * P],
                              KT[r:r + HD1, h // 2, 0:(it + 1) * P], start=True, stop=True).then_inc(sc, 1)

            def turn_scores(it, g):
                n = base[it] + g
                if n >= 1:
                    pe.wait_ge(tev, n)
                for j in range(4):
                    last = pe.transpose(ps[2][:, (3 - j) * P:(4 - j) * P], SC[:, g * JG + 8 * j:g * JG + 8 * j + 8, :],
                                        core.ident[:, :])
                last.then_inc(tt_, 1)

            def hidden(it, g):
                n = base[it] + g
                pe.wait_ge(tev, n + 1)
                for hf in range(2):
                    if n >= 1:
                        pe.wait_ge(hs, 2 * n + hf - 1)
                    pe.matmul(ps[3 + hf][:, :], core.W1S[:, hf, :], TS[:, n % 2, :], start=True,
                              stop=True).then_inc(h1, 1)

            def refine(it, g):
                n = base[it] + g
                pe.wait_ge(gl, 2 * n + 2)
                if n >= 1:
                    pe.wait_ge(fa, n)
                for j in range(4):
                    for hf in range(2):
                        o = (8 * j + 4 * hf) * H1
                        last = pe.matmul(ps[5][:, o:o + 64], HG[:, (2 * n + hf) % 4, (3 - j) * P:(4 - j) * P],
                                         core.W2B[:, :], start=True, stop=True)
                last.then_inc(l2, 1)

            def turn_probs(it, h):
                n = H1 * it + h
                pe.wait_ge(ex, n + 1)
                if h >= 2:
                    pe.wait_ge(pt, n - 1)
                for j in range(it + 1):
                    last = pe.transpose(ps[n % 2][:, j * P:(j + 1) * P], PR[:, n % 3, j * P:(j + 1) * P],
                                        core.ident[:, :])
                last.then_inc(tr, 1)

            def values(it, h):
                n = H1 * it + h
                pe.wait_ge(pt, n + 1)
                for j in range(it + 1):
                    last = pe.matmul(ps[6 + h // 8][:, (h % 8) * HD1:(h % 8 + 1) * HD1], PTS[:, n % 2, j * P:(j + 1) * P],
                                     V[:, j, h * HD1:(h + 1) * HD1], start=(j == 0), stop=(j == it))
                last.then_inc(pv, 1)

            def out(it):
                pe.wait_ge(on, it + 1)
                for c in range(8):
                    last = pe.transpose(ps[3 + c // 4][:, (c % 4) * P:(c % 4 + 1) * P], O[:, c * P:(c + 1) * P],
                                        core.ident[:, :])
                last.then_inc(ot, 1)
                pe.wait_ge(otr, it + 1)
                for c in range(8):
                    last = pe.matmul(ps[5][:, 0:D], OT[:, c, :], core.WO1[:, c, :], start=(c == 0), stop=(c == 7))
                last.then_inc(y, 1)

            scores(0)
            for it in range(TT):
                pe.wait_ge(scc, H1 * (it + 1))
                if it >= 1:
                    pe.wait_ge(norm.var_ready, it)
                turn_scores(it, 0)
                for g in range(last_group(it) + 1):
                    if g < last_group(it):
                        turn_scores(it, g + 1)
                    hidden(it, g)
                    if g >= 1:
                        refine(it, g - 1)
                refine(it, last_group(it))
                if it >= 1:
                    pe.wait_ge(on, it)
                for h in range(H1 + 1):
                    if h < H1:
                        turn_probs(it, h)
                    if h >= 1:
                        values(it, h - 1)
                if it + 1 < TT:
                    scores(it + 1)
                out(it)

        @block.scalar
        def _(act):
            def copy_turned(act, t):
                for i in range(4):
                    n = 4 * t + i
                    act.wait_ge(tq, n + 1)
                    dst = (QT if i < 2 else KT)[:, 4 * (i % 2):4 * (i % 2) + 4, t * P:(t + 1) * P]
                    act.mul(dst, ps[6 + n % 2][:, :].rearrange("p (a b) -> p a b", a=4),
                            1.0 if i < 2 else 1.0 / math.sqrt(HD1)).then_inc(qk, 1)

            turn.act(act)
            for t in range(TT):
                for i in range(2):
                    act.wait_ge(proj, 6 * t + 5 + i)
                    act.copy(V[:, t, i * 512:(i + 1) * 512], ps[4 + i][:, :]).then_inc(vcop, 1)
                if t >= 1:
                    copy_turned(act, t - 1)
            copy_turned(act, TT - 1)

            def copy_scores(it):
                for h in range(H1):
                    n = H1 * it + h
                    act.wait_ge(sc, n + 1)
                    act.copy(SC[:, 0:(it + 1) * P, h], ps[n % 2][:, 0:(it + 1) * P]).then_inc(scc, 1)

            copy_scores(0)
            for it in range(TT):
                for g in range(last_group(it) + 1):
                    n = base[it] + g
                    for hf in range(2):
                        z = 2 * n + hf
                        act.wait_ge(hs, z + 1)
                        if z >= 4:
                            act.wait_ge(l2, n - 1)
                        act.activation(HG[:, z % 4, :], HS[:, z % 2, :], ACT.Gelu).then_inc(gl, 1)
                act.wait_ge(mx, it + 1)
                w = (it + 1) * P
                for h in range(H1):
                    n = H1 * it + h
                    if n >= 3:
                        act.wait_ge(tr, n - 2)
                    act.activation(PR[:, n % 3, 0:w], SC[:, 0:w, h], ACT.Exp, bias=NM[:, n:n + 1],
                                   accum_out=DEN[:, n:n + 1]).then_inc(ex, 1)
                if it + 1 < TT:
                    act.wait_ge(ex, H1 * (it + 1))
                    copy_scores(it + 1)

        @block.vector
        def _(dve):
            own = core.own_dve
            turn.dve(dve)
            for t in range(TT):
                for i in range(4):
                    n = 4 * t + i
                    dve.wait_ge(proj, 6 * t + i + 1)
                    if n >= 2:
                        dve.wait_ge(rot, n - 1)
                    x = ps[i][:, :].rearrange("p (h d) -> p h d", h=8)
                    m1 = M1[:, n % 2, :].rearrange("p (h d) -> p h d", h=8)
                    m2 = M2[:, n % 2, :].rearrange("p (h d) -> p h d", h=8)
                    dve.tensor_tensor(m1, x, free(core.rope[:, t, 0, :], (0, 8), (1, HD1)), ALU.mult)
                    dve.tensor_tensor(m2[:, :, 0:32], x[:, :, 32:64], free(core.rope[:, t, 1, 0:32], (0, 8), (1, 32)), ALU.mult)
                    dve.tensor_tensor(m2[:, :, 32:64], x[:, :, 0:32], free(core.rope[:, t, 1, 32:64], (0, 8), (1, 32)),
                                      ALU.mult).then_inc(roped, 1)

            def copy_turned_scores(it, g):
                n = base[it] + g
                dve.wait_ge(tt_, n + 1)
                if n >= 2:
                    dve.wait_ge(h1, 2 * (n - 1))
                if g == 0 and it >= 1:
                    dve.wait_ge(y, it)
                dve.tensor_copy(TS[:, n % 2, :], ps[2][:, :]).then_inc(tev, 1)

            def add_refined(it, g):
                n = base[it] + g
                dve.wait_ge(l2, n + 1)
                dve.wait_ge(kf, n + 1)
                c = SC[:, g * JG:(g + 1) * JG, :]
                dve.tensor_tensor(c, ps[5][:, :].rearrange("p (j h) -> p j h", h=H1), c, ALU.add).then_inc(fa, 1)

            for it in range(TT):
                w = (it + 1) * P
                copy_turned_scores(it, 0)
                for g in range(last_group(it) + 1):
                    if g < last_group(it):
                        copy_turned_scores(it, g + 1)
                    n = base[it] + g
                    for hf in range(2):
                        z = 2 * n + hf
                        dve.wait_ge(h1, z + 1)
                        if z >= 2:
                            dve.wait_ge(gl, z - 1)
                        dve.tensor_tensor(HS[:, z % 2, :].rearrange("p (c i) -> p c i", c=4),
                                          ps[3 + hf][:, :].rearrange("p (c i) -> p c i", c=4), table(it, g, hf),
                                          ALU.add).then_inc(hs, 1)
                    if g >= 1:
                        add_refined(it, g - 1)
                add_refined(it, last_group(it))
                dve.wait_ge(fa, base[it + 1])
                dve.tensor_reduce(NM[:, H1 * it:H1 * (it + 1)], SC[:, 0:w, :].rearrange("p j h -> p h j"), AX.X, ALU.max,
                                  negate=True).then_inc(mx, 1)
                for h in range(H1):
                    n = H1 * it + h
                    dve.wait_ge(tr, n + 1)
                    if n >= 2:
                        dve.wait_ge(pv, n - 1)
                    dve.tensor_copy(PTS[:, n % 2, 0:w], ps[n % 2][:, 0:w]).then_inc(pt, 1)
                dve.wait_ge(ex, H1 * (it + 1))
                own(dve, dve.reciprocal(RD[:, H1 * it:H1 * (it + 1)], DEN[:, H1 * it:H1 * (it + 1)]))
                dve.wait_ge(pv, H1 * (it + 1))
                for k in range(2):
                    last = dve.tensor_tensor(O[:, 512 * k:512 * (k + 1)].rearrange("p (h d) -> p h d", h=8),
                                             ps[6 + k][:, :].rearrange("p (h d) -> p h d", h=8),
                                             free(RD[:, H1 * it + 8 * k:H1 * it + 8 * k + 1], (1, 8), (0, HD1)), ALU.mult)
                last.then_inc(on, 1)
                dve.wait_ge(ot, it + 1)
                dve.tensor_copy(OT[:, 0:4, :], ps[3][:, :].rearrange("p (c t) -> p c t", c=4))
                dve.tensor_copy(OT[:, 4:8, :], ps[4][:, :].rearrange("p (c t) -> p c t", c=4)).then_inc(otr, 1)
                dve.wait_ge(y, it + 1)
                norm.stats(dve, it, ps[5][:, 0:D])
            for t in range(TT):
                norm.apply(dve, t)



def decoder(nc, dram, layers=LAYERS):
    with ExitStack() as ctx:
        core = Core(nc, ctx, dram)
        with core.semaphores():
            setup(core)
        with nc.Fori(0, B) as b:
            with core.semaphores():
                layer0(core, b, layers)
            with core.semaphores():
                layer1(core, b, layers)


def layer0(core, b, layers):
    dram, none = core.dram, lambda sp: None
    weights_in = [core.sem(f"c_weights_loaded{i}") for i in range(2)]
    qkv_in = core.sem("d_weights_loaded")

    def first_experts(sp):
        for s in range(2):
            sp.dma_start(slots0(core)[s], dram["w_e0"][s]).then_inc(weights_in[s], 16)

    def qkv(sp):
        sp.dma_start(core.work[:, WQKV_AT:WQKV_AT + DC * 3072].rearrange("p (c n) -> p c n", c=DC),
                     dram["w_qkv"].rearrange("(c p) n -> p c n", p=P)).then_inc(qkv_in, 16)
        sp.wait_ge(qkv_in, 16)

    phase_attention(core, b)
    if layers > 1:
        mlstm(core, 0, "b", 1e-6, first_experts if layers > 2 else none)
    if layers > 2:
        silu_experts(core, weights_in, qkv if layers > 3 else none)


def layer1(core, b, layers):
    dram, none = core.dram, lambda sp: None
    weights_in = [core.sem(f"f_weights_loaded{i}") for i in range(2)]

    def first_experts(sp):
        for s in range(2):
            sp.dma_start(slots1(core)[s], dram["w_e1"][s]).then_inc(weights_in[s], 16)

    if layers > 3:
        rope_attention(core)
    if layers > 4:
        mlstm(core, 1, "e", 1e-5, first_experts if layers > 5 else none)
    if layers > 5:
        relu_experts(core, weights_in, b)
    else:
        st = core.sem("dev_store")
        with core.nc.Block() as block:
            @block.sync
            def _(sp):
                sp.dma_start(dram["out"][b].rearrange("(t p) d -> p t d", p=P), core.X[:, :, :]).then_inc(st, 16)
                sp.wait_ge(st, 16)


def _constants():
    i = np.arange(P)
    mask = np.where(i[None, :] > i[:, None], np.float32(NEG), np.float32(0)).astype(np.float32)
    c = {"ident": np.eye(P, dtype=np.float32), "mask": mask}
    c["maskT"] = mask.T
    sel = np.zeros((NH, NH, P), np.float32)
    for h in range(NH):
        sel[h, h] = 1.0
    c["sel"] = sel
    e = np.arange(8)
    c["tri"] = np.broadcast_to((e[None, :] < e[:, None]).astype(np.float32), (P, 8, 8)).copy()
    inv = (1.0 / np.float32(10000.0) ** (np.arange(0, HD1, 2, dtype=np.float32) / np.float32(HD1))).astype(np.float32)
    f = np.outer(np.arange(S, dtype=np.float32), inv).astype(np.float32)
    cos, sin = np.cos(f), np.sin(f)
    rope = np.stack([np.concatenate([cos, cos], 1), np.concatenate([-sin, sin], 1)], 1)
    c["rope"] = np.ascontiguousarray(rope.reshape(TT, P, 2, HD1).transpose(1, 0, 2, 3)).astype(np.float32)
    jj = np.repeat(np.arange(4), H1)
    c["dist_c"] = np.abs(np.arange(640)[None, :] - P - jj[:, None]).astype(np.float32)
    c["dist_r"] = np.abs(i[:, None] - np.arange(S)[None, :] + (S - P)).astype(np.float32)
    return c


def _block_diagonal(w, n):
    k, m = w.shape
    out = np.zeros((n * k, n * m), w.dtype)
    for i in range(n):
        out[i * k:(i + 1) * k, i * m:(i + 1) * m] = w
    return out


def _arrays(i):
    g = {k: np.asarray(v) for k, v in i.items()}
    a = dict(_constants())
    a["x"], a["ctx"] = g["x"], g["ctx_1024"]
    a["wa"] = np.concatenate([g["L0_attn_" + n] for n in ("Wq", "Wk", "Wqp", "Wkp", "Wv")], 1)
    a["woa"] = g["L0_attn_Wo"]
    a["lambda"] = g["L0_attn_lambda_raw"]
    a["gate0"] = np.concatenate([g["L0_xattn_ig_kernel"], g["L0_xattn_fg_kernel"]], 1)
    a["gate_bias0"] = np.stack([g["L0_xattn_ig_bias"], g["L0_xattn_fg_bias"]], 1)
    a["norm_w0"] = g["L0_xattn_outnorm_weight"].reshape(-1)
    a["gate1"] = np.concatenate([g["L1_xattn_w_igate"], g["L1_xattn_w_fgate"]], 0).T
    a["gate_bias1"] = np.stack([g["L1_xattn_b_igate"], g["L1_xattn_b_fgate"]], 1)
    a["norm_w1"] = g["L1_xattn_ln_weight"]
    a["wr0"] = g["L0_ffn_gate_w"].T
    a["rb0"] = g["L0_ffn_gate_b"]

    def chunked(w):
        return w.reshape(-1, P, w.shape[1]).transpose(1, 0, 2).reshape(P, -1)

    w1 = np.concatenate([g["L0_ffn_w1"], g["L0_ffn_ws1"].reshape(2, I0, D)], 0)
    w3 = np.concatenate([g["L0_ffn_w3"], g["L0_ffn_ws3"].reshape(2, I0, D)], 0)
    w2 = np.concatenate([g["L0_ffn_w2"], g["L0_ffn_ws2"].reshape(D, 2, I0).transpose(1, 0, 2)], 0)
    b1 = np.concatenate([g["L0_ffn_b1"], g["L0_ffn_bs1"].reshape(2, I0)], 0)
    b3 = np.concatenate([g["L0_ffn_b3"], g["L0_ffn_bs3"].reshape(2, I0)], 0)
    a["w_e0"] = np.stack([np.concatenate([chunked(w1[e].T), chunked(w3[e].T), chunked(w2[e].T),
                                          b1[e].reshape(2, P).T, b3[e].reshape(2, P).T], 1) for e in range(E0A)])
    a["b2"] = np.concatenate([g["L0_ffn_b2"], g["L0_ffn_bs2"][None], np.zeros((1, D), np.float32)], 0)
    a["w_qkv"] = g["L1_attn_w_qkv"]
    a["wo1"] = g["L1_attn_w_o"]
    a["log_p"], a["log_a"] = g["L1_attn_log_p"].reshape(-1), g["L1_attn_log_a"].reshape(-1)
    a["b2a"] = g["L1_attn_b2"]
    a["pa_col"] = np.stack([np.tile(a["log_p"], 4), np.tile(a["log_a"], 4)], 1)
    a["b1_col"] = np.tile(g["L1_attn_b1"], 4)[:, None]
    w1 = g["L1_attn_w1"]
    big = _block_diagonal(w1[0:H1], 8)
    a["w1s"] = np.stack([big[:, 0:P], big[:, P:2 * P]], 1)
    a["w1k"] = _block_diagonal(w1[H1:], 4)
    a["w2b"] = _block_diagonal(g["L1_attn_w2"], 4)
    a["wr1"] = g["L1_ffn_Wr"]
    a["w_e1"] = np.stack([np.concatenate([chunked(g["L1_ffn_W1"][e]), chunked(g["L1_ffn_W2"][e])], 1) for e in range(E1)])
    return {k: np.ascontiguousarray(v) for k, v in a.items()}


def kernel(**inputs):
    import concourse.bacc as bacc
    from concourse.bass_utils import run_bass_kernel_spmd

    nc, arrays = _build(bacc, inputs)
    r = run_bass_kernel_spmd(nc, [arrays], core_ids=[0])
    return r.results[0]["out_dram"]


def _build(bacc, inputs, layers=LAYERS):
    nc = bacc.Bacc("TRN2", target_bir_lowering=False, num_devices=1)
    arrays, dram = {}, {}
    for name, x in _arrays(inputs).items():
        arrays[f"in_{name}_dram"] = x
        dram[name] = nc.dram_tensor(f"in_{name}_dram", x.shape, mybir.dt.from_np(x.dtype), kind="ExternalInput").ap()
    dram["gates0"] = nc.dram_tensor("gates0_dram", (E0A, S), F32, kind="Internal").ap()
    dram["gates1"] = nc.dram_tensor("gates1_dram", (E1, S), F32, kind="Internal").ap()
    dram["out"] = nc.dram_tensor("out_dram", (B, S, D), F32, kind="ExternalOutput").ap()
    decoder(nc, dram, layers)
    return nc, arrays
```

```python
import math
from contextlib import ExitStack, contextmanager

import numpy as np
import concourse.bass as bass
from concourse import mybir

F32 = mybir.dt.float32
BF16 = mybir.dt.bfloat16
F32R = mybir.dt.float32r
ALU = mybir.AluOpType
ACT = mybir.ActivationFunctionType
AX = mybir.AxisListType

P = 128
B, S, D = 4, 512, 256
TT = S // P
DC = D // P
NEG = -1e30

H0, HD0 = 16, 16
HS0 = 64
NH, DH = 4, 64
E0, I0 = 8, 256
E0A = 10
H1, HD1 = 16, 64
E1, F1 = 8, 1024
JG = 32

FIRST_SEM = 120

FG_ROW = 32
C0 = 6 * P
C1 = 4 * P
W0, W1 = 2 * C0, 8 * C1
PARTS0 = 2 * 4 * C0 + 2 * DC * S + 2 * 2 * S
PARTS1 = 2 * 8 * C1 + 2 * DC * S + 2 * 4 * S
W0_AT = 8200
W1_AT = 8200
WQKV_AT = 3 * 4096

LAYERS = 6


def free(ap, *dims):
    return bass.AP(ap.tensor, ap.offset, [list(ap.ap[0])] + [list(d) for d in dims])


def absolute(dve, out, x):
    return dve.scalar_tensor_tensor(out=out, in0=x, scalar=-1.0, in1=x, op0=ALU.mult, op1=ALU.max)


class Own:

    def __init__(self, sem):
        self.sem, self.n = sem, 0

    def __call__(self, eng, ins):
        self.n += 1
        ins.then_inc(self.sem, 1)
        eng.wait_ge(self.sem, self.n)


class Arena:

    def __init__(self, base, size):
        self.base, self.size, self.at = base, size, 0

    def take(self, *dims):
        n = int(np.prod(dims))
        a = self.base[:, self.at:self.at + n]
        self.at += n
        assert self.at <= self.size, (self.at, self.size)
        if len(dims) == 2:
            return a.rearrange("p (a b) -> p a b", a=dims[0])
        if len(dims) == 3:
            return a.rearrange("p (a b c) -> p a b c", a=dims[0], b=dims[1])
        if len(dims) == 4:
            return a.rearrange("p (a b c d) -> p a b c d", a=dims[0], b=dims[1], c=dims[2])
        return a


class Core:

    def __init__(self, nc, ctx, dram):
        self.nc, self.ctx, self.dram = nc, ctx, dram
        sb = self.sb
        self.ident = sb("ident", [P, P])
        self.ident_bf = sb("ident_bf", [P, P], BF16)
        self.mask_bf = sb("mask_bf", [P, P], BF16)
        self.maskT_bf = sb("maskT_bf", [P, P], BF16)
        self.X = sb("X", [P, TT, D])
        self.XT = sb("XT", [P, DC, S])
        self.CV = sb("CV", [P, TT, NH, DH + 1])
        self.CT = sb("CT", [P, DC, S])
        self.R = sb("R", [P, TT, D])
        self.stats = sb("stats", [P, TT, 6])
        self.mv = sb("mv", [P, TT, 2])
        self.rstd = sb("rstd", [P, TT])
        self.mhalf = sb("mhalf", [P, 16])
        self.halfpi = sb("halfpi", [P, 1])
        self.ones = sb("ones", [NH, S])
        self.zero_bf = sb("zero_bf", [P, S], BF16)
        self.WA = sb("WA", [P, DC, 5 * D])
        self.WOA = sb("WOA", [P, DC, D])
        self.lam = sb("lam", [P, H0])
        self.gate = [sb(f"gate{i}", [P, 6, FG_ROW + NH]) for i in range(2)]
        self.gate_bias = [sb(f"gate_bias{i}", [NH, 2]) for i in range(2)]
        self.norm_w = [sb(f"norm_w{i}", [P, D]) for i in range(2)]
        self.sel = sb("sel", [NH, NH, P])
        self.WR0 = sb("WR0", [P, DC, E0])
        self.rb0 = sb("rb0", [P, E0])
        self.WR1 = sb("WR1", [P, DC, E1])
        self.B2 = sb("B2", [E0A, D])
        self.tri = sb("tri", [P, E0, E0])
        self.rope = sb("rope", [P, TT, 2, HD1])
        self.W1S = sb("W1S", [P, 2, P])
        self.W2B = sb("W2B", [P, 64])
        self.TB = sb("TB", [P, 640])
        self.KF = sb("KF", [P, S, H1])
        self.WO1 = sb("WO1", [P, 8, D])
        size = 29760
        base = nc.sbuf_base
        self.work = sb("work", [P, size])
        self.size = size
        self.parts = [nc.alloc_sbuf_tensor_at(f"parts{i}", [P, n], F32R, offset=base + 4 * (size - n))
                      for i, n in enumerate((PARTS0, PARTS1))]
        self.ps = [ctx.enter_context(nc.psum_tensor(f"ps{i}", [P, 512], F32)) for i in range(8)]

    def sb(self, name, shape, dt=F32):
        return self.ctx.enter_context(self.nc.sbuf_tensor(name, shape, dt))

    def sem(self, name):
        s = self.sem_ctx.enter_context(self.nc.semaphore(name, num=FIRST_SEM + len(self.sems)))
        self.sems.append(s)
        return s

    @contextmanager
    def semaphores(self):
        with ExitStack() as self.sem_ctx:
            self.sems = []
            self.own_dve = Own(self.sem("dve_own"))
            self.own_act = Own(self.sem("act_own"))
            self.own_pool = Own(self.sem("pool_own"))
            yield
            self.nc.all_engine_barrier(sems_to_clear=range(FIRST_SEM, FIRST_SEM + len(self.sems)))

    def arena(self):
        return Arena(self.work, self.size)



class Norm:

    def __init__(self, core, name, eps=1e-5):
        self.c, self.eps = core, eps
        self.var_ready = core.sem(f"{name}_var_ready")
        self.rstd_ready = core.sem(f"{name}_rstd_ready")
        self.x_ready = core.sem(f"{name}_x_normed")

    def stats(self, dve, t, y):
        c = self.c
        c.own_dve(dve, dve.tensor_tensor(c.R[:, t, :], y, c.X[:, t, :], ALU.add))
        c.own_dve(dve, dve.bn_stats(c.stats[:, t, :], c.R[:, t, :]))
        dve.bn_aggr(c.mv[:, t, :], c.stats[:, t, :]).then_inc(self.var_ready, 1)

    def pool(self, pool, t):
        c = self.c
        pool.wait_ge(self.var_ready, t + 1)
        c.own_pool(pool, pool.tensor_scalar(c.rstd[:, t:t + 1], c.mv[:, t, 1:2], self.eps, None, ALU.add))
        pool.tensor_tensor(c.rstd[:, t:t + 1], c.rstd[:, t:t + 1], c.mhalf[:, 0:1],
                           ALU.pow).then_inc(self.rstd_ready, 1)

    def apply(self, dve, t):
        c = self.c
        dve.wait_ge(self.rstd_ready, t + 1)
        dve.tensor_scalar(c.X[:, t, :], c.R[:, t, :], c.mv[:, t, 0:1], c.rstd[:, t:t + 1],
                          ALU.subtract, ALU.mult).then_inc(self.x_ready, 1)


class Turn:

    def __init__(self, core, name, src, dst, banks=(0, 1)):
        self.c, self.src, self.dst, self.banks = core, src, dst, banks
        self.turned = core.sem(f"{name}_x_turned")
        self.ready = core.sem(f"{name}_feature_major")

    def pe(self, pe):
        c = self.c
        for k in range(DC):
            for t in range(TT):
                last = pe.transpose(c.ps[self.banks[k]][:, t * P:(t + 1) * P], self.src(t, k), c.ident[:, :])
            last.then_inc(self.turned, 1)

    def dve(self, dve):
        dve.wait_ge(self.turned, 1)
        dve.tensor_copy(self.dst[:, 0, :], self.c.ps[self.banks[0]][:, :]).then_inc(self.ready, 1)

    def act(self, act):
        act.wait_ge(self.turned, 2)
        act.copy(self.dst[:, 1, :], self.c.ps[self.banks[1]][:, :]).then_inc(self.ready, 1)


def turn_x(core, name):
    return Turn(core, name, lambda t, k: core.X[:, t, k * P:(k + 1) * P], core.XT)



def setup(core):
    nc, d = core.nc, core.dram
    a = core.arena()
    par = a.take(3, H1)
    sp = a.take(6, H1)
    col = a.take(4)
    spc = a.take(8)
    dist_c = a.take(640)
    dist_r = a.take(S)
    maskf, maskTf = a.take(P), a.take(P)
    w1k = a.take(P)
    lamr = a.take(H0)
    lam1 = a.take(H0)
    loaded = core.sem("constants_loaded")
    p_ready = core.sem("softplus_ready")
    kerple_ready = core.sem("kerple_ready")
    kcol_ready = core.sem("kerple_column_ready")
    tb_ready = core.sem("table_product_ready")
    lam_t = core.sem("lambda_tanh")
    loads = [
        (core.ident[:, :], d["ident"]), (maskTf, d["maskT"]), (core.WA[:, :, :], d["wa"].rearrange("(c p) n -> p c n", p=P)),
        (core.WOA[:, :, :], d["woa"].rearrange("(c p) n -> p c n", p=P)), (lamr, d["lambda"].partition_broadcast(P)),
        (core.sel[:, :, :], d["sel"]), (core.tri[:, :, :], d["tri"]), (core.rope[:, :, :, :], d["rope"]),
        (core.WR0[:, :, :], d["wr0"].rearrange("(c p) n -> p c n", p=P)), (core.rb0[:, :], d["rb0"].partition_broadcast(P)),
        (core.WR1[:, :, :], d["wr1"].rearrange("(c p) n -> p c n", p=P)), (core.B2[:, :], d["b2"]),
        (core.W1S[:, :, :], d["w1s"]), (w1k[0:64, :], d["w1k"]), (core.W2B[:, :], d["w2b"]),
        (core.WO1[:, :, :], d["wo1"].rearrange("(c p) n -> p c n", p=P)),
        (par[:, 0, :], d["log_p"].partition_broadcast(P)), (par[:, 1, :], d["log_a"].partition_broadcast(P)),
        (par[:, 2, :], d["b2a"].partition_broadcast(P)), (col[0:64, 0:2], d["pa_col"]), (col[:, 2:3], d["b1_col"]),
        (dist_c[0:64, :], d["dist_c"]), (dist_r, d["dist_r"]), (maskf, d["mask"]),
    ]
    for i in range(2):
        loads += [(core.gate[i][:, :, :], d[f"gate{i}"].rearrange("(c p) n -> p c n", p=P)),
                  (core.gate_bias[i][:, :], d[f"gate_bias{i}"]),
                  (core.norm_w[i][:, :], d[f"norm_w{i}"].partition_broadcast(P))]
    n_loads = 16 * len(loads)

    with nc.Block() as block:
        @block.sync
        def _(sp_):
            for dst, src in loads:
                sp_.dma_start(dst, src).then_inc(loaded, 16)
            sp_.wait_ge(loaded, n_loads)

        @block.scalar
        def _(act):
            own = core.own_act
            act.wait_ge(loaded, n_loads)
            act.activation(lam1, lamr, ACT.Tanh).then_inc(lam_t, 1)
            act.wait_ge(p_ready, 2)
            own(act, act.activation(sp[:, 2:4, :], sp[:, 0:2, :], ACT.Exp, scale=-1.0))
            own(act, act.activation(spc[0:64, 2:4], spc[0:64, 0:2], ACT.Exp, scale=-1.0))
            own(act, act.activation(sp[:, 4:6, :], sp[:, 2:4, :], ACT.Ln, bias=1.0))
            act.activation(spc[0:64, 4:6], spc[0:64, 2:4], ACT.Ln, bias=1.0).then_inc(kcol_ready, 1)
            act.wait_ge(p_ready, 5)
            act.activation(core.KF[:, :, :], core.KF[:, :, :], ACT.Ln, bias=1.0).then_inc(kerple_ready, 1)
            act.activation(dist_c[0:64, :], dist_c[0:64, :], ACT.Ln, bias=1.0,
                           scale=spc[0:64, 7:8]).then_inc(kerple_ready, 1)

        @block.vector
        def _(dve):
            own = core.own_dve
            dve.memset(core.mhalf[:, :], -0.5)
            dve.memset(core.ones[:, :], 1.0)
            dve.memset(core.zero_bf[:, :], 0.0)
            dve.memset(core.halfpi[:, :], math.pi / 2)
            dve.wait_ge(loaded, n_loads)
            dve.tensor_copy(core.ident_bf[:, :], core.ident[:, :])
            dve.tensor_copy(core.mask_bf[:, :], maskf)
            dve.tensor_copy(core.maskT_bf[:, :], maskTf)
            absolute(dve, sp[:, 0:2, :], par[:, 0:2, :]).then_inc(p_ready, 1)
            absolute(dve, spc[0:64, 0:2], col[0:64, 0:2]).then_inc(p_ready, 1)
            dve.tensor_scalar(core.norm_w[1][:, :], core.norm_w[1][:, :], 1.0, None, ALU.add)
            dve.wait_ge(lam_t, 1)
            dve.tensor_scalar(core.lam[:, :], lam1, 0.5 / math.sqrt(HD0), None, ALU.mult)
            dve.wait_ge(kcol_ready, 1)
            own(dve, dve.scalar_tensor_tensor(out=sp[:, 0:2, :], in0=par[:, 0:2, :], scalar=0.0, in1=sp[:, 4:6, :],
                                              op0=ALU.max, op1=ALU.add))
            dve.scalar_tensor_tensor(out=spc[0:64, 6:8], in0=col[0:64, 0:2], scalar=0.0, in1=spc[0:64, 4:6],
                                     op0=ALU.max, op1=ALU.add).then_inc(p_ready, 1)
            dve.wait_ge(p_ready, 3)
            dve.tensor_scalar(spc[0:64, 0:1], spc[0:64, 6:7], -1.0, None, ALU.mult).then_inc(p_ready, 1)
            dve.tensor_tensor(core.KF[:, :, :], free(dist_r, (1, S), (0, H1)), free(sp[:, 1, :], (0, S), (1, H1)),
                              ALU.mult).then_inc(p_ready, 1)
            dve.wait_ge(kerple_ready, 2)
            dve.tensor_scalar(dist_c[0:64, :], dist_c[0:64, :], spc[0:64, 0:1], None, ALU.mult).then_inc(kcol_ready, 1)
            own(dve, dve.tensor_tensor(core.KF[:, :, :], core.KF[:, :, :], free(sp[:, 0, :], (0, S), (1, H1)), ALU.mult))
            own(dve, dve.tensor_tensor(core.KF[:, :, :], free(par[:, 2, :], (0, S), (1, H1)), core.KF[:, :, :],
                                       ALU.subtract))
            dve.tensor_tensor(core.KF[:, S - P:S, :], core.KF[:, S - P:S, :], free(maskf, (1, P), (0, H1)), ALU.add)
            dve.wait_ge(tb_ready, 1)
            dve.tensor_scalar(core.TB[:, 0:512], core.ps[0][:, :], col[:, 2:3], None, ALU.add)
            dve.tensor_scalar(core.TB[:, 512:640], core.ps[1][:, 0:128], col[:, 2:3], None, ALU.add)

        @block.tensor
        def _(pe):
            pe.wait_ge(kcol_ready, 2)
            pe.wait_ge(loaded, n_loads)
            pe.matmul(core.ps[0][:, :], w1k[0:64, :], dist_c[0:64, 0:512], start=True, stop=True)
            pe.matmul(core.ps[1][:, 0:128], w1k[0:64, :], dist_c[0:64, 512:640], start=True,
                      stop=True).then_inc(tb_ready, 1)



def phase_attention(core, b):
    nc, ps = core.nc, core.ps
    a = core.arena()
    QT, KT = a.take(8, S), a.take(8, S)
    RAW, AMP = a.take(TT, 2 * D), a.take(TT, 2 * D)
    SN, CS = a.take(TT, 2 * D), a.take(TT, 2 * D)
    V = a.take(TT, D)
    Q3 = a.take(2, 2, H0, HS0)
    SQ = a.take(TT, 2 * D)
    QZ = a.take(2, 2, S)
    SS = a.take(TT, 2 * H0)
    RN = a.take(TT, 2 * H0)
    a2 = Arena(core.work, core.size)
    a2.take(16 * S)
    PR, PTS = a2.take(3, S), a2.take(2, S)
    NM, DEN, RD = a2.take(64), a2.take(64), a2.take(64)
    O, OT = a2.take(TT, D), a2.take(DC, S)
    assert a2.at <= 16 * S + 4 * TT * 2 * D

    x_in = core.sem("a_x_loaded")
    ctx_in = core.sem("a_context_loaded")
    turn = turn_x(core, "a")
    turn_c = Turn(core, "a_context", lambda t, k: core.R[:, t, k * P:(k + 1) * P], core.CT, banks=(6, 7))
    qz = core.sem("a_padded_q_ready")
    proj = core.sem("a_projected")
    raw = core.sem("a_raw_ready")
    tanh = core.sem("a_tanh_ready")
    absph = core.sem("a_abs_phase_ready")
    absraw = core.sem("a_abs_raw_ready")
    sin = core.sem("a_sin_cos_ready")
    lnp = core.sem("a_log1p_ready")
    ssq = core.sem("a_square_sums_ready")
    rn = core.sem("a_amp_norm_ready")
    zeroed = core.sem("a_zeroed")
    q3raw = core.sem("a_q3_raw_ready")
    q3 = core.sem("a_q3_ready")
    tp = core.sem("a_turned")
    ev = (core.sem("a_qk_copied_even"), core.sem("a_qk_copied_odd"))
    sc = core.sem("a_scores_ready")
    mx = core.sem("a_max_ready")
    ex = core.sem("a_probs_ready")
    tr = core.sem("a_probs_turned")
    pt = core.sem("a_probsT_ready")
    pv = core.sem("a_pv_done")
    on = core.sem("a_out_ready")
    ot = core.sem("a_out_turned")
    otr = core.sem("a_outT_ready")
    y = core.sem("a_y_ready")
    norm = Norm(core, "a")
    steps = [(h, it) for h in range(H0) for it in range(TT)]
    N = len(steps)
    PROJ = [2, 5]
    SB, PB = (0, 1, 2), (3, 4)
    OB = lambda it: ps[5 + it // 2][:, (it % 2) * D:(it % 2 + 1) * D]
    YB = lambda t: ps[(2, 3, 4, 7)[t]][:, 0:D]

    with nc.Block() as block:
        @block.sync
        def _(sp):
            sp.dma_start(core.X[:, :, :], core.dram["x"][b].rearrange("(t p) d -> p t d", p=P)).then_inc(x_in, 16)
            sp.dma_start(core.R[:, :, :], core.dram["ctx"][b].rearrange("(t p) d -> p t d", p=P)).then_inc(ctx_in, 16)
            for t in range(TT):
                sp.dma_start(core.CV[:, t, :, 0:DH], core.dram["ctx"][b, t * P:(t + 1) * P, :].rearrange(
                    "p (h d) -> p h d", h=NH)).then_inc(ctx_in, 16)
            sp.wait_ge(ctx_in, 16 * (TT + 1))

        @block.gpsimd
        def _(pool):
            pool.memset(core.CV[:, :, :, DH:DH + 1], 1.0)
            pool.memset(QZ[:, :, :, :], 0.0)
            pool.memset(Q3[:, :, :, :, 48:64], 0.0).then_inc(zeroed, 1)
            for t in range(TT):
                pool.wait_ge(raw, t + 1)
                if t >= 2:
                    pool.wait_ge(tp, 4 * (t - 1))
                src = RAW[:, t, :].rearrange("p (s h d) -> p s h d", s=2, h=H0)
                pool.tensor_copy(Q3[:, t % 2, 0, :, 0:16], src[:, 0])
                pool.tensor_scalar(Q3[:, t % 2, 1, :, 0:16], src[:, 1], 1.0 / math.sqrt(HD0), None,
                                   ALU.mult).then_inc(q3raw, 1)
            for pair in range(H0 // 2):
                if pair == 0:
                    pool.wait_ge(ev[0], 8)
                    pool.wait_ge(ev[1], 8)
                if pair >= 2:
                    pool.wait_ge(sc, 8 * (pair - 1))
                for k in range(2):
                    r = slice(64 * k, 64 * k + 64)
                    pool.tensor_copy(QZ[r, pair % 2, k, :], QT[r, pair, :]).then_inc(qz, 1)
            for t in range(TT):
                norm.pool(pool, t)

        @block.tensor
        def _(pe):
            pe.wait_ge(x_in, 16)
            turn.pe(pe)
            pe.wait_ge(turn.ready, 2)
            for t in range(TT):
                if t == 1:
                    pe.wait_ge(ctx_in, 16 * (TT + 1))
                    turn_c.pe(pe)
                    pe.wait_ge(turn_c.ready, 2)
                if t >= 2:
                    pe.wait_ge(raw, t - 1)
                    pe.wait_ge(tanh, t - 1)
                for i, w in enumerate((512, 512, 256)):
                    for k in range(DC):
                        last = pe.matmul(ps[PROJ[t % 2] + i][:, 0:w], core.XT[:, k, t * P:(t + 1) * P],
                                         core.WA[:, k, 512 * i:512 * i + w], start=(k == 0), stop=(k == DC - 1))
                last.then_inc(proj, 1)
            for t in range(TT):
                pe.wait_ge(q3, t + 1)
                for i in range(4):
                    n = 4 * t + i
                    if n >= 4:
                        pe.wait_ge(ev[n % 2], (n - 4) // 2 + 1)
                    for j in range(4):
                        pair = 4 * (i % 2) + j
                        last = pe.transpose(ps[n % 4][:, j * P:(j + 1) * P],
                                            Q3[:, t % 2, i // 2, 2 * pair:2 * pair + 2, :], core.ident[:, :])
                    last.then_inc(tp, 1)

            def scores(n):
                h, it = steps[n]
                if n >= 3:
                    pe.wait_ge(ex, n - 2)
                w = (it + 1) * P
                if it == 0:
                    pe.wait_ge(qz, h + 1)
                pe.matmul(ps[SB[n % 3]][:, 0:w], QZ[:, h // 2 % 2, h % 2, it * P:w], KT[:, h // 2, 0:w],
                          start=True, stop=False)
                pe.matmul(ps[SB[n % 3]][:, w - P:w], core.ident_bf[:, :], core.mask_bf[:, :],
                          start=False, stop=True).then_inc(sc, 1)

            def turn_probs(n):
                _, it = steps[n]
                pe.wait_ge(ex, n + 1)
                if n >= 2:
                    pe.wait_ge(pt, n - 1)
                for j in range(it + 1):
                    last = pe.transpose(ps[PB[n % 2]][:, j * P:(j + 1) * P], PR[:, n % 3, j * P:(j + 1) * P],
                                        core.ident[:, :])
                last.then_inc(tr, 1)

            def values(n):
                h, it = steps[n]
                pe.wait_ge(pt, n + 1)
                for j in range(it + 1):
                    last = pe.matmul(OB(it)[:, h * HD0:(h + 1) * HD0], PTS[:, n % 2, j * P:(j + 1) * P],
                                     V[:, j, h * HD0:(h + 1) * HD0], start=(j == 0), stop=(j == it))
                last.then_inc(pv, 1)

            scores(0)
            scores(1)
            for n in range(N + 1):
                if n + 2 < N:
                    scores(n + 2)
                if n < N:
                    turn_probs(n)
                if n >= 1:
                    values(n - 1)
            pe.wait_ge(on, TT)
            for k in range(DC):
                for t in range(TT):
                    last = pe.transpose(ps[k][:, t * P:(t + 1) * P], O[:, t, k * P:(k + 1) * P], core.ident[:, :])
            last.then_inc(ot, 1)
            pe.wait_ge(otr, 1)
            for t in range(TT):
                for k in range(DC):
                    last = pe.matmul(YB(t), OT[:, k, t * P:(t + 1) * P], core.WOA[:, k, :],
                                     start=(k == 0), stop=(k == DC - 1))
                last.then_inc(y, 1)

        @block.scalar
        def _(act):
            turn.act(act)
            for t in range(TT):
                if t == 1:
                    turn_c.act(act)
                act.wait_ge(proj, t + 1)
                act.activation(SN[:, t, :], ps[PROJ[t % 2] + 1][:, :], ACT.Tanh).then_inc(tanh, 1)
            act.wait_ge(absraw, TT)
            core.own_act(act, act.activation(AMP, AMP, ACT.Exp, scale=-1.0))
            act.activation(AMP, AMP, ACT.Ln, bias=1.0).then_inc(lnp, 1)
            act.wait_ge(absph, TT)
            act.activation(SN, SN, ACT.Sin, scale=math.pi)
            act.activation(CS, CS, ACT.Sin, scale=-math.pi, bias=core.halfpi[:, :]).then_inc(sin, 1)
            act.wait_ge(ssq, 1)
            core.own_act(act, act.activation(RN, SS, ACT.Ln))
            act.activation(RN, RN, ACT.Exp, scale=-0.5).then_inc(rn, 1)
            for n in range(1, 16, 2):
                act.wait_ge(tp, n + 1)
                t, i = n // 4, n % 4
                dst = (QT if i < 2 else KT)[:, 4 * (i % 2):4 * (i % 2) + 4, t * P:(t + 1) * P]
                act.copy(dst, ps[n % 4][:, :].rearrange("p (a b) -> p a b", a=4)).then_inc(ev[1], 1)
            for n in range(N):
                w = (steps[n][1] + 1) * P
                act.wait_ge(mx, n + 1)
                if n >= 3:
                    act.wait_ge(tr, n - 2)
                act.activation(PR[:, n % 3, 0:w], ps[SB[n % 3]][:, 0:w], ACT.Exp, bias=NM[:, n:n + 1],
                               accum_out=DEN[:, n:n + 1]).then_inc(ex, 1)

        @block.vector
        def _(dve):
            own = core.own_dve
            turn.dve(dve)
            for t in range(TT):
                if t == 1:
                    turn_c.dve(dve)
                dve.wait_ge(proj, t + 1)
                dve.tensor_copy(V[:, t, :], ps[PROJ[t % 2] + 2][:, 0:D])
                dve.tensor_copy(RAW[:, t, :], ps[PROJ[t % 2]][:, :]).then_inc(raw, 1)
                dve.wait_ge(raw, t + 1)
                absolute(dve, AMP[:, t, :], RAW[:, t, :]).then_inc(absraw, 1)
            for t in range(TT):
                dve.wait_ge(tanh, t + 1)
                absolute(dve, CS[:, t, :], SN[:, t, :]).then_inc(absph, 1)
            dve.wait_ge(lnp, 1)
            own(dve, dve.scalar_tensor_tensor(out=AMP, in0=RAW, scalar=0.0, in1=AMP, op0=ALU.max, op1=ALU.add))
            own(dve, dve.tensor_tensor(SQ, AMP, AMP, ALU.mult))
            own(dve, dve.tensor_reduce(SS, SQ.rearrange("p t (h d) -> p t h d", d=HD0), AX.X, ALU.add))
            dve.tensor_scalar(SS, SS, 1.0 / HD0, 1e-6, ALU.mult, ALU.add).then_inc(ssq, 1)
            dve.wait_ge(zeroed, 1)
            dve.wait_ge(rn, 1)
            own(dve, dve.tensor_tensor(RN[:, :, H0:], RN[:, :, H0:], free(core.lam[:, :], (0, TT), (1, H0)), ALU.mult))
            dve.wait_ge(sin, 1)
            for t in range(TT):
                amp = AMP[:, t, :].rearrange("p (h d) -> p h d", d=HD0)
                own(dve, dve.tensor_tensor(amp, amp, free(RN[:, t, :], (1, 2 * H0), (0, HD0)), ALU.mult))
                if t >= 2:
                    dve.wait_ge(tp, 4 * (t - 1))
                dve.wait_ge(q3raw, t + 1)
                q = Q3[:, t % 2].rearrange("p s h d -> p (s h) d")
                dve.tensor_tensor(q[:, :, 16:32], amp, CS[:, t, :].rearrange("p (h d) -> p h d", d=HD0), ALU.mult)
                dve.tensor_tensor(q[:, :, 32:48], amp, SN[:, t, :].rearrange("p (h d) -> p h d", d=HD0),
                                  ALU.mult).then_inc(q3, 1)
                for n in range(4 * t, 4 * t + 4, 2):
                    dve.wait_ge(tp, n + 1)
                    i = n % 4
                    dst = (QT if i < 2 else KT)[:, 4 * (i % 2):4 * (i % 2) + 4, t * P:(t + 1) * P]
                    dve.tensor_copy(dst, ps[n % 4][:, :].rearrange("p (a b) -> p a b", a=4)).then_inc(ev[0], 1)

            for n in range(N + 1):
                if n < N:
                    w = (steps[n][1] + 1) * P
                    dve.wait_ge(sc, n + 1)
                    dve.tensor_reduce(NM[:, n:n + 1], ps[SB[n % 3]][:, 0:w], AX.X, ALU.max,
                                      negate=True).then_inc(mx, 1)
                if n >= 1:
                    m = n - 1
                    w = (steps[m][1] + 1) * P
                    dve.wait_ge(tr, m + 1)
                    if m >= 2:
                        dve.wait_ge(pv, m - 1)
                    dve.tensor_copy(PTS[:, m % 2, 0:w], ps[PB[m % 2]][:, 0:w]).then_inc(pt, 1)
            dve.wait_ge(ex, N)
            own(dve, dve.reciprocal(RD, DEN))
            dve.wait_ge(pv, N)
            for it in range(TT):
                dve.tensor_tensor(O[:, it, :].rearrange("p (h d) -> p h d", h=H0),
                                  OB(it).rearrange("p (h d) -> p h d", h=H0),
                                  free(RD[:, it:it + 1], (TT, H0), (0, HD0)), ALU.mult).then_inc(on, 1)
            dve.wait_ge(ot, 1)
            dve.tensor_copy(OT[:, 0, :], ps[0][:, :])
            dve.tensor_copy(OT[:, 1, :], ps[1][:, :]).then_inc(otr, 1)
            for t in range(TT):
                dve.wait_ge(y, t + 1)
                norm.stats(dve, t, YB(t))
            for t in range(TT):
                norm.apply(dve, t)



def mlstm(core, which, name, head_eps, prefetch):
    nc, ps = core.nc, core.ps
    a = core.arena()
    FG, AF, IG, NMR = a.take(S), a.take(S), a.take(S), a.take(S)
    LF, CUM, A, M, NL = FG, AF, IG, FG, AF
    AT, EN = a.take(16), a.take(16)
    DD = a.take(2, S)
    CC = a.take(2, 10 * P)
    XZ = a.take(NH, S)
    DN, RD = a.take(16), a.take(16)
    HH = Arena(core.work, core.size).take(TT, NH, DH)
    ST, MV, RS = a.take(16, 6), a.take(16, 2), a.take(16)
    assert a.at <= W0_AT, a.at
    offs = [0, 4 * P, 7 * P, 9 * P]

    turn = turn_x(core, name)
    xz = core.sem(name + "_padded_q_ready")
    gates = core.sem(name + "_gates_ready")
    absf = core.sem(name + "_abs_f_ready")
    lnf = core.sem(name + "_log1p_ready")
    rows = core.sem(name + "_gate_rows_ready")
    cols = core.sem(name + "_gate_columns_turned")
    at = core.sem(name + "_columns_ready")
    en = core.sem(name + "_exp_neg_max_ready")
    nm = core.sem(name + "_neg_max_spread")
    qk = core.sem(name + "_qk_ready")
    dd = core.sem(name + "_decay_ready")
    cc = core.sem(name + "_c_ready")
    pv = core.sem(name + "_values_done")
    hv = core.sem(name + "_head_var_ready")
    hr = core.sem(name + "_head_rstd_ready")
    norm = Norm(core, name)

    with nc.Block() as block:
        @block.sync
        def _(sp):
            prefetch(sp)

        @block.gpsimd
        def _(pool):
            core.own_pool(pool, pool.memset(XZ, 0.0))
            pool.wait_ge(turn.ready, 2)
            for h in range(NH):
                r = slice(64 * (h % 2), 64 * (h % 2) + 64)
                pool.tensor_copy(XZ[r, h, :], core.XT[r, h // 2, :]).then_inc(xz, 1)
            pool.wait_ge(hv, 1)
            core.own_pool(pool, pool.tensor_scalar(RS, MV[:, :, 1], head_eps, None, ALU.add))
            pool.tensor_tensor(RS, RS, core.mhalf[:, 0:16], ALU.pow).then_inc(hr, 1)
            for t in range(TT):
                norm.pool(pool, t)

        @block.tensor
        def _(pe):
            turn.pe(pe)
            pe.wait_ge(turn.ready, 2)
            for c in range(6):
                rhs = core.XT[:, c, :] if c < 2 else core.CT[:, c % 2, :]
                last = pe.matmul(ps[4][0:FG_ROW + NH, :], core.gate[which][:, c, :], rhs, start=(c == 0), stop=(c == 5))
            last.then_inc(gates, 1)
            pe.wait_ge(rows, 1)
            for i, src in enumerate((A, NL)):
                for t in range(TT):
                    last = pe.transpose(ps[6 + i][:, 4 * t:4 * t + 4], src[0:NH, t * P:(t + 1) * P],
                                        core.ident[0:NH, 0:NH])
            last.then_inc(cols, 1)
            pe.wait_ge(at, 1)
            pe.wait_ge(en, 1)

            def spread(h):
                if h >= 1:
                    pe.wait_ge(dd, 4 * h)
                pe.matmul(ps[4][:, :], core.sel[:, h, :], NMR[0:NH, :], start=True, stop=True)
                pe.matmul(ps[5][:, :], core.sel[:, h, :], NMR[0:NH, :], start=True, stop=False)
                pe.matmul(ps[5][:, :], core.ident_bf[:, :], free(core.maskT_bf[:, :], (0, TT), (1, P)),
                          start=False, stop=True).then_inc(nm, 1)

            def scores(h):
                pe.wait_ge(xz, h + 1)
                for j in range(TT):
                    m = 4 * h + j
                    if m >= 2:
                        pe.wait_ge(cc, m - 1)
                    pe.matmul(ps[6 + m % 2][:, j * P:S], core.CT[:, h // 2, j * P:(j + 1) * P],
                              XZ[:, h, j * P:S], start=True, stop=True).then_inc(qk, 1)

            def values(h):
                pe.wait_ge(cc, 4 * (h + 1))
                for it in range(TT):
                    for j in range(it + 1):
                        o = offs[j] + (it - j) * P
                        last = pe.matmul(ps[it][:, h * (DH + 1):(h + 1) * (DH + 1)], CC[:, h % 2, o:o + P],
                                         core.CV[:, j, h, :], start=(j == 0), stop=(j == it))
                last.then_inc(pv, 1)

            for h in range(NH):
                spread(h)
                scores(h)
                if h >= 1:
                    values(h - 1)
            values(NH - 1)

        @block.scalar
        def _(act):
            turn.act(act)
            act.wait_ge(absf, 1)
            core.own_act(act, act.activation(AF[0:NH, :], AF[0:NH, :], ACT.Exp, scale=-1.0))
            act.activation(AF[0:NH, :], AF[0:NH, :], ACT.Ln, bias=1.0).then_inc(lnf, 1)
            act.wait_ge(cols, 1)
            act.activation(EN, ps[7][:, 0:16], ACT.Exp).then_inc(en, 1)
            act.wait_ge(at, 1)
            for h in range(NH):
                act.wait_ge(nm, h + 1)
                for j in range(TT):
                    m = 4 * h + j
                    if m >= 2:
                        act.wait_ge(cc, m - 1)
                    bias = AT[:, 4 * j + h:4 * j + h + 1]
                    last = act.activation(DD[:, m % 2, j * P:(j + 1) * P], ps[5][:, j * P:(j + 1) * P], ACT.Exp, bias=bias)
                    if j < TT - 1:
                        last = act.activation(DD[:, m % 2, (j + 1) * P:S], ps[4][:, (j + 1) * P:S], ACT.Exp, bias=bias)
                    last.then_inc(dd, 1)

        @block.vector
        def _(dve):
            own = core.own_dve
            g = slice(0, NH)
            turn.dve(dve)
            dve.wait_ge(gates, 1)
            own(dve, dve.tensor_scalar(FG[g, :], ps[4][FG_ROW:FG_ROW + NH, :], core.gate_bias[which][:, 1:2], None, ALU.add))
            absolute(dve, AF[g, :], FG[g, :]).then_inc(absf, 1)
            dve.tensor_scalar(IG[g, :], ps[4][g, :], core.gate_bias[which][:, 0:1], None, ALU.add)
            dve.wait_ge(lnf, 1)
            own(dve, dve.scalar_tensor_tensor(out=LF[g, :], in0=FG[g, :], scalar=0.0, in1=AF[g, :],
                                              op0=ALU.min, op1=ALU.subtract))
            own(dve, dve.tensor_tensor_scan(CUM[g, :], core.ones[g, :],
                                            LF[g, :], 0.0, ALU.mult, ALU.add))
            own(dve, dve.tensor_tensor(A[g, :], IG[g, :], CUM[g, :], ALU.subtract))
            own(dve, dve.tensor_tensor_scan(M[g, :], A[g, :], A[g, :], -3e38, ALU.max, ALU.max))
            dve.tensor_scalar(NMR[g, :], M[g, :], -1.0, None, ALU.mult)
            dve.scalar_tensor_tensor(out=NL[g, :], in0=CUM[g, :], scalar=-1.0, in1=M[g, :],
                                     op0=ALU.mult, op1=ALU.subtract).then_inc(rows, 1)
            dve.wait_ge(cols, 1)
            dve.tensor_copy(AT, ps[6][:, 0:16]).then_inc(at, 1)
            for m in range(4 * NH):
                h, j = m // 4, m % 4
                dve.wait_ge(qk, m + 1)
                dve.wait_ge(dd, m + 1)
                if j == 0 and h >= 2:
                    dve.wait_ge(pv, h - 1)
                dve.scalar_tensor_tensor(out=CC[:, h % 2, offs[j]:offs[j] + S - j * P], in0=ps[6 + m % 2][:, j * P:S],
                                         scalar=1.0 / math.sqrt(DH), in1=DD[:, m % 2, j * P:S],
                                         op0=ALU.mult, op1=ALU.mult).then_inc(cc, 1)
            dve.wait_ge(pv, NH)
            for t in range(TT):
                o = ps[t][:, 0:NH * (DH + 1)].rearrange("p (h d) -> p h d", h=NH)
                last = dve.tensor_copy(DN[:, 4 * t:4 * t + 4], o[:, :, DH])
            own(dve, last)
            own(dve, absolute(dve, DN, DN))
            dve.wait_ge(en, 1)
            own(dve, dve.tensor_tensor(DN, DN, EN, ALU.max))
            own(dve, dve.tensor_scalar(DN, DN, 1e-6, None, ALU.add))
            own(dve, dve.reciprocal(RD, DN))
            for t in range(TT):
                o = ps[t][:, 0:NH * (DH + 1)].rearrange("p (h d) -> p h d", h=NH)
                last = dve.tensor_tensor(HH[:, t], o[:, :, 0:DH], free(RD[:, 4 * t:4 * t + 1], (1, NH), (0, DH)), ALU.mult)
            own(dve, last)
            for n in range(16):
                last = dve.bn_stats(ST[:, n, :], HH[:, n // 4, n % 4, :])
            own(dve, last)
            for n in range(16):
                last = dve.bn_aggr(MV[:, n, :], ST[:, n, :])
            last.then_inc(hv, 1)
            dve.wait_ge(hr, 1)
            for n in range(16):
                last = dve.tensor_scalar(HH[:, n // 4, n % 4, :], HH[:, n // 4, n % 4, :], MV[:, n, 0:1], RS[:, n:n + 1],
                                         ALU.subtract, ALU.mult)
            own(dve, last)
            hh = HH.rearrange("p t h d -> p t (h d)")
            own(dve, dve.tensor_tensor(hh, hh, free(core.norm_w[which][:, :], (0, TT), (1, D)), ALU.mult))
            for t in range(TT):
                norm.stats(dve, t, hh[:, t, :])
            for t in range(TT):
                norm.apply(dve, t)



class Router:

    def __init__(self, core, a, name, wr, bias, extra, renormalise, gates_dram, x_in):
        self.x_in = x_in
        self.c, self.wr, self.bias, self.extra, self.renorm, self.dram = core, wr, bias, extra, renormalise, gates_dram
        self.n = 8 + extra
        self.L, self.NMX, self.SM = a.take(TT, 8), a.take(TT), a.take(TT)
        self.CMP, self.EQ = a.take(TT, 8, 8), a.take(TT, 8, 8)
        self.RK, self.G, self.GT = a.take(TT, 8), a.take(TT, self.n), a.take(S)
        s = lambda x: core.sem(f"{name}_{x}")
        self.logits, self.shifted, self.exped = s("logits_ready"), s("logits_shifted"), s("exp_logits_ready")
        self.gated, self.turned, self.gt, self.stored = s("gates_ready"), s("gates_turned"), s("gatesT_ready"), s("gates_stored")

    def pe(self, pe):
        c = self.c
        for t in range(TT):
            for k in range(DC):
                last = pe.matmul(c.ps[6][:, 8 * t:8 * t + 8], c.XT[:, k, t * P:(t + 1) * P], self.wr[:, k, :],
                                 start=(k == 0), stop=(k == DC - 1))
        last.then_inc(self.logits, 1)

    def pe_turn(self, pe):
        c = self.c
        pe.wait_ge(self.gated, 1)
        for t in range(TT):
            last = pe.transpose(c.ps[7][0:self.n, t * P:(t + 1) * P], self.G[:, t, :], c.ident[:, :])
        last.then_inc(self.turned, 1)
        pe.wait_ge(self.gt, 1)

    def act(self, act):
        act.wait_ge(self.shifted, 1)
        act.activation(self.L, self.L, ACT.Exp).then_inc(self.exped, 1)

    def dve(self, dve, parts):
        c, own = self.c, self.c.own_dve
        dve.wait_ge(self.x_in, 2)
        parts.x(dve)
        logits = c.ps[6][:, 0:8 * TT].rearrange("p (t e) -> p t e", t=TT)
        dve.wait_ge(self.logits, 1)
        if self.bias is not None:
            own(dve, dve.tensor_tensor(self.L, logits, free(self.bias[:, :], (0, TT), (1, 8)), ALU.add))
        else:
            own(dve, dve.tensor_copy(self.L, logits))
        own(dve, dve.tensor_reduce(self.NMX, self.L, AX.X, ALU.max, negate=True))
        dve.tensor_tensor(self.L, self.L, free(self.NMX, (1, TT), (0, 8)), ALU.add).then_inc(self.shifted, 1)
        dve.wait_ge(self.exped, 1)
        own(dve, dve.tensor_reduce(self.SM, self.L, AX.X, ALU.add))
        own(dve, dve.reciprocal(self.SM, self.SM))
        own(dve, dve.tensor_tensor(self.L, self.L, free(self.SM, (1, TT), (0, 8)), ALU.mult))
        sk, sj = free(self.L, (8, TT), (0, 8), (1, 8)), free(self.L, (8, TT), (1, 8), (0, 8))
        dve.tensor_tensor(self.CMP, sk, sj, ALU.is_gt)
        own(dve, dve.tensor_tensor(self.EQ, sk, sj, ALU.is_equal))
        own(dve, dve.tensor_tensor(self.EQ, self.EQ, free(c.tri[:, :, :], (0, TT), (8, 8), (1, 8)), ALU.mult))
        own(dve, dve.tensor_tensor(self.CMP, self.CMP, self.EQ, ALU.add))
        own(dve, dve.tensor_reduce(self.RK, self.CMP, AX.X, ALU.add))
        last = dve.scalar_tensor_tensor(out=self.G[:, :, 0:8], in0=self.RK, scalar=1.5, in1=self.L,
                                        op0=ALU.is_lt, op1=ALU.mult)
        if self.renorm:
            own(dve, last)
            own(dve, dve.tensor_reduce(self.SM, self.G, AX.X, ALU.add))
            own(dve, dve.reciprocal(self.SM, self.SM))
            last = dve.tensor_tensor(self.G, self.G, free(self.SM, (1, TT), (0, 8)), ALU.mult)
        if self.extra:
            last = dve.memset(self.G[:, :, 8:self.n], 1.0)
        last.then_inc(self.gated, 1)
        dve.wait_ge(self.turned, 1)
        dve.tensor_copy(self.GT[0:self.n, :], c.ps[7][0:self.n, :]).then_inc(self.gt, 1)

    def store(self, sp):
        sp.wait_ge(self.gt, 1)
        sp.dma_start(self.dram, self.GT[0:self.n, :]).then_inc(self.stored, 16)
        sp.wait_ge(self.stored, 16)


class Combine:

    def __init__(self, core, a, name):
        self.c, self.YT = core, a.take(DC, S)
        self.sum = core.sem(name + "_experts_summed")
        self.copied = core.sem(name + "_sum_copied")
        self.turned = core.sem(name + "_sum_turned")
        self.norm = Norm(core, name)

    def pe(self, pe):
        c = self.c
        pe.wait_ge(self.copied, 1)
        for t in range(TT):
            for k in range(DC):
                last = pe.transpose(c.ps[2 + t][:, k * P:(k + 1) * P],
                                    self.YT[:, k, t * P:(t + 1) * P], c.ident[:, :])
            last.then_inc(self.turned, 1)

    def dve(self, dve):
        c = self.c
        dve.wait_ge(self.sum, 1)
        dve.tensor_copy(self.YT[:, 0, :], c.ps[0][:, :])
        dve.tensor_copy(self.YT[:, 1, :], c.ps[1][:, :]).then_inc(self.copied, 1)
        for t in range(TT):
            dve.wait_ge(self.turned, t + 1)
            self.norm.stats(dve, t, c.ps[2 + t][:, 0:D])
        for t in range(TT):
            self.norm.apply(dve, t)


def raw0(core):
    return [core.work[:, W0_AT + i * W0:W0_AT + (i + 1) * W0] for i in range(2)]


def raw1(core):
    return [core.work[:, W1_AT + i * 2 * C1:W1_AT + (i + 1) * 2 * C1] for i in range(4)]


class Parts:

    def __init__(self, core, name, tensor, chunk, slots, hid):
        self.c = core
        at = 0

        def take(n):
            nonlocal at
            at += n
            return tensor[:, at - n:at]
        self.W = [[take(chunk) for _ in range(slots)] for _ in range(2)]
        self.X = [take(DC * S).rearrange("p (c n) -> p c n", c=DC) for _ in range(2)]
        self.H = [[take(S) for _ in range(hid)] for _ in range(2)]
        assert at == tensor.shape[1]
        self.x_parts = core.sem(name + "_x_parts_ready")

    def x(self, dve):
        dve.tensor_copy(self.X[0], self.c.XT[:, :, :]).then_inc(self.x_parts, 1)
        dve.wait_ge(self.x_parts, 1)
        rest(dve, self.X[1], self.c.XT[:, :, :], self.X[0]).then_inc(self.x_parts, 1)

    def product(self, pe, out, slot, at, rhs, ks, start=False, stop=False):
        n = 0
        for k in ks:
            for a, b in ((0, 0), (0, 1), (1, 0)):
                n += 1
                last = pe.matmul(out, self.W[a][slot][:, at(k):at(k) + P], rhs(b, k),
                                 start=start and n == 1, stop=stop and n == 3 * len(ks))
        return last


def rest(eng, out, x, hi):
    return eng.tensor_tensor(out, x, hi.bitcast(F32), ALU.subtract)


def silu_experts(core, w_in, prefetch):
    nc, ps = core.nc, core.ps
    a = core.arena()
    RAW = raw0(core)
    GB = a.take(2, S)
    BB = a.take(2, 4)
    SL, HF = a.take(2, S), a.take(2, S)
    turn = turn_x(core, "c")
    router = Router(core, a, "c", core.WR0, core.rb0, 2, False, core.dram["gates0"], turn.ready)
    combine = Combine(core, a, "c")
    assert a.at <= W0_AT and W0_AT + 2 * W0 <= WQKV_AT and WQKV_AT + DC * 3072 + PARTS0 <= core.size
    parts = Parts(core, "c", core.parts[0], C0, 4, 2)
    g_in = [core.sem(f"c_gate_loaded{i}") for i in range(2)]
    uwh, uwl = core.sem("c_up_weights_hi_ready"), core.sem("c_up_weights_lo_ready")
    dwh, dwl = core.sem("c_down_weights_hi_ready"), core.sem("c_down_weights_lo_ready")
    up, sl, sg = core.sem("c_up_ready"), core.sem("c_silu_ready"), core.sem("c_gated_silu_ready")
    hf = core.sem("c_hidden_ready")
    hh, hl = core.sem("c_hidden_hi_ready"), core.sem("c_hidden_lo_ready")
    dn = core.sem("c_down_done")
    pairs, UP = E0A // 2, 2 * DC * P

    def raw(r):
        return RAW[r // 2][:, r % 2 * C0:(r % 2 + 1) * C0]


    with nc.Block() as block:
        @block.sync
        def _(sp):
            router.store(sp)

            def gates(e, s):
                sp.dma_start(GB[:, s, :], row(core.dram["gates0"], e)).then_inc(g_in[s], 16)
                sp.dma_start(BB[:, s, :], core.dram["b_e0"][e]).then_inc(g_in[s], 16)
            for s in range(2):
                gates(s, s)
            with sp.Fori(0, pairs - 1) as i:
                for s in range(2):
                    sp.wait_ge(uwl, 4 * i + (2 * s + 2))
                    sp.wait_ge(dwl, 4 * i + (2 * s + 2))
                    sp.dma_start(RAW[s], core.dram["w_e0"][2 * i + (2 + s)]).then_inc(w_in[s], 16)
                for s in range(2):
                    sp.wait_ge(hf, 4 * i + (2 * s + 4))
                    gates(2 * i + (2 + s), s)
            prefetch(sp)

        @block.tensor
        def _(pe):
            turn.pe(pe)
            pe.wait_ge(turn.ready, 2)
            router.pe(pe)
            pe.wait_ge(parts.x_parts, 2)

            def up_chunk(i, r):
                pe.wait_ge(uwl, 4 * i + (r + 1))
                pe.wait_ge(hf, 4 * i + (r + 1))
                for kind in range(2):
                    last = parts.product(pe, ps[2 + 2 * (r % 2) + kind][:, :], r, lambda k: (kind * DC + k) * P,
                                         lambda b, k: parts.X[b][:, k, :], range(DC), start=True, stop=True)
                last.then_inc(up, 1)

            def down_chunk(i, r, end):
                pe.wait_ge(dwl, 4 * i + (r + 1))
                pe.wait_ge(hl, 4 * i + (r + 1))
                for d in range(DC):
                    last = parts.product(pe, ps[d][:, :], r, lambda k: (2 * DC + d) * P,
                                         lambda b, k: parts.H[b][r % 2], (0,), stop=end)
                last.then_inc(combine.sum if end else dn, 1)

            up_chunk(0, 0)
            up_chunk(0, 1)
            router.pe_turn(pe)
            for k in range(DC):
                pe.matmul(ps[k][:, :], core.B2[:, k * P:(k + 1) * P], router.GT[0:E0A, :], start=True, stop=False)
            with pe.Fori(0, pairs - 1) as i:
                for r in range(4):
                    up_chunk(i + (r + 2) // 4, (r + 2) % 4)
                    down_chunk(i, r, False)
            for r in range(4):
                if r < 2:
                    up_chunk(pairs - 1, r + 2)
                down_chunk(pairs - 1, r, r == 3)
            combine.pe(pe)

        @block.scalar
        def _(act):
            turn.act(act)

            def up_weights_hi(i, r):
                act.wait_ge(w_in[r // 2], 16 * i + 16)
                act.copy(parts.W[0][r][:, 0:UP], raw(r)[:, 0:UP]).then_inc(uwh, 1)

            def down_weights_hi(i, r):
                act.wait_ge(dn, 4 * i + (r + 1))
                act.copy(parts.W[0][r][:, UP:C0], raw(r)[:, UP:C0]).then_inc(dwh, 1)

            def chunk(i, r, end):
                act.wait_ge(g_in[r // 2], 32 * i + 32)
                act.wait_ge(up, 4 * i + (r + 1))
                act.activation(SL[:, r % 2, :], ps[2 + 2 * (r % 2)][:, :], ACT.Silu,
                               bias=BB[:, r // 2, r % 2:r % 2 + 1]).then_inc(sl, 1)
                if r == 0 or not end:
                    up_weights_hi(i + (r + 3) // 4, (r + 3) % 4)
                act.wait_ge(hf, 4 * i + (r + 3))
                act.wait_ge(dn, 4 * i + (r + 3))
                act.copy(parts.H[0][r % 2], HF[:, r % 2, :]).then_inc(hh, 1)
                if r == 0 or not end:
                    down_weights_hi(i + (r + 3) // 4, (r + 3) % 4)

            for r in range(3):
                up_weights_hi(0, r)
                down_weights_hi(0, r)
            router.act(act)
            with act.Fori(0, pairs - 1) as i:
                for r in range(4):
                    chunk(i, r, False)
            for r in range(4):
                chunk(pairs - 1, r, True)

        @block.gpsimd
        def _(pool):
            def up_weights_lo(i, r):
                pool.wait_ge(uwh, 4 * i + (r + 1))
                rest(pool, parts.W[1][r][:, 0:UP], raw(r)[:, 0:UP], parts.W[0][r][:, 0:UP]).then_inc(uwl, 1)

            def down_weights_lo(i, r):
                pool.wait_ge(dwh, 4 * i + (r + 1))
                rest(pool, parts.W[1][r][:, UP:C0], raw(r)[:, UP:C0], parts.W[0][r][:, UP:C0]).then_inc(dwl, 1)

            def chunk(i, r, end):
                pool.wait_ge(g_in[r // 2], 32 * i + 32)
                pool.wait_ge(sl, 4 * i + (r + 1))
                pool.tensor_tensor(SL[:, r % 2, :], SL[:, r % 2, :], GB[:, r // 2, :], ALU.mult).then_inc(sg, 1)
                if r == 0 or not end:
                    up_weights_lo(i + (r + 3) // 4, (r + 3) % 4)
                if r < 2 or not end:
                    down_weights_lo(i + (r + 2) // 4, (r + 2) % 4)

            for r in range(3):
                up_weights_lo(0, r)
                if r < 2:
                    down_weights_lo(0, r)
            with pool.Fori(0, pairs - 1) as i:
                for r in range(4):
                    chunk(i, r, False)
            for r in range(4):
                chunk(pairs - 1, r, True)
            for t in range(TT):
                combine.norm.pool(pool, t)

        @block.vector
        def _(dve):
            dve.sem_inc(hf, 2)
            dve.sem_inc(dn, 4)
            turn.dve(dve)
            router.dve(dve, parts)
            with dve.Fori(0, pairs) as i:
                for r in range(4):
                    dve.wait_ge(sg, 4 * i + (r + 1))
                    dve.scalar_tensor_tensor(out=HF[:, r % 2, :], in0=ps[3 + 2 * (r % 2)][:, :],
                                             scalar=BB[:, r // 2, 2 + r % 2:3 + r % 2], in1=SL[:, r % 2, :],
                                             op0=ALU.add, op1=ALU.mult).then_inc(hf, 1)
                    dve.wait_ge(hh, 4 * i + (r + 1))
                    rest(dve, parts.H[1][r % 2], HF[:, r % 2, :], parts.H[0][r % 2]).then_inc(hl, 1)
            combine.dve(dve)


def row(dram, e):
    return (dram[e, :] if isinstance(e, int) else dram[bass.ds(e, 1), :]).partition_broadcast(P)


def relu_experts(core, w_in, b):
    nc, ps = core.nc, core.ps
    a = core.arena()
    RAW = raw1(core)
    GB, HF = a.take(2, S), a.take(4, S)
    turn = turn_x(core, "f")
    router = Router(core, a, "f", core.WR1, None, 0, True, core.dram["gates1"], turn.ready)
    combine = Combine(core, a, "f")
    assert a.at <= W1_AT and W1_AT + W1 + PARTS1 <= core.size
    parts = Parts(core, "f", core.parts[1], C1, 8, 4)
    g_in = [core.sem(f"f_gate_loaded{i}") for i in range(2)]
    wh, wl = core.sem("f_weights_hi_ready"), core.sem("f_weights_lo_ready")
    up = core.sem("f_up_ready")
    hf = core.sem("f_hidden_ready")
    hh, hl = core.sem("f_hidden_hi_ready"), core.sem("f_hidden_lo_ready")
    dn = core.sem("f_down_done")
    stored = core.sem("f_out_stored")
    pairs, MC, LEAD = E1 // 2, F1 // P, 4
    N = 2 * MC

    def raw(r):
        return RAW[r % MC // 2][:, r % 2 * C1:(r % 2 + 1) * C1]

    with nc.Block() as block:
        @block.sync
        def _(sp):
            router.store(sp)

            def gates(e, s):
                sp.dma_start(GB[:, s, :], row(core.dram["gates1"], e)).then_inc(g_in[s], 16)

            def weights(i, s, e):
                for k in range(4):
                    sp.wait_ge(wl, N * i + (MC * s + 2 * k + 2))
                    sp.dma_start(RAW[k], core.dram["w_e1"][e][:, 2 * k * C1:2 * (k + 1) * C1]).then_inc(w_in[k], 16)
            for s in range(2):
                gates(s, s)
            with sp.Fori(0, pairs - 1) as i:
                weights(i, 0, 2 * i + 1)
                sp.wait_ge(hf, N * i + (MC + 4))
                gates(2 * i + 2, 0)
                weights(i, 1, 2 * i + 2)
                sp.wait_ge(hf, N * i + (2 * MC + 4))
                gates(2 * i + 3, 1)
            weights(pairs - 1, 0, E1 - 1)
            for t in range(TT):
                sp.wait_ge(combine.norm.x_ready, t + 1)
                sp.dma_start(core.dram["out"][b, t * P:(t + 1) * P, :], core.X[:, t, :]).then_inc(stored, 16)
            sp.wait_ge(stored, 16 * TT)

        @block.tensor
        def _(pe):
            turn.pe(pe)
            pe.wait_ge(turn.ready, 2)
            router.pe(pe)
            for k in range(DC):
                pe.matmul(ps[k][:, :], core.ident_bf[:, :], core.zero_bf[:, :], start=True, stop=False)
            pe.wait_ge(parts.x_parts, 2)

            def up_chunk(i, r):
                pe.wait_ge(wl, N * i + (r + 1))
                pe.wait_ge(hf, N * i + (r + 1))
                parts.product(pe, ps[2 + r % 4][:, :], r % MC, lambda k: k * P, lambda b, k: parts.X[b][:, k, :],
                              range(DC), start=True, stop=True).then_inc(up, 1)

            def down_chunk(i, r, end):
                pe.wait_ge(hl, N * i + (r + 1))
                for d in range(DC):
                    last = parts.product(pe, ps[d][:, :], r % MC, lambda k: (DC + d) * P,
                                         lambda b, k: parts.H[b][r % 4], (0,), stop=end)
                last.then_inc(combine.sum if end else dn, 1)

            up_chunk(0, 0)
            up_chunk(0, 1)
            router.pe_turn(pe)
            with pe.Fori(0, pairs - 1) as i:
                for r in range(N):
                    up_chunk(i + (r + 2) // N, (r + 2) % N)
                    down_chunk(i, r, False)
            for r in range(N):
                if r + 2 < N:
                    up_chunk(pairs - 1, r + 2)
                down_chunk(pairs - 1, r, r == N - 1)
            combine.pe(pe)

        @block.scalar
        def _(act):
            turn.act(act)

            def weights_hi(i, r):
                act.wait_ge(w_in[r % MC // 2], 32 * i + (16 * (r // MC) + 16))
                act.wait_ge(dn, N * i + (r + 1))
                act.copy(parts.W[0][r % MC], raw(r)).then_inc(wh, 1)

            def chunk(i, r, end):
                if r + LEAD < N or not end:
                    weights_hi(i + (r + LEAD) // N, (r + LEAD) % N)
                act.wait_ge(hf, N * i + (r + 5))
                act.wait_ge(dn, N * i + (r + 5))
                act.copy(parts.H[0][r % 4], HF[:, r % 4, :]).then_inc(hh, 1)

            act.wait_ge(dn, MC)
            for r in range(LEAD):
                weights_hi(0, r)
            router.act(act)
            with act.Fori(0, pairs - 1) as i:
                for r in range(N):
                    chunk(i, r, False)
            for r in range(N):
                chunk(pairs - 1, r, True)

        @block.gpsimd
        def _(pool):
            with pool.Fori(0, pairs) as i:
                for r in range(N):
                    pool.wait_ge(wh, N * i + (r + 1))
                    rest(pool, parts.W[1][r % MC], raw(r), parts.W[0][r % MC]).then_inc(wl, 1)
            for t in range(TT):
                combine.norm.pool(pool, t)

        @block.vector
        def _(dve):
            dve.sem_inc(hf, 4)
            dve.sem_inc(dn, MC)
            turn.dve(dve)
            router.dve(dve, parts)

            def hidden(i, r):
                if r % MC == 0:
                    dve.wait_ge(g_in[r // MC], 16 * i + 16)
                dve.wait_ge(up, N * i + (r + 1))
                dve.scalar_tensor_tensor(out=HF[:, r % 4, :], in0=ps[2 + r % 4][:, :], scalar=0.0,
                                         in1=GB[:, r // MC, :], op0=ALU.max, op1=ALU.mult).then_inc(hf, 1)

            def hidden_lo(i, r):
                dve.wait_ge(hh, N * i + (r + 1))
                rest(dve, parts.H[1][r % 4], HF[:, r % 4, :], parts.H[0][r % 4]).then_inc(hl, 1)

            hidden(0, 0)
            with dve.Fori(0, pairs - 1) as i:
                for r in range(N):
                    hidden(i + (r + 1) // N, (r + 1) % N)
                    hidden_lo(i, r)
            for r in range(N):
                if r + 1 < N:
                    hidden(pairs - 1, r + 1)
                hidden_lo(pairs - 1, r)
            combine.dve(dve)



def rope_attention(core):
    nc, ps = core.nc, core.ps
    a = core.arena()
    QT, KT, V = a.take(8, S), a.take(8, S), a.take(TT, H1 * HD1)
    assert a.at == WQKV_AT
    SC = a.take(S, H1)
    W = core.work[:, WQKV_AT:WQKV_AT + DC * 3072].rearrange("p (c n) -> p c n", c=DC)
    end = a.at
    M1, M2, RT = a.take(2, S), a.take(2, S), a.take(4, S)
    a.at = end
    TS, HS, HG = a.take(2, S), a.take(2, S), a.take(4, S)
    PR, PTS = a.take(3, S), a.take(2, S)
    QZ = a.take(H1, P)
    MG = a.take(JG // 2, H1)
    RX = HS.rearrange("p a b -> p (a b)")
    OT = TS.rearrange("p a b -> p (a b)").rearrange("p (c t) -> p c t", c=8)
    NM, DEN, RD = a.take(64), a.take(64), a.take(64)

    turn = turn_x(core, "d")
    s = lambda x: core.sem("d_" + x)
    proj, roped, vcop = s("projected"), s("rope_products_ready"), s("v_ready")
    rot, tq, qk = s("rotated"), s("qk_turned"), s("qkT_ready")
    sc, scc, tt_, tev, kf = s("scores_ready"), s("scores_copied"), s("scores_turned"), s("scoresT_ready"), s("kerple_added")
    h1, hs, gl, l2, fa = s("hidden_product"), s("hidden_biased"), s("gelu_ready"), s("refined_ready"), s("refined_added")
    mx, ex, tr, pt, pv = s("max_ready"), s("probs_ready"), s("probs_turned"), s("probsT_ready"), s("values_done")
    bcc = s("spread_inverses_copied")
    rd, bc, otr, y = s("denominators_inverted"), s("inverses_spread"), s("outT_ready"), s("y_ready")
    qz, gm = s("padded_q_ready"), s("group_max_ready")
    norm = Norm(core, "d")
    base = [2 * it * (it + 1) for it in range(TT + 1)]
    last_group = lambda it: 4 * (it + 1) - 1

    def table(it, g, hf):
        o = P * (it + 1) - JG * g - 24 - 4 * hf
        return free(core.TB[:, o:o + 1], (8, 4), (1, P))

    with nc.Block() as block:
        @block.gpsimd
        def _(pool):
            def pad_q(it):
                pool.wait_ge(qk, 4 * (it + 1))
                if it >= 1:
                    pool.wait_ge(sc, H1 * it)
                    pool.wait_ge(kf, base[it])
                else:
                    pool.wait_ge(rot, 4 * 3)
                for k in range(2):
                    r = slice(64 * k, 64 * k + 64)
                    pool.tensor_copy(QZ[r].rearrange("p (h k) t -> p h k t", k=2)[:, :, k, :],
                                     QT[r, :, it * P:(it + 1) * P]).then_inc(qz, 1)
                pool.wait_ge(qz, 2 * (it + 1))

            core.own_pool(pool, pool.memset(QZ, 0.0))
            for t in range(TT):
                for i in range(4):
                    n = 4 * t + i
                    pool.wait_ge(roped, n + 1)
                    if t >= 1 and i == 0:
                        pool.wait_ge(tq, 4 * t)
                    pool.tensor_tensor(RT[:, i, :], M1[:, n % 2, :], M2[:, n % 2, :], ALU.add).then_inc(rot, 1)
                if t == 2:
                    pad_q(0)
            for it in range(TT):
                for g in range(last_group(it) + 1):
                    n = base[it] + g
                    pool.wait_ge(tt_, n + 1)
                    v = S - P - it * P + g * JG
                    pool.tensor_tensor(SC[:, g * JG:(g + 1) * JG, :], SC[:, g * JG:(g + 1) * JG, :],
                                       core.KF[:, v:v + JG, :], ALU.add).then_inc(kf, 1)
                if it + 1 < TT:
                    pad_q(it + 1)
            for t in range(TT):
                norm.pool(pool, t)

        @block.tensor
        def _(pe):
            turn.pe(pe)
            pe.wait_ge(turn.ready, 2)

            def project(t):
                for i in range(6):
                    if t >= 1:
                        if i < 4:
                            pe.wait_ge(roped, 4 * (t - 1) + i + 1)
                        else:
                            pe.wait_ge(vcop, 2 * (t - 1) + i - 3)
                    for k in range(DC):
                        last = pe.matmul(ps[i][:, :], core.XT[:, k, t * P:(t + 1) * P],
                                         W[:, k, i * 512:(i + 1) * 512], start=(k == 0), stop=(k == DC - 1))
                    last.then_inc(proj, 1)

            def turn_qk(t):
                for i in range(4):
                    n = 4 * t + i
                    pe.wait_ge(rot, n + 1)
                    if n >= 2:
                        pe.wait_ge(qk, n - 1)
                    for j in range(4):
                        last = pe.transpose(ps[6 + n % 2][:, j * P:(j + 1) * P], RT[:, i, j * P:(j + 1) * P],
                                            core.ident[:, :])
                    last.then_inc(tq, 1)

            def scores(it):
                if it >= 1:
                    pe.wait_ge(pt, H1 * it)
                else:
                    pe.wait_ge(roped, 4 * (TT - 1) + 2)
                pe.wait_ge(qz, 2 * (it + 1))
                for h in range(H1):
                    n = H1 * it + h
                    if h >= 2:
                        pe.wait_ge(scc, n - 1)
                    pe.matmul(ps[n % 2][:, 0:(it + 1) * P], QZ[:, h, :], KT[:, h // 2, 0:(it + 1) * P], start=True, stop=True).then_inc(sc, 1)

            def turn_scores(it, g):
                n = base[it] + g
                if n >= 1:
                    pe.wait_ge(tev, n)
                for j in range(4):
                    last = pe.transpose(ps[2][:, (3 - j) * P:(4 - j) * P], SC[:, g * JG + 8 * j:g * JG + 8 * j + 8, :],
                                        core.ident[:, :])
                last.then_inc(tt_, 1)

            def hidden(it, g):
                n = base[it] + g
                pe.wait_ge(tev, n + 1)
                for hf in range(2):
                    if n >= 1:
                        pe.wait_ge(hs, 2 * n + hf - 1)
                    pe.matmul(ps[3 + hf][:, :], core.W1S[:, hf, :], TS[:, n % 2, :], start=True,
                              stop=True).then_inc(h1, 1)

            def refine(it, g):
                n = base[it] + g
                pe.wait_ge(gl, 2 * n + 2)
                if n >= 1:
                    pe.wait_ge(fa, n)
                for j in range(4):
                    for hf in range(2):
                        o = (8 * j + 4 * hf) * H1
                        last = pe.matmul(ps[5][:, o:o + 64], HG[:, (2 * n + hf) % 4, (3 - j) * P:(4 - j) * P],
                                         core.W2B[:, :], start=True, stop=True)
                last.then_inc(l2, 1)

            def turn_probs(it, h):
                n = H1 * it + h
                pe.wait_ge(ex, n + 1)
                if h >= 2:
                    pe.wait_ge(pt, n - 1)
                for j in range(it + 1):
                    last = pe.transpose(ps[n % 2][:, j * P:(j + 1) * P], PR[:, n % 3, j * P:(j + 1) * P],
                                        core.ident[:, :])
                last.then_inc(tr, 1)

            def values(it, h):
                n = H1 * it + h
                pe.wait_ge(pt, n + 1)
                rows = slice(h % 2 * HD1, (h % 2 + 1) * HD1)
                for j in range(it + 1):
                    last = pe.matmul(ps[6 + h // 8][rows, h % 8 // 2 * P:(h % 8 // 2 + 1) * P],
                                     V[:, j, h * HD1:(h + 1) * HD1], PTS[:, n % 2, j * P:(j + 1) * P],
                                     start=(j == 0), stop=(j == it))
                last.then_inc(pv, 1)

            def spread_inverses(it):
                pe.wait_ge(rd, it + 1)
                for p in range(H1 // 2):
                    last = pe.matmul(ps[3 + p // 4][:, (p % 4) * P:(p % 4 + 1) * P],
                                     RX[:, p * P:(p + 1) * P], core.ident[:, :], start=True, stop=True)
                last.then_inc(bc, 1)

            def out(it):
                pe.wait_ge(otr, it + 1)
                for c in range(8):
                    last = pe.matmul(ps[5][:, 0:D], OT[:, c, :], core.WO1[:, c, :], start=(c == 0), stop=(c == 7))
                last.then_inc(y, 1)

            project(0)
            for t in range(TT):
                if t + 1 < TT:
                    project(t + 1)
                else:
                    scores(0)
                turn_qk(t)
            for it in range(TT):
                pe.wait_ge(scc, H1 * (it + 1))
                if it >= 1:
                    pe.wait_ge(norm.var_ready, it)
                turn_scores(it, 0)
                for g in range(last_group(it) + 1):
                    if g < last_group(it):
                        turn_scores(it, g + 1)
                    hidden(it, g)
                    if g >= 1:
                        refine(it, g - 1)
                refine(it, last_group(it))
                if it == 0:
                    pe.wait_ge(vcop, 2 * TT)
                for h in range(H1 + 1):
                    if h < H1:
                        turn_probs(it, h)
                    if h >= 1:
                        values(it, h - 1)
                spread_inverses(it)
                if it == 0:
                    pe.wait_ge(qk, 4 * TT)
                if it + 1 < TT:
                    scores(it + 1)
                out(it)

        @block.scalar
        def _(act):
            def copy_turned(act, t):
                for i in range(4):
                    n = 4 * t + i
                    act.wait_ge(tq, n + 1)
                    dst = (QT if i < 2 else KT)[:, 4 * (i % 2):4 * (i % 2) + 4, t * P:(t + 1) * P]
                    act.mul(dst, ps[6 + n % 2][:, :].rearrange("p (a b) -> p a b", a=4),
                            1.0 if i < 2 else 1.0 / math.sqrt(HD1)).then_inc(qk, 1)

            turn.act(act)
            for t in range(TT):
                for i in range(2):
                    act.wait_ge(proj, 6 * t + 5 + i)
                    act.copy(V[:, t, i * 512:(i + 1) * 512], ps[4 + i][:, :]).then_inc(vcop, 1)
                if t >= 1:
                    copy_turned(act, t - 1)

            def copy_scores(it):
                for h in range(H1):
                    n = H1 * it + h
                    act.wait_ge(sc, n + 1)
                    act.copy(SC[:, 0:(it + 1) * P, h], ps[n % 2][:, 0:(it + 1) * P]).then_inc(scc, 1)

            copy_scores(0)
            copy_turned(act, TT - 1)
            for it in range(TT):
                for g in range(last_group(it) + 1):
                    n = base[it] + g
                    for hf in range(2):
                        z = 2 * n + hf
                        act.wait_ge(hs, z + 1)
                        if z >= 4:
                            act.wait_ge(l2, n - 1)
                        act.activation(HG[:, z % 4, :], HS[:, z % 2, :], ACT.Gelu).then_inc(gl, 1)
                act.wait_ge(mx, it + 1)
                w = (it + 1) * P
                for h in range(H1):
                    n = H1 * it + h
                    if n >= 3:
                        act.wait_ge(tr, n - 2)
                    act.activation(PR[:, n % 3, 0:w], SC[:, 0:w, h], ACT.Exp, bias=NM[:, n:n + 1],
                                   accum_out=DEN[:, n:n + 1]).then_inc(ex, 1)
                act.wait_ge(bc, it + 1)
                act.copy(HG[:, 0, :], ps[3][:, :])
                act.copy(HG[:, 1, :], ps[4][:, :]).then_inc(bcc, 1)
                if it + 1 < TT:
                    copy_scores(it + 1)

        @block.vector
        def _(dve):
            own = core.own_dve
            turn.dve(dve)
            for t in range(TT):
                for i in range(4):
                    n = 4 * t + i
                    dve.wait_ge(proj, 6 * t + i + 1)
                    if n >= 2:
                        dve.wait_ge(rot, n - 1)
                    x = ps[i][:, :].rearrange("p (h d) -> p h d", h=8)
                    m1 = M1[:, n % 2, :].rearrange("p (h d) -> p h d", h=8)
                    m2 = M2[:, n % 2, :].rearrange("p (h d) -> p h d", h=8)
                    dve.tensor_tensor(m1, x, free(core.rope[:, t, 0, :], (0, 8), (1, HD1)), ALU.mult)
                    dve.tensor_tensor(m2[:, :, 0:32], x[:, :, 32:64], free(core.rope[:, t, 1, 0:32], (0, 8), (1, 32)), ALU.mult)
                    dve.tensor_tensor(m2[:, :, 32:64], x[:, :, 0:32], free(core.rope[:, t, 1, 32:64], (0, 8), (1, 32)),
                                      ALU.mult).then_inc(roped, 1)

            def copy_turned_scores(it, g):
                n = base[it] + g
                dve.wait_ge(tt_, n + 1)
                if n >= 2:
                    dve.wait_ge(h1, 2 * (n - 1))
                if g == 0 and it >= 1:
                    dve.wait_ge(y, it)
                dve.tensor_copy(TS[:, n % 2, :], ps[2][:, :]).then_inc(tev, 1)

            def add_refined(it, g):
                n = base[it] + g
                dve.wait_ge(l2, n + 1)
                dve.wait_ge(kf, n + 1)
                c = SC[:, g * JG:(g + 1) * JG, :]
                dve.tensor_tensor(c, ps[5][:, :].rearrange("p (j h) -> p j h", h=H1), c, ALU.add).then_inc(fa, 1)
                dve.wait_ge(fa, n + 1)
                dve.tensor_reduce(MG[:, g, :], c.rearrange("p j h -> p h j"), AX.X, ALU.max).then_inc(gm, 1)

            for it in range(TT):
                w = (it + 1) * P
                copy_turned_scores(it, 0)
                for g in range(last_group(it) + 1):
                    if g < last_group(it):
                        copy_turned_scores(it, g + 1)
                    n = base[it] + g
                    for hf in range(2):
                        z = 2 * n + hf
                        dve.wait_ge(h1, z + 1)
                        if z >= 2:
                            dve.wait_ge(gl, z - 1)
                        dve.tensor_tensor(HS[:, z % 2, :].rearrange("p (c i) -> p c i", c=4),
                                          ps[3 + hf][:, :].rearrange("p (c i) -> p c i", c=4), table(it, g, hf),
                                          ALU.add).then_inc(hs, 1)
                    if g >= 1:
                        add_refined(it, g - 1)
                add_refined(it, last_group(it))
                dve.wait_ge(gm, base[it + 1])
                dve.tensor_reduce(NM[:, H1 * it:H1 * (it + 1)],
                                  MG[:, 0:last_group(it) + 1, :].rearrange("p g h -> p h g"), AX.X, ALU.max,
                                  negate=True).then_inc(mx, 1)
                for h in range(H1):
                    n = H1 * it + h
                    dve.wait_ge(tr, n + 1)
                    if n >= 2:
                        dve.wait_ge(pv, n - 1)
                    dve.tensor_copy(PTS[:, n % 2, 0:w], ps[n % 2][:, 0:w]).then_inc(pt, 1)
                dve.wait_ge(ex, H1 * (it + 1))
                inverse = RD[:, H1 * it:H1 * (it + 1)]
                own(dve, dve.reciprocal(inverse, DEN[:, H1 * it:H1 * (it + 1)]))
                dve.tensor_copy(RX.rearrange("p (h d) -> p h d", h=H1), free(inverse, (1, H1), (0, HD1))).then_inc(rd, 1)
                dve.wait_ge(pv, H1 * (it + 1))
                dve.wait_ge(bcc, it + 1)
                for k in range(2):
                    last = dve.tensor_tensor(OT[:, 4 * k:4 * k + 4, :], ps[6 + k][:, :].rearrange("p (c t) -> p c t", c=4),
                                             HG[:, k, :].rearrange("p (c t) -> p c t", c=4), ALU.mult)
                last.then_inc(otr, 1)
                dve.wait_ge(y, it + 1)
                norm.stats(dve, it, ps[5][:, 0:D])
            for t in range(TT):
                norm.apply(dve, t)



def decoder(nc, dram, layers=LAYERS):
    with ExitStack() as ctx:
        core = Core(nc, ctx, dram)
        with core.semaphores():
            setup(core)
        with nc.Fori(0, B) as b:
            with core.semaphores():
                layer0(core, b, layers)
            with core.semaphores():
                layer1(core, b, layers)


def layer0(core, b, layers):
    dram, none = core.dram, lambda sp: None
    weights_in = [core.sem(f"c_weights_loaded{i}") for i in range(2)]
    qkv_in = core.sem("d_weights_loaded")

    def first_experts(sp):
        for s in range(2):
            sp.dma_start(raw0(core)[s], dram["w_e0"][s]).then_inc(weights_in[s], 16)

    def qkv(sp):
        sp.dma_start(core.work[:, WQKV_AT:WQKV_AT + DC * 3072].rearrange("p (c n) -> p c n", c=DC),
                     dram["w_qkv"].rearrange("(c p) n -> p c n", p=P)).then_inc(qkv_in, 16)
        sp.wait_ge(qkv_in, 16)

    phase_attention(core, b)
    if layers > 1:
        mlstm(core, 0, "b", 1e-6, first_experts if layers > 2 else none)
    if layers > 2:
        silu_experts(core, weights_in, qkv if layers > 3 else none)


def layer1(core, b, layers):
    dram, none = core.dram, lambda sp: None
    weights_in = [core.sem(f"f_weights_loaded{i}") for i in range(4)]

    def first_experts(sp):
        for k in range(4):
            sp.dma_start(raw1(core)[k], dram["w_e1"][0][:, 2 * k * C1:2 * (k + 1) * C1]).then_inc(weights_in[k], 16)

    if layers > 3:
        rope_attention(core)
    if layers > 4:
        mlstm(core, 1, "e", 1e-5, first_experts if layers > 5 else none)
    if layers > 5:
        relu_experts(core, weights_in, b)
    else:
        st = core.sem("dev_store")
        with core.nc.Block() as block:
            @block.sync
            def _(sp):
                sp.dma_start(dram["out"][b].rearrange("(t p) d -> p t d", p=P), core.X[:, :, :]).then_inc(st, 16)
                sp.wait_ge(st, 16)


def _constants():
    i = np.arange(P)
    mask = np.where(i[None, :] > i[:, None], np.float32(NEG), np.float32(0)).astype(np.float32)
    c = {"ident": np.eye(P, dtype=np.float32), "mask": mask}
    c["maskT"] = mask.T
    sel = np.zeros((NH, NH, P), np.float32)
    for h in range(NH):
        sel[h, h] = 1.0
    c["sel"] = sel
    e = np.arange(8)
    c["tri"] = np.broadcast_to((e[None, :] < e[:, None]).astype(np.float32), (P, 8, 8)).copy()
    inv = (1.0 / np.float32(10000.0) ** (np.arange(0, HD1, 2, dtype=np.float32) / np.float32(HD1))).astype(np.float32)
    f = np.outer(np.arange(S, dtype=np.float32), inv).astype(np.float32)
    cos, sin = np.cos(f), np.sin(f)
    rope = np.stack([np.concatenate([cos, cos], 1), np.concatenate([-sin, sin], 1)], 1)
    c["rope"] = np.ascontiguousarray(rope.reshape(TT, P, 2, HD1).transpose(1, 0, 2, 3)).astype(np.float32)
    jj = np.repeat(np.arange(4), H1)
    c["dist_c"] = np.abs(np.arange(640)[None, :] - P - jj[:, None]).astype(np.float32)
    c["dist_r"] = np.abs(i[:, None] - np.arange(S)[None, :] + (S - P)).astype(np.float32)
    return c


def _block_diagonal(w, n):
    k, m = w.shape
    out = np.zeros((n * k, n * m), w.dtype)
    for i in range(n):
        out[i * k:(i + 1) * k, i * m:(i + 1) * m] = w
    return out


def _gate_columns(ig, fg):
    out = np.zeros((ig.shape[0], FG_ROW + NH), ig.dtype)
    out[:, 0:NH], out[:, FG_ROW:] = ig, fg
    return out


def _arrays(i):
    g = {k: np.asarray(v) for k, v in i.items()}
    a = dict(_constants())
    a["x"], a["ctx"] = g["x"], g["ctx_1024"]
    a["wa"] = np.concatenate([g["L0_attn_" + n] for n in ("Wq", "Wk", "Wqp", "Wkp", "Wv")], 1)
    a["woa"] = g["L0_attn_Wo"]
    a["lambda"] = g["L0_attn_lambda_raw"]
    a["gate0"] = _gate_columns(g["L0_xattn_ig_kernel"], g["L0_xattn_fg_kernel"])
    a["gate_bias0"] = np.stack([g["L0_xattn_ig_bias"], g["L0_xattn_fg_bias"]], 1)
    a["norm_w0"] = g["L0_xattn_outnorm_weight"].reshape(-1)
    a["gate1"] = _gate_columns(g["L1_xattn_w_igate"].T, g["L1_xattn_w_fgate"].T)
    a["gate_bias1"] = np.stack([g["L1_xattn_b_igate"], g["L1_xattn_b_fgate"]], 1)
    a["norm_w1"] = g["L1_xattn_ln_weight"]
    a["wr0"] = g["L0_ffn_gate_w"].T
    a["rb0"] = g["L0_ffn_gate_b"]

    w1 = np.concatenate([g["L0_ffn_w1"], g["L0_ffn_ws1"].reshape(2, I0, D)], 0)
    w3 = np.concatenate([g["L0_ffn_w3"], g["L0_ffn_ws3"].reshape(2, I0, D)], 0)
    w2 = np.concatenate([g["L0_ffn_w2"], g["L0_ffn_ws2"].reshape(D, 2, I0).transpose(1, 0, 2)], 0)
    b1 = np.concatenate([g["L0_ffn_b1"], g["L0_ffn_bs1"].reshape(2, I0)], 0)
    b3 = np.concatenate([g["L0_ffn_b3"], g["L0_ffn_bs3"].reshape(2, I0)], 0)
    def columns(w, m):
        return w[:, m * P:(m + 1) * P].reshape(DC, P, P).transpose(1, 0, 2).reshape(P, -1)
    a["w_e0"] = np.stack([np.concatenate([x for m in range(I0 // P) for x in (
        columns(w1[e].T, m), columns(w3[e].T, m), w2[e].T[m * P:(m + 1) * P])], 1) for e in range(E0A)])
    a["b_e0"] = np.stack([np.concatenate([b1[e].reshape(2, P).T, b3[e].reshape(2, P).T], 1) for e in range(E0A)])
    a["b2"] = np.concatenate([g["L0_ffn_b2"], g["L0_ffn_bs2"][None], np.zeros((1, D), np.float32)], 0)
    a["w_qkv"] = g["L1_attn_w_qkv"]
    a["wo1"] = g["L1_attn_w_o"]
    a["log_p"], a["log_a"] = g["L1_attn_log_p"].reshape(-1), g["L1_attn_log_a"].reshape(-1)
    a["b2a"] = g["L1_attn_b2"]
    a["pa_col"] = np.stack([np.tile(a["log_p"], 4), np.tile(a["log_a"], 4)], 1)
    a["b1_col"] = np.tile(g["L1_attn_b1"], 4)[:, None]
    w1 = g["L1_attn_w1"]
    big = _block_diagonal(w1[0:H1], 8)
    a["w1s"] = np.stack([big[:, 0:P], big[:, P:2 * P]], 1)
    a["w1k"] = _block_diagonal(w1[H1:], 4)
    a["w2b"] = _block_diagonal(g["L1_attn_w2"], 4)
    a["wr1"] = g["L1_ffn_Wr"]
    a["w_e1"] = np.stack([np.concatenate([x for m in range(F1 // P) for x in (
        columns(g["L1_ffn_W1"][e], m), g["L1_ffn_W2"][e][m * P:(m + 1) * P])], 1) for e in range(E1)])
    return {k: np.ascontiguousarray(v) for k, v in a.items()}


def kernel(**inputs):
    import concourse.bacc as bacc
    from concourse.bass_utils import run_bass_kernel_spmd

    nc, arrays = _build(bacc, inputs)
    r = run_bass_kernel_spmd(nc, [arrays], core_ids=[0])
    return r.results[0]["out_dram"]


def _build(bacc, inputs, layers=LAYERS):
    nc = bacc.Bacc("TRN2", target_bir_lowering=False, num_devices=1)
    arrays, dram = {}, {}
    for name, x in _arrays(inputs).items():
        arrays[f"in_{name}_dram"] = x
        dram[name] = nc.dram_tensor(f"in_{name}_dram", x.shape, mybir.dt.from_np(x.dtype), kind="ExternalInput").ap()
    dram["gates0"] = nc.dram_tensor("gates0_dram", (E0A, S), F32, kind="Internal").ap()
    dram["gates1"] = nc.dram_tensor("gates1_dram", (E1, S), F32, kind="Internal").ap()
    dram["out"] = nc.dram_tensor("out_dram", (B, S, D), F32, kind="ExternalOutput").ap()
    decoder(nc, dram, layers)
    return nc, arrays
```

```python
import math
from contextlib import ExitStack, contextmanager

import numpy as np
import concourse.bass as bass
from concourse import mybir

F32 = mybir.dt.float32
BF16 = mybir.dt.bfloat16
F32R = mybir.dt.float32r
ALU = mybir.AluOpType
ACT = mybir.ActivationFunctionType
AX = mybir.AxisListType

P = 128
B, S, D = 4, 512, 256
TT = S // P
DC = D // P
NEG = -1e30

H0, HD0 = 16, 16
HS0 = 64
NH, DH = 4, 64
E0, I0 = 8, 256
E0A = 10
H1, HD1 = 16, 64
E1, F1 = 8, 1024
JG = 32

FIRST_SEM = 120

FG_ROW = 32
C0 = 6 * P
C1 = 4 * P
W0, W1 = 2 * C0, 8 * C1
PARTS0 = 2 * 4 * C0 + 2 * DC * S + 2 * 2 * S
PARTS1 = 2 * 8 * C1 + 2 * DC * S + 2 * 4 * S
W0_AT = 9216
W1_AT = 9216
WQKV_AT = 3 * 4096
XN_AT = 14400
TS_AT = WQKV_AT + S * H1


def free(ap, *dims):
    return bass.AP(ap.tensor, ap.offset, [list(ap.ap[0])] + [list(d) for d in dims])


def absolute(dve, out, x):
    return dve.scalar_tensor_tensor(out=out, in0=x, scalar=-1.0, in1=x, op0=ALU.mult, op1=ALU.max)


class Own:

    def __init__(self, sem):
        self.sem, self.n = sem, 0

    def __call__(self, eng, ins):
        self.n += 1
        ins.then_inc(self.sem, 1)
        eng.wait_ge(self.sem, self.n)


class Arena:

    def __init__(self, base, size):
        self.base, self.size, self.at = base, size, 0

    def take(self, *dims):
        n = int(np.prod(dims))
        a = self.base[:, self.at:self.at + n]
        self.at += n
        assert self.at <= self.size, (self.at, self.size)
        if len(dims) == 2:
            return a.rearrange("p (a b) -> p a b", a=dims[0])
        if len(dims) == 3:
            return a.rearrange("p (a b c) -> p a b c", a=dims[0], b=dims[1])
        if len(dims) == 4:
            return a.rearrange("p (a b c d) -> p a b c d", a=dims[0], b=dims[1], c=dims[2])
        return a


class Core:

    def __init__(self, nc, ctx, dram):
        self.nc, self.ctx, self.dram = nc, ctx, dram
        sb = self.sb
        self.ident = sb("ident", [P, P])
        self.ident_bf = sb("ident_bf", [P, P], BF16)
        self.mask_bf = sb("mask_bf", [P, P], BF16)
        self.maskT_bf = sb("maskT_bf", [P, P], BF16)
        self.X = sb("X", [P, TT, D])
        self.XT = sb("XT", [P, DC, S])
        self.CV = sb("CV", [P, TT, NH, DH + 1])
        self.CT = sb("CT", [P, DC, S])
        self.R = sb("R", [P, TT, D])
        self.stats = sb("stats", [P, TT, 6])
        self.mv = sb("mv", [P, TT, 2])
        self.rstd = sb("rstd", [P, TT])
        self.mhalf = sb("mhalf", [P, 16])
        self.halfpi = sb("halfpi", [P, 1])
        self.ones = sb("ones", [NH, S])
        self.zero_bf = sb("zero_bf", [P, S], BF16)
        self.WA = sb("WA", [P, DC, 5 * D])
        self.WOA = sb("WOA", [P, DC, D])
        self.lam = sb("lam", [P, H0])
        self.gate = [sb(f"gate{i}", [P, 6, FG_ROW + NH]) for i in range(2)]
        self.gate_bias = [sb(f"gate_bias{i}", [NH, 2]) for i in range(2)]
        self.norm_w = [sb(f"norm_w{i}", [P, D]) for i in range(2)]
        self.sel = sb("sel", [NH, NH, P])
        self.WR0 = sb("WR0", [P, DC, E0])
        self.rb0 = sb("rb0", [P, E0])
        self.WR1 = sb("WR1", [P, DC, E1])
        self.B2 = sb("B2", [E0A, D])
        self.tri = sb("tri", [P, E0, E0])
        self.rope = sb("rope", [P, TT, 2, HD1])
        self.W1H = sb("W1H", [P, 2, P], F32R)
        self.W1L = sb("W1L", [P, 2, P], F32R)
        self.W2B = sb("W2B", [P, 64])
        self.TB = sb("TB", [P, 640])
        self.KF = sb("KF", [P, S, H1])
        self.WO1 = sb("WO1", [P, 8, D])
        size = 29760
        base = nc.sbuf_base
        self.work = sb("work", [P, size])
        self.size = size
        self.parts = [nc.alloc_sbuf_tensor_at(f"parts{i}", [P, n], F32R, offset=base + 4 * (size - n))
                      for i, n in enumerate((PARTS0, PARTS1))]
        self.turned_scores = nc.alloc_sbuf_tensor_at("turned_scores", [P, 4 * S], F32R, offset=base + 4 * TS_AT)
        self.x_next = self.work[:, XN_AT:XN_AT + TT * D].rearrange("p (t d) -> p t d", t=TT)
        self.stored = ctx.enter_context(nc.semaphore("out_stored", num=FIRST_SEM - 1))
        self.ps = [ctx.enter_context(nc.psum_tensor(f"ps{i}", [P, 512], F32)) for i in range(8)]

    def sb(self, name, shape, dt=F32):
        return self.ctx.enter_context(self.nc.sbuf_tensor(name, shape, dt))

    def sem(self, name):
        s = self.sem_ctx.enter_context(self.nc.semaphore(name, num=FIRST_SEM + len(self.sems)))
        self.sems.append(s)
        return s

    @contextmanager
    def semaphores(self):
        with ExitStack() as self.sem_ctx:
            self.sems = []
            self.own_dve = Own(self.sem("dve_own"))
            self.own_act = Own(self.sem("act_own"))
            self.own_pool = Own(self.sem("pool_own"))
            yield
            self.nc.all_engine_barrier(sems_to_clear=range(FIRST_SEM, FIRST_SEM + len(self.sems)))

    def arena(self):
        return Arena(self.work, self.size)



class Norm:

    def __init__(self, core, name, eps=1e-5):
        self.c, self.eps = core, eps
        self.var_ready = core.sem(f"{name}_var_ready")
        self.rstd_ready = core.sem(f"{name}_rstd_ready")
        self.x_ready = core.sem(f"{name}_x_normed")

    def stats(self, dve, t, y):
        c = self.c
        c.own_dve(dve, dve.tensor_tensor(c.R[:, t, :], y, c.X[:, t, :], ALU.add))
        c.own_dve(dve, dve.bn_stats(c.stats[:, t, :], c.R[:, t, :]))
        dve.bn_aggr(c.mv[:, t, :], c.stats[:, t, :]).then_inc(self.var_ready, 1)

    def pool(self, pool, t):
        c = self.c
        pool.wait_ge(self.var_ready, t + 1)
        c.own_pool(pool, pool.tensor_scalar(c.rstd[:, t:t + 1], c.mv[:, t, 1:2], self.eps, None, ALU.add))
        pool.tensor_tensor(c.rstd[:, t:t + 1], c.rstd[:, t:t + 1], c.mhalf[:, 0:1],
                           ALU.pow).then_inc(self.rstd_ready, 1)

    def all_stats(self, dve):
        c = self.c
        for t in range(TT):
            last = dve.bn_stats(c.stats[:, t, :], c.R[:, t, :])
        c.own_dve(dve, last)
        for t in range(TT):
            dve.bn_aggr(c.mv[:, t, :], c.stats[:, t, :]).then_inc(self.var_ready, 1)

    def all_pool(self, pool):
        c = self.c
        pool.wait_ge(self.var_ready, TT)
        c.own_pool(pool, pool.tensor_scalar(c.rstd[:, :], c.mv[:, :, 1], self.eps, None, ALU.add))
        pool.tensor_tensor(c.rstd[:, :], c.rstd[:, :], c.mhalf[:, 0:TT], ALU.pow).then_inc(self.rstd_ready, TT)

    def apply(self, dve, t):
        c = self.c
        dve.wait_ge(self.rstd_ready, t + 1)
        dve.tensor_scalar(c.X[:, t, :], c.R[:, t, :], c.mv[:, t, 0:1], c.rstd[:, t:t + 1],
                          ALU.subtract, ALU.mult).then_inc(self.x_ready, 1)


class Turn:

    def __init__(self, core, name, src, dst, banks=(0, 1)):
        self.c, self.src, self.dst, self.banks = core, src, dst, banks
        self.turned = core.sem(f"{name}_x_turned")
        self.ready = core.sem(f"{name}_feature_major")

    def pe(self, pe):
        c = self.c
        for k in range(DC):
            for t in range(TT):
                last = pe.transpose(c.ps[self.banks[k]][:, t * P:(t + 1) * P], self.src(t, k), c.ident[:, :])
            last.then_inc(self.turned, 1)

    def dve(self, dve):
        dve.wait_ge(self.turned, 1)
        dve.tensor_copy(self.dst[:, 0, :], self.c.ps[self.banks[0]][:, :]).then_inc(self.ready, 1)

    def act(self, act):
        act.wait_ge(self.turned, 2)
        act.copy(self.dst[:, 1, :], self.c.ps[self.banks[1]][:, :]).then_inc(self.ready, 1)


def turn_x(core, name):
    return Turn(core, name, lambda t, k: core.X[:, t, k * P:(k + 1) * P], core.XT)



def setup(core):
    nc, d = core.nc, core.dram
    a = core.arena()
    par = a.take(3, H1)
    sp = a.take(6, H1)
    col = a.take(4)
    spc = a.take(8)
    dist_c = a.take(640)
    dist_r = a.take(S)
    maskf, maskTf = a.take(P), a.take(P)
    w1k = a.take(P)
    w1raw = a.take(2, P)
    lamr = a.take(H0)
    lam1 = a.take(H0)
    tables_in = core.sem("table_inputs_loaded")
    x_in = core.sem("first_x_loaded")
    loaded = core.sem("constants_loaded")
    p_ready = core.sem("softplus_ready")
    kerple_ready = core.sem("kerple_ready")
    kcol_ready = core.sem("kerple_column_ready")
    tb_ready = core.sem("table_product_ready")
    lam_t = core.sem("lambda_tanh")
    table_loads = [
        (par[:, 0, :], d["log_p"].partition_broadcast(P)), (par[:, 1, :], d["log_a"].partition_broadcast(P)),
        (par[:, 2, :], d["b2a"].partition_broadcast(P)), (col[0:64, 0:2], d["pa_col"]), (col[:, 2:3], d["b1_col"]),
        (dist_c[0:64, :], d["dist_c"]), (dist_r, d["dist_r"]), (maskf, d["mask"]), (w1k[0:64, :], d["w1k"]),
    ]
    loads = [
        (core.ident[:, :], d["ident"]), (maskTf, d["maskT"]), (core.WA[:, :, :], d["wa"].rearrange("(c p) n -> p c n", p=P)),
        (core.WOA[:, :, :], d["woa"].rearrange("(c p) n -> p c n", p=P)), (lamr, d["lambda"].partition_broadcast(P)),
        (core.sel[:, :, :], d["sel"]), (core.tri[:, :, :], d["tri"]), (core.rope[:, :, :, :], d["rope"]),
        (core.WR0[:, :, :], d["wr0"].rearrange("(c p) n -> p c n", p=P)), (core.rb0[:, :], d["rb0"].partition_broadcast(P)),
        (core.WR1[:, :, :], d["wr1"].rearrange("(c p) n -> p c n", p=P)), (core.B2[:, :], d["b2"]),
        (w1raw, d["w1s"]), (core.W2B[:, :], d["w2b"]),
        (core.WO1[:, :, :], d["wo1"].rearrange("(c p) n -> p c n", p=P)),
    ]
    for i in range(2):
        loads += [(core.gate[i][:, :, :], d[f"gate{i}"].rearrange("(c p) n -> p c n", p=P)),
                  (core.gate_bias[i][:, :], d[f"gate_bias{i}"]),
                  (core.norm_w[i][:, :], d[f"norm_w{i}"].partition_broadcast(P))]
    n_tables, n_loads = 16 * len(table_loads), 16 * len(loads)

    with nc.Block() as block:
        @block.sync
        def _(sp_):
            for dst, src in table_loads:
                sp_.dma_start(dst, src).then_inc(tables_in, 16)
            for dst, src in loads:
                sp_.dma_start(dst, src).then_inc(loaded, 16)
            sp_.dma_start(core.x_next, d["x"][0].rearrange("(t p) d -> p t d", p=P)).then_inc(x_in, 16)
            sp_.wait_ge(loaded, n_loads)
            sp_.wait_ge(x_in, 16)

        @block.scalar
        def _(act):
            own = core.own_act
            act.wait_ge(p_ready, 2)
            own(act, act.activation(sp[:, 2:4, :], sp[:, 0:2, :], ACT.Exp, scale=-1.0))
            own(act, act.activation(spc[0:64, 2:4], spc[0:64, 0:2], ACT.Exp, scale=-1.0))
            own(act, act.activation(sp[:, 4:6, :], sp[:, 2:4, :], ACT.Ln, bias=1.0))
            act.activation(spc[0:64, 4:6], spc[0:64, 2:4], ACT.Ln, bias=1.0).then_inc(kcol_ready, 1)
            act.wait_ge(p_ready, 3)
            act.wait_ge(tables_in, n_tables)
            act.activation(dist_c[0:64, :], dist_c[0:64, :], ACT.Ln, bias=1.0,
                           scale=spc[0:64, 7:8]).then_inc(kerple_ready, 1)
            for h in range(H1):
                act.activation(core.KF[:, :, h], dist_r, ACT.Ln, bias=1.0,
                               scale=sp[:, 1, h:h + 1]).then_inc(kerple_ready, 1)
            act.wait_ge(loaded, n_loads)
            act.activation(lam1, lamr, ACT.Tanh).then_inc(lam_t, 1)

        @block.vector
        def _(dve):
            own = core.own_dve
            dve.sem_inc(core.stored, 16 * TT)
            dve.memset(core.mhalf[:, :], -0.5)
            dve.memset(core.ones[:, :], 1.0)
            dve.memset(core.zero_bf[:, :], 0.0)
            dve.memset(core.halfpi[:, :], math.pi / 2)
            dve.wait_ge(tables_in, n_tables)
            dve.tensor_copy(core.mask_bf[:, :], maskf)
            absolute(dve, sp[:, 0:2, :], par[:, 0:2, :]).then_inc(p_ready, 1)
            absolute(dve, spc[0:64, 0:2], col[0:64, 0:2]).then_inc(p_ready, 1)
            dve.wait_ge(kcol_ready, 1)
            own(dve, dve.scalar_tensor_tensor(out=sp[:, 0:2, :], in0=par[:, 0:2, :], scalar=0.0, in1=sp[:, 4:6, :],
                                              op0=ALU.max, op1=ALU.add))
            dve.scalar_tensor_tensor(out=spc[0:64, 6:8], in0=col[0:64, 0:2], scalar=0.0, in1=spc[0:64, 4:6],
                                     op0=ALU.max, op1=ALU.add).then_inc(p_ready, 1)
            dve.wait_ge(p_ready, 3)
            dve.tensor_scalar(spc[0:64, 0:1], spc[0:64, 6:7], -1.0, None, ALU.mult)
            own(dve, dve.tensor_scalar(sp[:, 2, :], sp[:, 0, :], -1.0, None, ALU.mult))
            dve.wait_ge(kerple_ready, 1)
            dve.tensor_scalar(dist_c[0:64, :], dist_c[0:64, :], spc[0:64, 0:1], None, ALU.mult).then_inc(kcol_ready, 1)
            for h in range(H1):
                if h == 3 * H1 // 4:
                    dve.wait_ge(tb_ready, 1)
                    dve.tensor_scalar(core.TB[:, 0:512], core.ps[0][:, :], col[:, 2:3], None, ALU.add)
                    dve.tensor_scalar(core.TB[:, 512:640], core.ps[1][:, 0:128], col[:, 2:3], None, ALU.add)
                    dve.wait_ge(loaded, n_loads)
                    own(dve, dve.tensor_copy(core.W1H[:, :, :], w1raw))
                    rest(dve, core.W1L[:, :, :], w1raw, core.W1H[:, :, :])
                    dve.tensor_copy(core.ident_bf[:, :], core.ident[:, :])
                    dve.tensor_copy(core.maskT_bf[:, :], maskTf)
                    dve.tensor_scalar(core.norm_w[1][:, :], core.norm_w[1][:, :], 1.0, None, ALU.add)
                dve.wait_ge(kerple_ready, h + 2)
                last = dve.tensor_scalar(core.KF[:, :, h], core.KF[:, :, h], sp[:, 2, h:h + 1], par[:, 2, h:h + 1],
                                         ALU.mult, ALU.add)
            own(dve, last)
            dve.tensor_tensor(core.KF[:, S - P:S, :], core.KF[:, S - P:S, :], free(maskf, (1, P), (0, H1)), ALU.add)
            dve.wait_ge(lam_t, 1)
            dve.tensor_scalar(core.lam[:, :], lam1, 0.5 / math.sqrt(HD0), None, ALU.mult)

        @block.tensor
        def _(pe):
            pe.wait_ge(kcol_ready, 2)
            pe.wait_ge(tables_in, n_tables)
            pe.matmul(core.ps[0][:, :], w1k[0:64, :], dist_c[0:64, 0:512], start=True, stop=True)
            pe.matmul(core.ps[1][:, 0:128], w1k[0:64, :], dist_c[0:64, 512:640], start=True,
                      stop=True).then_inc(tb_ready, 1)



def phase_attention(core, b):
    nc, ps = core.nc, core.ps
    a = core.arena()
    QT, KT = a.take(8, S), a.take(8, S)
    RAW, AMP = a.take(TT, 2 * D), a.take(TT, 2 * D)
    SN, CS = a.take(TT, 2 * D), a.take(TT, 2 * D)
    V = a.take(TT, D)
    Q3 = a.take(2, 2, H0, HS0)
    SQ = a.take(TT, 2 * D)
    QZ = a.take(2, 2, S)
    SS = a.take(TT, 2 * H0)
    RN = a.take(TT, 2 * H0)
    a2 = Arena(core.work, core.size)
    a2.take(16 * S)
    PR, PTS = a2.take(3, S), a2.take(3, S)
    NM, DEN, RD = a2.take(64), a2.take(64), a2.take(64)
    O, OT = a2.take(TT, D), a2.take(DC, S)
    assert a2.at <= 16 * S + 4 * TT * 2 * D

    x_copied = core.sem("a_x_copied")
    ctx_in = core.sem("a_context_loaded")
    turn = Turn(core, "a", lambda t, k: core.x_next[:, t, k * P:(k + 1) * P], core.XT)
    turn_c = Turn(core, "a_context", lambda t, k: core.R[:, t, k * P:(k + 1) * P], core.CT, banks=(6, 7))
    qz = core.sem("a_padded_q_ready")
    proj = core.sem("a_projected")
    raw = core.sem("a_raw_ready")
    tanh = core.sem("a_tanh_ready")
    absph = core.sem("a_abs_phase_ready")
    absraw = core.sem("a_abs_raw_ready")
    amp_ready, scaled = core.sem("a_amplitudes_ready"), core.sem("a_amplitudes_scaled")
    sin = core.sem("a_sin_cos_ready")
    lnp = core.sem("a_log1p_ready")
    ssq = core.sem("a_square_sums_ready")
    rn = core.sem("a_amp_norm_ready")
    zeroed = core.sem("a_zeroed")
    q3raw = core.sem("a_q3_raw_ready")
    q3 = core.sem("a_q3_ready")
    tp = core.sem("a_turned")
    ev = (core.sem("a_qk_copied_even"), core.sem("a_qk_copied_odd"))
    sc = core.sem("a_scores_ready")
    mx = core.sem("a_max_ready")
    ex = core.sem("a_probs_ready")
    tr = core.sem("a_probs_turned")
    pt = core.sem("a_probsT_ready")
    pv = core.sem("a_pv_done")
    on = core.sem("a_out_ready")
    ot = core.sem("a_out_turned")
    otr = core.sem("a_outT_ready")
    y = core.sem("a_y_ready")
    norm = Norm(core, "a")
    steps = [(h, it) for h in range(H0) for it in range(TT)]
    N = len(steps)
    PROJ = [2, 5]
    SB, PB = (0, 1, 2), (3, 4, 7)
    OB = lambda it: ps[5 + it // 2][:, (it % 2) * D:(it % 2 + 1) * D]
    YB = lambda t: ps[(2, 3, 4, 7)[t]][:, 0:D]

    with nc.Block() as block:
        @block.sync
        def _(sp):
            sp.dma_start(core.R[:, :, :], core.dram["ctx"][b].rearrange("(t p) d -> p t d", p=P)).then_inc(ctx_in, 16)
            for t in range(TT):
                sp.dma_start(core.CV[:, t, :, 0:DH], core.dram["ctx"][b, t * P:(t + 1) * P, :].rearrange(
                    "p (h d) -> p h d", h=NH)).then_inc(ctx_in, 16)
            sp.wait_ge(ctx_in, 16 * (TT + 1))

        @block.gpsimd
        def _(pool):
            pool.memset(core.CV[:, :, :, DH:DH + 1], 1.0)
            pool.memset(QZ[:, :, :, :], 0.0)
            pool.memset(Q3[:, :, :, :, 48:64], 0.0).then_inc(zeroed, 1)
            for t in range(TT):
                pool.wait_ge(raw, t + 1)
                if t >= 2:
                    pool.wait_ge(tp, 4 * (t - 1))
                src = RAW[:, t, :].rearrange("p (s h d) -> p s h d", s=2, h=H0)
                pool.tensor_copy(Q3[:, t % 2, 0, :, 0:16], src[:, 0])
                pool.tensor_scalar(Q3[:, t % 2, 1, :, 0:16], src[:, 1], 1.0 / math.sqrt(HD0), None,
                                   ALU.mult).then_inc(q3raw, 1)
            pool.wait_ge(q3raw, TT)
            for pair in range(H0 // 2):
                if pair == 0:
                    for t in range(TT):
                        pool.wait_ge(ev[0], 2 * t + 1)
                        for k in range(2):
                            r = slice(64 * k, 64 * k + 64)
                            pool.tensor_copy(QZ[r, 0, k, t * P:(t + 1) * P], QT[r, 0, t * P:(t + 1) * P]).then_inc(qz, 1)
                    pool.wait_ge(ev[0], 8)
                    pool.wait_ge(ev[1], 8)
                    continue
                if pair >= 2:
                    pool.wait_ge(sc, 8 * (pair - 1))
                for k in range(2):
                    r = slice(64 * k, 64 * k + 64)
                    pool.tensor_copy(QZ[r, pair % 2, k, :], QT[r, pair, :]).then_inc(qz, 1)
            for t in range(TT):
                norm.pool(pool, t)

        @block.tensor
        def _(pe):
            turn.pe(pe)
            pe.wait_ge(turn.ready, 2)
            for t in range(TT):
                if t == 1:
                    pe.wait_ge(ctx_in, 16 * (TT + 1))
                    turn_c.pe(pe)
                    pe.wait_ge(turn_c.ready, 2)
                if t >= 2:
                    pe.wait_ge(raw, t - 1)
                    pe.wait_ge(tanh, t - 1)
                for i, w in enumerate((512, 512, 256)):
                    for k in range(DC):
                        last = pe.matmul(ps[PROJ[t % 2] + i][:, 0:w], core.XT[:, k, t * P:(t + 1) * P],
                                         core.WA[:, k, 512 * i:512 * i + w], start=(k == 0), stop=(k == DC - 1))
                last.then_inc(proj, 1)
            for t in range(TT):
                pe.wait_ge(q3, t + 1)
                for i in range(4):
                    n = 4 * t + i
                    if n >= 4:
                        pe.wait_ge(ev[n % 2], (n - 4) // 2 + 1)
                    for j in range(4):
                        pair = 4 * (i % 2) + j
                        last = pe.transpose(ps[n % 4][:, j * P:(j + 1) * P],
                                            Q3[:, t % 2, i // 2, 2 * pair:2 * pair + 2, :], core.ident[:, :])
                    last.then_inc(tp, 1)

            def scores(n):
                h, it = steps[n]
                if n >= 3:
                    pe.wait_ge(ex, n - 2)
                w = (it + 1) * P
                if h < 2:
                    pe.wait_ge(qz, 2 * it + h + 1)
                elif it == 0:
                    pe.wait_ge(qz, 2 * TT + h - 1)
                pe.matmul(ps[SB[n % 3]][:, 0:w], QZ[:, h // 2 % 2, h % 2, it * P:w], KT[:, h // 2, 0:w],
                          start=True, stop=False)
                pe.matmul(ps[SB[n % 3]][:, w - P:w], core.ident_bf[:, :], core.mask_bf[:, :],
                          start=False, stop=True).then_inc(sc, 1)

            def turn_probs(n):
                _, it = steps[n]
                pe.wait_ge(ex, n + 1)
                if n >= 3:
                    pe.wait_ge(pt, n - 2)
                for j in range(it + 1):
                    last = pe.transpose(ps[PB[n % 3]][:, j * P:(j + 1) * P], PR[:, n % 3, j * P:(j + 1) * P],
                                        core.ident[:, :])
                last.then_inc(tr, 1)

            def values(n):
                h, it = steps[n]
                pe.wait_ge(pt, n + 1)
                for j in range(it + 1):
                    last = pe.matmul(OB(it)[:, h * HD0:(h + 1) * HD0], PTS[:, n % 3, j * P:(j + 1) * P],
                                     V[:, j, h * HD0:(h + 1) * HD0], start=(j == 0), stop=(j == it))
                last.then_inc(pv, 1)

            for e in ev:
                pe.wait_ge(e, 2 * TT)
            scores(0)
            scores(1)
            for n in range(N + 2):
                if n + 2 < N:
                    scores(n + 2)
                if n < N:
                    turn_probs(n)
                if n >= 2:
                    values(n - 2)
            pe.wait_ge(on, TT)
            for k in range(DC):
                for t in range(TT):
                    last = pe.transpose(ps[k][:, t * P:(t + 1) * P], O[:, t, k * P:(k + 1) * P], core.ident[:, :])
                last.then_inc(ot, 1)
            pe.wait_ge(otr, 2)
            for t in range(TT):
                for k in range(DC):
                    last = pe.matmul(YB(t), OT[:, k, t * P:(t + 1) * P], core.WOA[:, k, :],
                                     start=(k == 0), stop=(k == DC - 1))
                last.then_inc(y, 1)

        @block.scalar
        def _(act):
            turn.act(act)
            act.wait_ge(core.stored, 16 * TT * b + 16 * TT)
            act.copy(core.X[:, :, :], core.x_next).then_inc(x_copied, 1)
            for t in range(TT):
                if t == 1:
                    turn_c.act(act)
                act.wait_ge(proj, t + 1)
                act.activation(SN[:, t, :], ps[PROJ[t % 2] + 1][:, :], ACT.Tanh).then_inc(tanh, 1)
                act.wait_ge(absraw, t + 1)
                last = act.activation(AMP[:, t, :], AMP[:, t, :], ACT.Exp, scale=-1.0)
            core.own_act(act, last)
            for t in range(TT):
                act.activation(AMP[:, t, :], AMP[:, t, :], ACT.Ln, bias=1.0).then_inc(lnp, 1)
            act.wait_ge(absph, TT)
            act.activation(SN, SN, ACT.Sin, scale=math.pi)
            act.activation(CS, CS, ACT.Sin, scale=-math.pi, bias=core.halfpi[:, :]).then_inc(sin, 1)
            act.wait_ge(ssq, 1)
            act.activation(SS, SS, ACT.Sqrt).then_inc(rn, 1)
            for n in range(4 * TT):
                act.wait_ge(tp, n + 1)
                t, i = n // 4, n % 4
                dst = (QT if i < 2 else KT)[:, 4 * (i % 2):4 * (i % 2) + 4, t * P:(t + 1) * P]
                act.copy(dst, ps[n % 4][:, :].rearrange("p (a b) -> p a b", a=4)).then_inc(ev[n % 2], 1)
            for n in range(N):
                w = (steps[n][1] + 1) * P
                act.wait_ge(mx, n + 1)
                if n >= 3:
                    act.wait_ge(tr, n - 2)
                act.activation(PR[:, n % 3, 0:w], ps[SB[n % 3]][:, 0:w], ACT.Exp, bias=NM[:, n:n + 1],
                               accum_out=DEN[:, n:n + 1]).then_inc(ex, 1)
            act.wait_ge(ot, 2)
            act.copy(OT[:, 1, :], ps[1][:, :]).then_inc(otr, 1)

        @block.vector
        def _(dve):
            own = core.own_dve
            turn.dve(dve)
            for t in range(TT):
                if t == 1:
                    turn_c.dve(dve)
                dve.wait_ge(proj, t + 1)
                dve.tensor_copy(V[:, t, :], ps[PROJ[t % 2] + 2][:, 0:D])
                dve.tensor_copy(RAW[:, t, :], ps[PROJ[t % 2]][:, :]).then_inc(raw, 1)
                dve.wait_ge(raw, t + 1)
                absolute(dve, AMP[:, t, :], RAW[:, t, :]).then_inc(absraw, 1)
                dve.wait_ge(tanh, t + 1)
                if t == 0:
                    dve.wait_ge(x_copied, 1)
                absolute(dve, CS[:, t, :], SN[:, t, :]).then_inc(absph, 1)
            for t in range(TT + 1):
                if t < TT:
                    dve.wait_ge(lnp, t + 1)
                    dve.scalar_tensor_tensor(out=AMP[:, t, :], in0=RAW[:, t, :], scalar=0.0, in1=AMP[:, t, :],
                                             op0=ALU.max, op1=ALU.add).then_inc(amp_ready, 1)
                if t >= 1:
                    dve.wait_ge(amp_ready, t)
                    last = dve.tensor_tensor(SQ[:, t - 1, :], AMP[:, t - 1, :], AMP[:, t - 1, :], ALU.mult)
            own(dve, last)
            own(dve, dve.tensor_reduce(SS, SQ.rearrange("p t (h d) -> p t h d", d=HD0), AX.X, ALU.add))
            dve.tensor_scalar(SS, SS, 1.0 / HD0, 1e-6, ALU.mult, ALU.add).then_inc(ssq, 1)
            dve.wait_ge(zeroed, 1)
            dve.wait_ge(rn, 1)
            own(dve, dve.reciprocal(RN, SS))
            own(dve, dve.tensor_tensor(RN[:, :, H0:], RN[:, :, H0:], free(core.lam[:, :], (0, TT), (1, H0)), ALU.mult))
            def scale_amp(t):
                amp = AMP[:, t, :].rearrange("p (h d) -> p h d", d=HD0)
                dve.tensor_tensor(amp, amp, free(RN[:, t, :], (1, 2 * H0), (0, HD0)), ALU.mult).then_inc(scaled, 1)

            scale_amp(0)
            dve.wait_ge(sin, 1)
            for t in range(TT):
                if t + 1 < TT:
                    scale_amp(t + 1)
                dve.wait_ge(scaled, t + 1)
                if t >= 2:
                    dve.wait_ge(tp, 4 * (t - 1))
                dve.wait_ge(q3raw, t + 1)
                amp = AMP[:, t, :].rearrange("p (h d) -> p h d", d=HD0)
                q = Q3[:, t % 2].rearrange("p s h d -> p (s h) d")
                dve.tensor_tensor(q[:, :, 16:32], amp, CS[:, t, :].rearrange("p (h d) -> p h d", d=HD0), ALU.mult)
                dve.tensor_tensor(q[:, :, 32:48], amp, SN[:, t, :].rearrange("p (h d) -> p h d", d=HD0),
                                  ALU.mult).then_inc(q3, 1)

            for n in range(N + 1):
                if n < N:
                    w = (steps[n][1] + 1) * P
                    dve.wait_ge(sc, n + 1)
                    dve.tensor_reduce(NM[:, n:n + 1], ps[SB[n % 3]][:, 0:w], AX.X, ALU.max,
                                      negate=True).then_inc(mx, 1)
                if n >= 1:
                    m = n - 1
                    w = (steps[m][1] + 1) * P
                    dve.wait_ge(tr, m + 1)
                    if m >= 3:
                        dve.wait_ge(pv, m - 2)
                    dve.tensor_copy(PTS[:, m % 3, 0:w], ps[PB[m % 3]][:, 0:w]).then_inc(pt, 1)
            dve.wait_ge(ex, N)
            own(dve, dve.reciprocal(RD, DEN))
            dve.wait_ge(pv, N)
            for it in range(TT):
                dve.tensor_tensor(O[:, it, :].rearrange("p (h d) -> p h d", h=H0),
                                  OB(it).rearrange("p (h d) -> p h d", h=H0),
                                  free(RD[:, it:it + 1], (TT, H0), (0, HD0)), ALU.mult).then_inc(on, 1)
            dve.wait_ge(ot, 1)
            dve.tensor_copy(OT[:, 0, :], ps[0][:, :]).then_inc(otr, 1)
            for t in range(TT):
                dve.wait_ge(y, t + 1)
                norm.stats(dve, t, YB(t))
            for t in range(TT):
                norm.apply(dve, t)



def mlstm(core, which, name, head_eps, prefetch):
    nc, ps = core.nc, core.ps
    a = core.arena()
    FG, AF, IG, NMR = a.take(S), a.take(S), a.take(S), a.take(S)
    FN, CUM, NA, NL = FG, AF, IG, FG
    AT, EN = a.take(16), a.take(16)
    DD = a.take(4, S)
    CC = a.take(2, 10 * P)
    XZ = a.take(NH, S)
    DN, RD = a.take(16), a.take(16)
    HH = Arena(core.work, core.size).take(TT, NH, DH)
    ST, MV, RS = a.take(16, 6), a.take(16, 2), a.take(16)
    assert a.at <= W0_AT, a.at
    offs = [0, 4 * P, 7 * P, 9 * P]

    turn = turn_x(core, name)
    xz = core.sem(name + "_padded_q_ready")
    gates = core.sem(name + "_gates_ready")
    absf = core.sem(name + "_abs_f_ready")
    fn = core.sem(name + "_min_f_ready")
    lnf = core.sem(name + "_log1p_ready")
    rows = core.sem(name + "_gate_rows_ready")
    cols = core.sem(name + "_gate_columns_turned")
    at = core.sem(name + "_columns_ready")
    en = core.sem(name + "_exp_neg_max_ready")
    nm = core.sem(name + "_neg_max_spread")
    qk = core.sem(name + "_qk_ready")
    dd = core.sem(name + "_decay_ready")
    cc = core.sem(name + "_c_ready")
    pv = core.sem(name + "_values_done")
    taken = core.sem(name + "_values_taken")
    centred = core.sem(name + "_head_centred")
    hv = core.sem(name + "_head_var_ready")
    hr = core.sem(name + "_head_rstd_ready")
    norm = Norm(core, name)

    with nc.Block() as block:
        @block.sync
        def _(sp):
            prefetch(sp)

        @block.gpsimd
        def _(pool):
            core.own_pool(pool, pool.memset(XZ, 0.0))
            pool.wait_ge(turn.ready, 2)
            for h in range(NH):
                r = slice(64 * (h % 2), 64 * (h % 2) + 64)
                pool.tensor_copy(XZ[r, h, :], core.XT[r, h // 2, :]).then_inc(xz, 1)
            for h in range(NH):
                n = slice(TT * h, TT * (h + 1))
                pool.wait_ge(hv, h + 1)
                pool.wait_ge(*((xz, NH) if h == 0 else (hr, h)))
                core.own_pool(pool, pool.tensor_scalar(RS[:, n], MV[:, n, 1], head_eps, None, ALU.add))
                pool.tensor_tensor(RS[:, n], RS[:, n], core.mhalf[:, 0:TT], ALU.pow).then_inc(hr, 1)
            pool.wait_ge(hr, NH)
            norm.all_pool(pool)

        @block.tensor
        def _(pe):
            turn.pe(pe)
            pe.wait_ge(turn.ready, 2)
            for c in range(6):
                rhs = core.XT[:, c, :] if c < 2 else core.CT[:, c % 2, :]
                last = pe.matmul(ps[4][0:FG_ROW + NH, :], core.gate[which][:, c, :], rhs, start=(c == 0), stop=(c == 5))
            last.then_inc(gates, 1)
            pe.wait_ge(rows, 1)

            def columns(bank, src):
                for t in range(TT):
                    last = pe.transpose(bank[:, 4 * t:4 * t + 4], src[0:NH, t * P:(t + 1) * P],
                                        core.ident[0:NH, 0:NH])
                last.then_inc(cols, 1)

            columns(ps[6], NA)

            def spread(h):
                if h >= 1:
                    pe.wait_ge(dd, 4 * h)
                pe.matmul(ps[4][:, :], core.sel[:, h, :], NMR[0:NH, :], start=True, stop=True)
                pe.matmul(ps[5][:, :], core.sel[:, h, :], NMR[0:NH, :], start=True, stop=False)
                pe.matmul(ps[5][:, :], core.ident_bf[:, :], free(core.maskT_bf[:, :], (0, TT), (1, P)),
                          start=False, stop=True).then_inc(nm, 1)

            def scores(h):
                pe.wait_ge(xz, h + 1)
                for j in range(TT):
                    m = 4 * h + j
                    if m >= 2:
                        pe.wait_ge(cc, m - 1)
                    pe.matmul(ps[6 + m % 2][:, j * P:S], core.CT[:, h // 2, j * P:(j + 1) * P],
                              XZ[:, h, j * P:S], start=True, stop=True).then_inc(qk, 1)

            def values(h):
                pe.wait_ge(cc, 4 * (h + 1))
                if h >= 1:
                    pe.wait_ge(taken, h)
                for it in range(TT):
                    for j in range(it + 1):
                        o = offs[j] + (it - j) * P
                        last = pe.matmul(ps[it][:, h * (DH + 1):(h + 1) * (DH + 1)], CC[:, h % 2, o:o + P],
                                         core.CV[:, j, h, :], start=(j == 0), stop=(j == it))
                last.then_inc(pv, 1)

            for h in range(NH):
                spread(h)
                if h == 0:
                    pe.wait_ge(rows, 2)
                    columns(ps[7], NL)
                    pe.wait_ge(at, 1)
                    pe.wait_ge(en, 1)
                scores(h)
                if h >= 1:
                    values(h - 1)
            values(NH - 1)

        @block.scalar
        def _(act):
            turn.act(act)
            act.wait_ge(absf, 1)
            core.own_act(act, act.activation(AF[0:NH, :], AF[0:NH, :], ACT.Exp, scale=-1.0))
            act.activation(AF[0:NH, :], AF[0:NH, :], ACT.Ln, bias=1.0).then_inc(lnf, 1)
            act.wait_ge(cols, 2)
            act.activation(EN, ps[7][:, 0:16], ACT.Exp).then_inc(en, 1)
            act.wait_ge(at, 1)
            for h in range(NH):
                act.wait_ge(nm, h + 1)
                for j in range(TT):
                    m = 4 * h + j
                    if m >= 4:
                        act.wait_ge(cc, m - 3)
                    bias = AT[:, 4 * j + h:4 * j + h + 1]
                    last = act.activation(DD[:, m % 4, j * P:(j + 1) * P], ps[5][:, j * P:(j + 1) * P], ACT.Exp, bias=bias)
                    if j < TT - 1:
                        last = act.activation(DD[:, m % 4, (j + 1) * P:S], ps[4][:, (j + 1) * P:S], ACT.Exp, bias=bias)
                    last.then_inc(dd, 1)

        @block.vector
        def _(dve):
            own = core.own_dve
            g = slice(0, NH)
            turn.dve(dve)
            dve.wait_ge(gates, 1)
            own(dve, dve.tensor_scalar(FG[g, :], ps[4][FG_ROW:FG_ROW + NH, :], core.gate_bias[which][:, 1:2], None, ALU.add))
            absolute(dve, AF[g, :], FG[g, :]).then_inc(absf, 1)
            dve.tensor_scalar(IG[g, :], ps[4][g, :], core.gate_bias[which][:, 0:1], None, ALU.add)
            dve.wait_ge(absf, 1)
            dve.tensor_scalar(FN[g, :], FG[g, :], 0.0, None, ALU.min).then_inc(fn, 1)
            dve.wait_ge(lnf, 1)
            dve.wait_ge(fn, 1)
            own(dve, dve.tensor_tensor_scan(CUM[g, :], FN[g, :], AF[g, :], 0.0, ALU.add, ALU.subtract))
            own(dve, dve.tensor_tensor(NA[g, :], CUM[g, :], IG[g, :], ALU.subtract))
            dve.tensor_tensor_scan(NMR[g, :], NA[g, :], NA[g, :], 3e38, ALU.min, ALU.min).then_inc(rows, 1)
            dve.wait_ge(rows, 1)
            dve.tensor_tensor(NL[g, :], NMR[g, :], CUM[g, :], ALU.subtract).then_inc(rows, 1)
            dve.wait_ge(cols, 1)
            dve.tensor_scalar(AT, ps[6][:, 0:16], -1.0, None, ALU.mult).then_inc(at, 1)

            def weigh_scores(h):
                for j in range(TT):
                    m = 4 * h + j
                    dve.wait_ge(qk, m + 1)
                    dve.wait_ge(dd, m + 1)
                    if j == 0 and h >= 2:
                        dve.wait_ge(pv, h - 1)
                    dve.scalar_tensor_tensor(out=CC[:, h % 2, offs[j]:offs[j] + S - j * P], in0=ps[6 + m % 2][:, j * P:S],
                                             scalar=1.0 / math.sqrt(DH), in1=DD[:, m % 4, j * P:S],
                                             op0=ALU.mult, op1=ALU.mult).then_inc(cc, 1)

            def take_values(h):
                dve.wait_ge(pv, h + 1)
                if h == 0:
                    dve.wait_ge(en, 1)
                    dve.tensor_scalar(EN, EN, 1e-6, None, ALU.add)
                n, o = slice(TT * h, TT * (h + 1)), h * (DH + 1)
                for t in range(TT):
                    last = dve.tensor_copy(DN[:, TT * h + t:TT * h + t + 1], ps[t][:, o + DH:o + DH + 1])
                own(dve, last)
                own(dve, absolute(dve, DN[:, n], DN[:, n]))
                own(dve, dve.scalar_tensor_tensor(out=DN[:, n], in0=DN[:, n], scalar=1e-6,
                                                  in1=free(EN[:, h:h + 1], (NH, TT)), op0=ALU.add, op1=ALU.max))
                own(dve, dve.reciprocal(RD[:, n], DN[:, n]))
                for t in range(TT):
                    last = dve.tensor_scalar(HH[:, t, h, :], ps[t][:, o:o + DH], RD[:, TT * h + t:TT * h + t + 1], None,
                                             ALU.mult)
                last.then_inc(taken, 1)

            def head_stats(h):
                dve.wait_ge(taken, h + 1)
                for t in range(TT):
                    last = dve.bn_stats(ST[:, TT * h + t, :], HH[:, t, h, :])
                own(dve, last)
                for t in range(TT):
                    last = dve.bn_aggr(MV[:, TT * h + t, :], ST[:, TT * h + t, :])
                last.then_inc(hv, 1)
                dve.wait_ge(hv, h + 1)
                for t in range(TT):
                    last = dve.scalar_tensor_tensor(out=HH[:, t, h, :], in0=HH[:, t, h, :],
                                                    scalar=MV[:, TT * h + t, 0:1],
                                                    in1=core.norm_w[which][:, h * DH:(h + 1) * DH],
                                                    op0=ALU.subtract, op1=ALU.mult)
                last.then_inc(centred, 1)

            def add_head(h):
                dve.wait_ge(centred, h + 1)
                dve.wait_ge(hr, h + 1)
                for t in range(TT):
                    last = dve.scalar_tensor_tensor(out=core.R[:, t, h * DH:(h + 1) * DH], in0=HH[:, t, h, :],
                                                    scalar=RS[:, TT * h + t:TT * h + t + 1],
                                                    in1=core.X[:, t, h * DH:(h + 1) * DH], op0=ALU.mult, op1=ALU.add)
                return last

            for h in range(NH):
                weigh_scores(h)
                if h >= 2:
                    head_stats(h - 2)
                if h >= 1:
                    take_values(h - 1)
            for h in range(NH - 2):
                add_head(h)
            head_stats(NH - 2)
            take_values(NH - 1)
            add_head(NH - 2)
            head_stats(NH - 1)
            own(dve, add_head(NH - 1))
            norm.all_stats(dve)
            for t in range(TT):
                norm.apply(dve, t)



class Router:

    def __init__(self, core, a, name, wr, bias, extra, renormalise, gates_dram, x_in):
        self.x_in = x_in
        self.c, self.wr, self.bias, self.extra, self.renorm, self.dram = core, wr, bias, extra, renormalise, gates_dram
        self.n = 8 + extra
        self.L, self.NMX, self.SM = a.take(TT, 8), a.take(TT), a.take(TT)
        self.CMP, self.EQ = a.take(TT, 8, 8), a.take(TT, 8, 8)
        self.RK, self.G, self.GT = a.take(TT, 8), a.take(TT, self.n), a.take(S)
        s = lambda x: core.sem(f"{name}_{x}")
        self.logits, self.shifted, self.exped = s("logits_ready"), s("logits_shifted"), s("exp_logits_ready")
        self.spread = s("first_gates_spread")
        self.gated, self.turned, self.gt, self.stored = s("gates_ready"), s("gates_turned"), s("gatesT_ready"), s("gates_stored")

    def pe(self, pe):
        c = self.c
        for t in range(TT):
            for k in range(DC):
                last = pe.matmul(c.ps[6][:, 8 * t:8 * t + 8], c.XT[:, k, t * P:(t + 1) * P], self.wr[:, k, :],
                                 start=(k == 0), stop=(k == DC - 1))
        last.then_inc(self.logits, 1)

    def pe_turn(self, pe):
        c = self.c
        pe.wait_ge(self.gated, 1)
        for t in range(TT):
            last = pe.transpose(c.ps[7][0:self.n, t * P:(t + 1) * P], self.G[:, t, :], c.ident[:, :])
        last.then_inc(self.turned, 1)
        pe.wait_ge(self.gt, 1)
        for e in range(2):
            pe.matmul(c.ps[6 + e][:, :], c.sel[:, e, :], self.GT[0:NH, :], start=True, stop=True).then_inc(self.spread, 1)

    def act(self, act):
        act.wait_ge(self.shifted, 1)
        act.activation(self.L, self.L, ACT.Exp).then_inc(self.exped, 1)

    def act_gates(self, act, GB, loaded):
        for e in range(2):
            act.wait_ge(self.spread, e + 1)
            act.copy(GB[:, e, :], self.c.ps[6 + e][:, :]).then_inc(loaded[e], 16)

    def dve(self, dve, parts):
        c, own = self.c, self.c.own_dve
        dve.wait_ge(self.x_in, 2)
        parts.x(dve)
        logits = c.ps[6][:, 0:8 * TT].rearrange("p (t e) -> p t e", t=TT)
        dve.wait_ge(self.logits, 1)
        if self.bias is not None:
            own(dve, dve.tensor_tensor(self.L, logits, free(self.bias[:, :], (0, TT), (1, 8)), ALU.add))
        else:
            own(dve, dve.tensor_copy(self.L, logits))
        own(dve, dve.tensor_reduce(self.NMX, self.L, AX.X, ALU.max, negate=True))
        dve.tensor_tensor(self.L, self.L, free(self.NMX, (1, TT), (0, 8)), ALU.add).then_inc(self.shifted, 1)
        dve.wait_ge(self.exped, 1)
        own(dve, dve.tensor_reduce(self.SM, self.L, AX.X, ALU.add))
        own(dve, dve.reciprocal(self.SM, self.SM))
        own(dve, dve.tensor_tensor(self.L, self.L, free(self.SM, (1, TT), (0, 8)), ALU.mult))
        sk, sj = free(self.L, (8, TT), (0, 8), (1, 8)), free(self.L, (8, TT), (1, 8), (0, 8))
        dve.tensor_tensor(self.CMP, sk, sj, ALU.is_gt)
        own(dve, dve.tensor_tensor(self.EQ, sk, sj, ALU.is_equal))
        own(dve, dve.tensor_tensor(self.EQ, self.EQ, free(c.tri[:, :, :], (0, TT), (8, 8), (1, 8)), ALU.mult))
        own(dve, dve.tensor_tensor(self.CMP, self.CMP, self.EQ, ALU.add))
        own(dve, dve.tensor_reduce(self.RK, self.CMP, AX.X, ALU.add))
        last = dve.scalar_tensor_tensor(out=self.G[:, :, 0:8], in0=self.RK, scalar=1.5, in1=self.L,
                                        op0=ALU.is_lt, op1=ALU.mult)
        if self.renorm:
            own(dve, last)
            own(dve, dve.tensor_reduce(self.SM, self.G, AX.X, ALU.add))
            own(dve, dve.reciprocal(self.SM, self.SM))
            last = dve.tensor_tensor(self.G, self.G, free(self.SM, (1, TT), (0, 8)), ALU.mult)
        if self.extra:
            last = dve.memset(self.G[:, :, 8:self.n], 1.0)
        last.then_inc(self.gated, 1)
        dve.wait_ge(self.turned, 1)
        dve.tensor_copy(self.GT[0:self.n, :], c.ps[7][0:self.n, :]).then_inc(self.gt, 1)

    def store(self, sp):
        sp.wait_ge(self.gt, 1)
        sp.dma_start(self.dram, self.GT[0:self.n, :]).then_inc(self.stored, 16)
        sp.wait_ge(self.stored, 16)


class Combine:

    def __init__(self, core, a, name):
        self.c, self.YT = core, a.take(DC, S)
        self.sum = core.sem(name + "_experts_summed")
        self.copied = core.sem(name + "_sum_copied")
        self.turned = core.sem(name + "_sum_turned")
        self.norm = Norm(core, name)

    def pe(self, pe):
        c = self.c
        pe.wait_ge(self.copied, 2)
        for t in range(TT):
            for k in range(DC):
                last = pe.transpose(c.ps[2 + t][:, k * P:(k + 1) * P],
                                    self.YT[:, k, t * P:(t + 1) * P], c.ident[:, :])
            last.then_inc(self.turned, 1)

    def act(self, act):
        act.wait_ge(self.sum, 1)
        act.copy(self.YT[:, 1, :], self.c.ps[1][:, :]).then_inc(self.copied, 1)

    def dve(self, dve):
        c = self.c
        dve.wait_ge(self.sum, 1)
        dve.tensor_copy(self.YT[:, 0, :], c.ps[0][:, :]).then_inc(self.copied, 1)
        for t in range(TT):
            dve.wait_ge(self.turned, t + 1)
            self.norm.stats(dve, t, c.ps[2 + t][:, 0:D])
        for t in range(TT):
            self.norm.apply(dve, t)


def raw0(core):
    return [core.work[:, W0_AT + i * W0:W0_AT + (i + 1) * W0] for i in range(2)]


def raw1(core):
    return [core.work[:, W1_AT + i * 2 * C1:W1_AT + (i + 1) * 2 * C1] for i in range(4)]


class Parts:

    def __init__(self, core, name, tensor, chunk, slots, hid):
        self.c = core
        at = 0

        def take(n):
            nonlocal at
            at += n
            return tensor[:, at - n:at]
        self.W = [[take(chunk) for _ in range(slots)] for _ in range(2)]
        self.X = [take(DC * S).rearrange("p (c n) -> p c n", c=DC) for _ in range(2)]
        self.H = [[take(S) for _ in range(hid)] for _ in range(2)]
        assert at == tensor.shape[1]
        self.x_parts = core.sem(name + "_x_parts_ready")

    def x(self, dve):
        dve.tensor_copy(self.X[0], self.c.XT[:, :, :]).then_inc(self.x_parts, 1)
        dve.wait_ge(self.x_parts, 1)
        rest(dve, self.X[1], self.c.XT[:, :, :], self.X[0]).then_inc(self.x_parts, 1)

    def product(self, pe, out, slot, at, rhs, ks, start=False, stop=False):
        n = 0
        for k in ks:
            for a, b in ((0, 0), (0, 1), (1, 0)):
                n += 1
                last = pe.matmul(out, self.W[a][slot][:, at(k):at(k) + P], rhs(b, k),
                                 start=start and n == 1, stop=stop and n == 3 * len(ks))
        return last


def rest(eng, out, x, hi):
    return eng.tensor_tensor(out, x, hi.bitcast(F32), ALU.subtract)


def silu_experts(core, w_in, prefetch):
    nc, ps = core.nc, core.ps
    a = core.arena()
    RAW = raw0(core)
    GB = a.take(2, S)
    BB = a.take(2, 4)
    SL, HF = a.take(2, S), a.take(2, S)
    turn = turn_x(core, "c")
    router = Router(core, a, "c", core.WR0, core.rb0, 2, False, core.dram["gates0"], turn.ready)
    combine = Combine(core, a, "c")
    assert a.at <= W0_AT and W0_AT + 2 * W0 <= WQKV_AT and WQKV_AT + DC * 3072 + PARTS0 <= core.size
    parts = Parts(core, "c", core.parts[0], C0, 4, 2)
    g_in = [core.sem(f"c_gate_loaded{i}") for i in range(2)]
    uwh, uwl = core.sem("c_up_weights_hi_ready"), core.sem("c_up_weights_lo_ready")
    dwh, dwl = core.sem("c_down_weights_hi_ready"), core.sem("c_down_weights_lo_ready")
    up, sl, sg = core.sem("c_up_ready"), core.sem("c_silu_ready"), core.sem("c_gated_silu_ready")
    hf = core.sem("c_hidden_ready")
    hh, hl = core.sem("c_hidden_hi_ready"), core.sem("c_hidden_lo_ready")
    dn = core.sem("c_down_done")
    pairs, UP = E0A // 2, 2 * DC * P

    def raw(r):
        return RAW[r // 2][:, r % 2 * C0:(r % 2 + 1) * C0]


    with nc.Block() as block:
        @block.sync
        def _(sp):
            for s in range(2):
                sp.dma_start(BB[:, s, :], core.dram["b_e0"][s]).then_inc(g_in[s], 16)
            router.store(sp)

            def gates(e, s):
                sp.dma_start(GB[:, s, :], row(core.dram["gates0"], e)).then_inc(g_in[s], 16)
                sp.dma_start(BB[:, s, :], core.dram["b_e0"][e]).then_inc(g_in[s], 16)
            with sp.Fori(0, pairs - 1) as i:
                for s in range(2):
                    sp.wait_ge(uwl, 4 * i + (2 * s + 2))
                    sp.wait_ge(dwl, 4 * i + (2 * s + 2))
                    sp.dma_start(RAW[s], core.dram["w_e0"][2 * i + (2 + s)]).then_inc(w_in[s], 16)
                for s in range(2):
                    sp.wait_ge(hf, 4 * i + (2 * s + 4))
                    gates(2 * i + (2 + s), s)
            prefetch(sp)

        @block.tensor
        def _(pe):
            turn.pe(pe)
            pe.wait_ge(turn.ready, 2)
            router.pe(pe)
            pe.wait_ge(parts.x_parts, 2)

            def up_chunk(i, r):
                pe.wait_ge(uwl, 4 * i + (r + 1))
                pe.wait_ge(hf, 4 * i + (r + 1))
                for kind in range(2):
                    last = parts.product(pe, ps[2 + 2 * (r % 2) + kind][:, :], r, lambda k: (kind * DC + k) * P,
                                         lambda b, k: parts.X[b][:, k, :], range(DC), start=True, stop=True)
                last.then_inc(up, 1)

            def down_chunk(i, r, end):
                pe.wait_ge(dwl, 4 * i + (r + 1))
                pe.wait_ge(hl, 4 * i + (r + 1))
                for d in range(DC):
                    last = parts.product(pe, ps[d][:, :], r, lambda k: (2 * DC + d) * P,
                                         lambda b, k: parts.H[b][r % 2], (0,), stop=end)
                last.then_inc(combine.sum if end else dn, 1)

            up_chunk(0, 0)
            up_chunk(0, 1)
            router.pe_turn(pe)
            for k in range(DC):
                pe.matmul(ps[k][:, :], core.B2[:, k * P:(k + 1) * P], router.GT[0:E0A, :], start=True, stop=False)
            with pe.Fori(0, pairs - 1) as i:
                for r in range(4):
                    up_chunk(i + (r + 2) // 4, (r + 2) % 4)
                    down_chunk(i, r, False)
            for r in range(4):
                if r < 2:
                    up_chunk(pairs - 1, r + 2)
                down_chunk(pairs - 1, r, r == 3)
            combine.pe(pe)

        @block.scalar
        def _(act):
            turn.act(act)

            def up_weights_hi(i, r):
                act.wait_ge(w_in[r // 2], 16 * i + 16)
                act.copy(parts.W[0][r][:, 0:UP], raw(r)[:, 0:UP]).then_inc(uwh, 1)

            def down_weights_hi(i, r):
                act.wait_ge(dn, 4 * i + (r + 1))
                act.copy(parts.W[0][r][:, UP:C0], raw(r)[:, UP:C0]).then_inc(dwh, 1)

            def chunk(i, r, end):
                act.wait_ge(g_in[r // 2], 32 * i + 32)
                act.wait_ge(up, 4 * i + (r + 1))
                act.activation(SL[:, r % 2, :], ps[2 + 2 * (r % 2)][:, :], ACT.Silu,
                               bias=BB[:, r // 2, r % 2:r % 2 + 1]).then_inc(sl, 1)
                if r == 0 or not end:
                    up_weights_hi(i + (r + 3) // 4, (r + 3) % 4)
                act.wait_ge(hf, 4 * i + (r + 3))
                act.wait_ge(dn, 4 * i + (r + 3))
                act.copy(parts.H[0][r % 2], HF[:, r % 2, :]).then_inc(hh, 1)
                if r == 0 or not end:
                    down_weights_hi(i + (r + 3) // 4, (r + 3) % 4)

            for r in range(3):
                up_weights_hi(0, r)
                down_weights_hi(0, r)
            router.act(act)
            router.act_gates(act, GB, g_in)
            with act.Fori(0, pairs - 1) as i:
                for r in range(4):
                    chunk(i, r, False)
            for r in range(4):
                chunk(pairs - 1, r, True)
            combine.act(act)

        @block.gpsimd
        def _(pool):
            def up_weights_lo(i, r):
                pool.wait_ge(uwh, 4 * i + (r + 1))
                rest(pool, parts.W[1][r][:, 0:UP], raw(r)[:, 0:UP], parts.W[0][r][:, 0:UP]).then_inc(uwl, 1)

            def down_weights_lo(i, r):
                pool.wait_ge(dwh, 4 * i + (r + 1))
                rest(pool, parts.W[1][r][:, UP:C0], raw(r)[:, UP:C0], parts.W[0][r][:, UP:C0]).then_inc(dwl, 1)

            def chunk(i, r, end):
                pool.wait_ge(g_in[r // 2], 32 * i + 32)
                pool.wait_ge(sl, 4 * i + (r + 1))
                pool.tensor_tensor(SL[:, r % 2, :], SL[:, r % 2, :], GB[:, r // 2, :], ALU.mult).then_inc(sg, 1)
                if r == 0 or not end:
                    up_weights_lo(i + (r + 3) // 4, (r + 3) % 4)
                if r < 2 or not end:
                    down_weights_lo(i + (r + 2) // 4, (r + 2) % 4)

            for r in range(3):
                up_weights_lo(0, r)
                if r < 2:
                    down_weights_lo(0, r)
            with pool.Fori(0, pairs - 1) as i:
                for r in range(4):
                    chunk(i, r, False)
            for r in range(4):
                chunk(pairs - 1, r, True)
            for t in range(TT):
                combine.norm.pool(pool, t)

        @block.vector
        def _(dve):
            dve.sem_inc(hf, 2)
            dve.sem_inc(dn, 4)
            turn.dve(dve)
            router.dve(dve, parts)
            with dve.Fori(0, pairs) as i:
                for r in range(4):
                    dve.wait_ge(sg, 4 * i + (r + 1))
                    dve.scalar_tensor_tensor(out=HF[:, r % 2, :], in0=ps[3 + 2 * (r % 2)][:, :],
                                             scalar=BB[:, r // 2, 2 + r % 2:3 + r % 2], in1=SL[:, r % 2, :],
                                             op0=ALU.add, op1=ALU.mult).then_inc(hf, 1)
                    dve.wait_ge(hh, 4 * i + (r + 1))
                    rest(dve, parts.H[1][r % 2], HF[:, r % 2, :], parts.H[0][r % 2]).then_inc(hl, 1)
            combine.dve(dve)


def row(dram, e):
    return (dram[e, :] if isinstance(e, int) else dram[bass.ds(e, 1), :]).partition_broadcast(P)


def relu_experts(core, w_in, b):
    nc, ps = core.nc, core.ps
    a = core.arena()
    RAW = raw1(core)
    GB, HF = a.take(2, S), a.take(4, S)
    turn = turn_x(core, "f")
    router = Router(core, a, "f", core.WR1, None, 0, True, core.dram["gates1"], turn.ready)
    combine = Combine(core, a, "f")
    assert a.at <= W1_AT and W1_AT + W1 <= XN_AT and XN_AT + TT * D + PARTS1 <= core.size
    parts = Parts(core, "f", core.parts[1], C1, 8, 4)
    g_in = [core.sem(f"f_gate_loaded{i}") for i in range(2)]
    wh, wl = core.sem("f_weights_hi_ready"), core.sem("f_weights_lo_ready")
    up = core.sem("f_up_ready")
    hf = core.sem("f_hidden_ready")
    hh, hl = core.sem("f_hidden_hi_ready"), core.sem("f_hidden_lo_ready")
    dn = core.sem("f_down_done")
    x_in = core.sem("f_next_x_loaded")
    pairs, MC, LEAD = E1 // 2, F1 // P, 4
    N = 2 * MC

    def raw(r):
        return RAW[r % MC // 2][:, r % 2 * C1:(r % 2 + 1) * C1]

    with nc.Block() as block:
        @block.sync
        def _(sp):
            sp.dma_start(core.x_next, core.dram["x"][bass.ds(b + 1, 1)].rearrange(
                "b (t p) d -> p (b t) d", p=P)).then_inc(x_in, 16)
            router.store(sp)

            def gates(e, s):
                sp.dma_start(GB[:, s, :], row(core.dram["gates1"], e)).then_inc(g_in[s], 16)

            def weights(i, s, e):
                for k in range(4):
                    sp.wait_ge(wl, N * i + (MC * s + 2 * k + 2))
                    sp.dma_start(RAW[k], core.dram["w_e1"][e][:, 2 * k * C1:2 * (k + 1) * C1]).then_inc(w_in[k], 16)
            with sp.Fori(0, pairs - 1) as i:
                weights(i, 0, 2 * i + 1)
                sp.wait_ge(hf, N * i + (MC + 4))
                gates(2 * i + 2, 0)
                weights(i, 1, 2 * i + 2)
                sp.wait_ge(hf, N * i + (2 * MC + 4))
                gates(2 * i + 3, 1)
            weights(pairs - 1, 0, E1 - 1)
            for t in range(TT):
                sp.wait_ge(combine.norm.x_ready, t + 1)
                sp.dma_start(core.dram["out"][b, t * P:(t + 1) * P, :], core.X[:, t, :]).then_inc(core.stored, 16)
            sp.wait_ge(x_in, 16)

        @block.tensor
        def _(pe):
            turn.pe(pe)
            pe.wait_ge(turn.ready, 2)
            router.pe(pe)
            for k in range(DC):
                pe.matmul(ps[k][:, :], core.ident_bf[:, :], core.zero_bf[:, :], start=True, stop=False)
            pe.wait_ge(parts.x_parts, 2)

            def up_chunk(i, r):
                pe.wait_ge(wl, N * i + (r + 1))
                pe.wait_ge(hf, N * i + (r + 1))
                parts.product(pe, ps[2 + r % 4][:, :], r % MC, lambda k: k * P, lambda b, k: parts.X[b][:, k, :],
                              range(DC), start=True, stop=True).then_inc(up, 1)

            def down_chunk(i, r, end):
                pe.wait_ge(hl, N * i + (r + 1))
                for d in range(DC):
                    last = parts.product(pe, ps[d][:, :], r % MC, lambda k: (DC + d) * P,
                                         lambda b, k: parts.H[b][r % 4], (0,), stop=end)
                last.then_inc(combine.sum if end else dn, 1)

            up_chunk(0, 0)
            up_chunk(0, 1)
            router.pe_turn(pe)
            with pe.Fori(0, pairs - 1) as i:
                for r in range(N):
                    up_chunk(i + (r + 2) // N, (r + 2) % N)
                    down_chunk(i, r, False)
            for r in range(N):
                if r + 2 < N:
                    up_chunk(pairs - 1, r + 2)
                down_chunk(pairs - 1, r, r == N - 1)
            combine.pe(pe)

        @block.scalar
        def _(act):
            turn.act(act)

            def weights_hi(i, r):
                act.wait_ge(w_in[r % MC // 2], 32 * i + (16 * (r // MC) + 16))
                act.wait_ge(dn, N * i + (r + 1))
                act.copy(parts.W[0][r % MC], raw(r)).then_inc(wh, 1)

            def chunk(i, r, end):
                if r + LEAD < N or not end:
                    weights_hi(i + (r + LEAD) // N, (r + LEAD) % N)
                act.wait_ge(hf, N * i + (r + 5))
                act.wait_ge(dn, N * i + (r + 5))
                act.copy(parts.H[0][r % 4], HF[:, r % 4, :]).then_inc(hh, 1)

            act.wait_ge(dn, MC)
            for r in range(LEAD):
                weights_hi(0, r)
            router.act(act)
            router.act_gates(act, GB, g_in)
            with act.Fori(0, pairs - 1) as i:
                for r in range(N):
                    chunk(i, r, False)
            for r in range(N):
                chunk(pairs - 1, r, True)
            combine.act(act)

        @block.gpsimd
        def _(pool):
            with pool.Fori(0, pairs) as i:
                for r in range(N):
                    pool.wait_ge(wh, N * i + (r + 1))
                    rest(pool, parts.W[1][r % MC], raw(r), parts.W[0][r % MC]).then_inc(wl, 1)
            for t in range(TT):
                combine.norm.pool(pool, t)

        @block.vector
        def _(dve):
            dve.sem_inc(hf, 4)
            dve.sem_inc(dn, MC)
            turn.dve(dve)
            router.dve(dve, parts)

            def hidden(i, r):
                if r % MC == 0:
                    dve.wait_ge(g_in[r // MC], 16 * i + 16)
                dve.wait_ge(up, N * i + (r + 1))
                dve.scalar_tensor_tensor(out=HF[:, r % 4, :], in0=ps[2 + r % 4][:, :], scalar=0.0,
                                         in1=GB[:, r // MC, :], op0=ALU.max, op1=ALU.mult).then_inc(hf, 1)

            def hidden_lo(i, r):
                dve.wait_ge(hh, N * i + (r + 1))
                rest(dve, parts.H[1][r % 4], HF[:, r % 4, :], parts.H[0][r % 4]).then_inc(hl, 1)

            hidden(0, 0)
            with dve.Fori(0, pairs - 1) as i:
                for r in range(N):
                    hidden(i + (r + 1) // N, (r + 1) % N)
                    hidden_lo(i, r)
            for r in range(N):
                if r + 1 < N:
                    hidden(pairs - 1, r + 1)
                hidden_lo(pairs - 1, r)
            combine.dve(dve)



def rope_attention(core):
    nc, ps = core.nc, core.ps
    a = core.arena()
    QT, KT, V = a.take(8, S), a.take(8, S), a.take(TT, H1 * HD1)
    assert a.at == WQKV_AT
    SC = a.take(S, H1)
    W = core.work[:, WQKV_AT:WQKV_AT + DC * 3072].rearrange("p (c n) -> p c n", c=DC)
    end = a.at
    M1, M2, RT = a.take(2, S), a.take(2, S), a.take(4, S)
    a.at = end
    assert a.at == TS_AT
    a.take(2, S)
    PTS = a.take(2, S)
    HS, HG, PR = a.take(2, S), a.take(4, S), a.take(3, S)
    PTS = [PTS[:, 0, :], PTS[:, 1, :], HG[:, 2, :]]
    TH = [core.turned_scores[:, i * S:(i + 1) * S] for i in range(2)]
    TL = [core.turned_scores[:, i * S:(i + 1) * S] for i in range(2, 4)]
    QZ = a.take(H1, P)
    MG = a.take(JG // 2, H1)
    RX = HS.rearrange("p a b -> p (a b)")
    OT = PR[:, 0:2, :].rearrange("p a b -> p (a b)").rearrange("p (c t) -> p c t", c=8)
    NM, DEN, RD = a.take(64), a.take(64), a.take(64)

    turn = turn_x(core, "d")
    s = lambda x: core.sem("d_" + x)
    proj, roped, vcop = s("projected"), s("rope_products_ready"), s("v_ready")
    rot, tq, qk = s("rotated"), s("qk_turned"), s("qkT_ready")
    sc, scc, tt_, tev, kf = s("scores_ready"), s("scores_copied"), s("scores_turned"), s("scoresT_ready"), s("kerple_added")
    h1, hs, gl, l2, fa = s("hidden_product"), s("hidden_biased"), s("gelu_ready"), s("refined_ready"), s("refined_added")
    mx, ex, tr, pt, pv = s("max_ready"), s("probs_ready"), s("probs_turned"), s("probsT_ready"), s("values_done")
    bcc = s("spread_inverses_copied")
    th = s("scoresT_hi_ready")
    rd, bc, otr, y = s("denominators_inverted"), s("inverses_spread"), s("outT_ready"), s("y_ready")
    qz, gm = s("padded_q_ready"), s("group_max_ready")
    norm = Norm(core, "d")
    base = [2 * it * (it + 1) for it in range(TT + 1)]
    last_group = lambda it: 4 * (it + 1) - 1

    def table(it, g, hf):
        o = P * (it + 1) - JG * g - 24 - 4 * hf
        return free(core.TB[:, o:o + 1], (8, 4), (1, P))

    with nc.Block() as block:
        @block.gpsimd
        def _(pool):
            def pad_q(it):
                pool.wait_ge(qk, 4 * (it + 1))
                if it >= 1:
                    pool.wait_ge(sc, H1 * it)
                    pool.wait_ge(kf, base[it])
                else:
                    pool.wait_ge(rot, 4 * 3)
                for k in range(2):
                    r = slice(64 * k, 64 * k + 64)
                    pool.tensor_copy(QZ[r].rearrange("p (h k) t -> p h k t", k=2)[:, :, k, :],
                                     QT[r, :, it * P:(it + 1) * P]).then_inc(qz, 1)
                pool.wait_ge(qz, 2 * (it + 1))

            core.own_pool(pool, pool.memset(QZ, 0.0))
            for t in range(TT):
                for i in range(4):
                    n = 4 * t + i
                    pool.wait_ge(roped, n + 1)
                    if t >= 1 and i == 0:
                        pool.wait_ge(tq, 4 * t)
                    pool.tensor_tensor(RT[:, i, :], M1[:, n % 2, :], M2[:, n % 2, :], ALU.add).then_inc(rot, 1)
                if t == 2:
                    pad_q(0)
            for it in range(TT):
                for g in range(last_group(it) + 1):
                    n = base[it] + g
                    pool.wait_ge(tt_, n + 1)
                    v = S - P - it * P + g * JG
                    pool.tensor_tensor(SC[:, g * JG:(g + 1) * JG, :], SC[:, g * JG:(g + 1) * JG, :],
                                       core.KF[:, v:v + JG, :], ALU.add).then_inc(kf, 1)
                if it + 1 < TT:
                    pad_q(it + 1)
            for t in range(TT):
                norm.pool(pool, t)

        @block.tensor
        def _(pe):
            turn.pe(pe)
            pe.wait_ge(turn.ready, 2)

            def project(t):
                for i in range(6):
                    if t >= 1:
                        if i < 4:
                            pe.wait_ge(roped, 4 * (t - 1) + i + 1)
                        else:
                            pe.wait_ge(vcop, 2 * (t - 1) + i - 3)
                    for k in range(DC):
                        last = pe.matmul(ps[i][:, :], core.XT[:, k, t * P:(t + 1) * P],
                                         W[:, k, i * 512:(i + 1) * 512], start=(k == 0), stop=(k == DC - 1))
                    last.then_inc(proj, 1)

            def turn_qk(t):
                for i in range(4):
                    n = 4 * t + i
                    pe.wait_ge(rot, n + 1)
                    if n >= 2:
                        pe.wait_ge(qk, n - 1)
                    for j in range(4):
                        last = pe.transpose(ps[6 + n % 2][:, j * P:(j + 1) * P], RT[:, i, j * P:(j + 1) * P],
                                            core.ident[:, :])
                    last.then_inc(tq, 1)

            def scores(it):
                if it >= 1:
                    pe.wait_ge(pt, H1 * it)
                else:
                    pe.wait_ge(roped, 4 * (TT - 1) + 2)
                pe.wait_ge(qz, 2 * (it + 1))
                for h in range(H1):
                    n = H1 * it + h
                    if h >= 2:
                        pe.wait_ge(scc, n - 1)
                    pe.matmul(ps[n % 2][:, 0:(it + 1) * P], QZ[:, h, :], KT[:, h // 2, 0:(it + 1) * P],
                              start=True, stop=True).then_inc(sc, 1)

            def turn_scores(it, g):
                n = base[it] + g
                if n >= 1:
                    pe.wait_ge(tev, n)
                for j in range(4):
                    last = pe.transpose(ps[2][:, (3 - j) * P:(4 - j) * P], SC[:, g * JG + 8 * j:g * JG + 8 * j + 8, :],
                                        core.ident[:, :])
                last.then_inc(tt_, 1)

            def hidden(it, g):
                n = base[it] + g
                pe.wait_ge(tev, n + 1)
                for hf in range(2):
                    if n >= 1:
                        pe.wait_ge(hs, 2 * n + hf - 1)
                    hi, lo = core.W1H[:, hf, :], core.W1L[:, hf, :]
                    pe.matmul(ps[3 + hf][:, :], hi, TH[n % 2], start=True, stop=False)
                    pe.matmul(ps[3 + hf][:, :], lo, TH[n % 2], start=False, stop=False)
                    pe.matmul(ps[3 + hf][:, :], hi, TL[n % 2], start=False, stop=True).then_inc(h1, 1)

            def refine(it, g):
                n = base[it] + g
                pe.wait_ge(gl, 2 * n + 2)
                if n >= 1:
                    pe.wait_ge(fa, n)
                for j in range(4):
                    for hf in range(2):
                        o = (8 * j + 4 * hf) * H1
                        last = pe.matmul(ps[5][:, o:o + 64], HG[:, (2 * n + hf) % 4, (3 - j) * P:(4 - j) * P],
                                         core.W2B[:, :], start=True, stop=True)
                last.then_inc(l2, 1)

            def turn_probs(it, h):
                n = H1 * it + h
                pe.wait_ge(ex, n + 1)
                if h >= 3:
                    pe.wait_ge(pt, n - 2)
                elif n % 3 == 2:
                    pe.wait_ge(tev, base[it + 1])
                for j in range(it + 1):
                    last = pe.transpose(ps[n % 3][:, j * P:(j + 1) * P], PR[:, n % 3, j * P:(j + 1) * P],
                                        core.ident[:, :])
                last.then_inc(tr, 1)

            def values(it, h):
                n = H1 * it + h
                pe.wait_ge(pt, n + 1)
                rows = slice(h % 2 * HD1, (h % 2 + 1) * HD1)
                for j in range(it + 1):
                    last = pe.matmul(ps[6 + h // 8][rows, h % 8 // 2 * P:(h % 8 // 2 + 1) * P],
                                     V[:, j, h * HD1:(h + 1) * HD1], PTS[n % 3][:, j * P:(j + 1) * P],
                                     start=(j == 0), stop=(j == it))
                last.then_inc(pv, 1)

            def spread_inverses(it):
                pe.wait_ge(rd, it + 1)
                for p in range(H1 // 2):
                    last = pe.matmul(ps[3 + p // 4][:, (p % 4) * P:(p % 4 + 1) * P],
                                     RX[:, p * P:(p + 1) * P], core.ident[:, :], start=True, stop=True)
                last.then_inc(bc, 1)

            def out(it):
                pe.wait_ge(otr, it + 1)
                for c in range(8):
                    last = pe.matmul(ps[3][:, 0:D], OT[:, c, :], core.WO1[:, c, :], start=(c == 0), stop=(c == 7))
                last.then_inc(y, 1)

            project(0)
            for t in range(TT):
                if t + 1 < TT:
                    project(t + 1)
                else:
                    scores(0)
                turn_qk(t)
            for it in range(TT):
                pe.wait_ge(scc, H1 * (it + 1))
                turn_scores(it, 0)
                for g in range(last_group(it) + 1):
                    if g < last_group(it):
                        turn_scores(it, g + 1)
                    hidden(it, g)
                    if g >= 1:
                        refine(it, g - 1)
                refine(it, last_group(it))
                if it >= 1:
                    pe.wait_ge(hs, 2 * base[it + 1] - 1)
                    out(it - 1)
                if it == 0:
                    pe.wait_ge(vcop, 2 * TT)
                for h in range(H1 + 2):
                    if h < H1:
                        turn_probs(it, h)
                    if h >= 2:
                        values(it, h - 2)
                if it >= 1:
                    pe.wait_ge(norm.var_ready, it)
                spread_inverses(it)
                if it == 0:
                    pe.wait_ge(qk, 4 * TT)
                if it + 1 < TT:
                    scores(it + 1)
            out(TT - 1)

        @block.scalar
        def _(act):
            def copy_turned(act, t):
                for i in range(4):
                    n = 4 * t + i
                    act.wait_ge(tq, n + 1)
                    dst = (QT if i < 2 else KT)[:, 4 * (i % 2):4 * (i % 2) + 4, t * P:(t + 1) * P]
                    act.mul(dst, ps[6 + n % 2][:, :].rearrange("p (a b) -> p a b", a=4),
                            1.0 if i < 2 else 1.0 / math.sqrt(HD1)).then_inc(qk, 1)

            turn.act(act)
            for t in range(TT):
                for i in range(2):
                    act.wait_ge(proj, 6 * t + 5 + i)
                    act.copy(V[:, t, i * 512:(i + 1) * 512], ps[4 + i][:, :]).then_inc(vcop, 1)
                if t >= 1:
                    copy_turned(act, t - 1)

            def copy_scores(it):
                for h in range(H1):
                    n = H1 * it + h
                    act.wait_ge(sc, n + 1)
                    act.copy(SC[:, 0:(it + 1) * P, h], ps[n % 2][:, 0:(it + 1) * P]).then_inc(scc, 1)

            def copy_turned_scores(it, g):
                n = base[it] + g
                act.wait_ge(tt_, n + 1)
                if n >= 2:
                    act.wait_ge(h1, 2 * (n - 1))
                act.copy(TH[n % 2], ps[2][:, :]).then_inc(th, 1)

            copy_scores(0)
            copy_turned(act, TT - 1)
            for it in range(TT):
                copy_turned_scores(it, 0)
                for g in range(last_group(it) + 1):
                    if g < last_group(it):
                        copy_turned_scores(it, g + 1)
                    n = base[it] + g
                    for hf in range(2):
                        z = 2 * n + hf
                        act.wait_ge(hs, z + 1)
                        if z >= 4:
                            act.wait_ge(l2, n - 1)
                        act.activation(HG[:, z % 4, :], HS[:, z % 2, :], ACT.Gelu).then_inc(gl, 1)
                act.wait_ge(mx, it + 1)
                w = (it + 1) * P
                for h in range(H1):
                    n = H1 * it + h
                    if n >= 3:
                        act.wait_ge(tr, n - 2)
                    if h == 0 and it >= 1:
                        act.wait_ge(y, it)
                    act.activation(PR[:, n % 3, 0:w], SC[:, 0:w, h], ACT.Exp, bias=NM[:, n:n + 1],
                                   accum_out=DEN[:, n:n + 1]).then_inc(ex, 1)
                act.wait_ge(bc, it + 1)
                act.copy(HG[:, 0, :], ps[3][:, :])
                act.copy(HG[:, 1, :], ps[4][:, :]).then_inc(bcc, 1)
                if it + 1 < TT:
                    copy_scores(it + 1)

        @block.vector
        def _(dve):
            own = core.own_dve
            turn.dve(dve)
            for t in range(TT):
                for i in range(4):
                    n = 4 * t + i
                    dve.wait_ge(proj, 6 * t + i + 1)
                    if n >= 2:
                        dve.wait_ge(rot, n - 1)
                    x = ps[i][:, :].rearrange("p (h d) -> p h d", h=8)
                    m1 = M1[:, n % 2, :].rearrange("p (h d) -> p h d", h=8)
                    m2 = M2[:, n % 2, :].rearrange("p (h d) -> p h d", h=8)
                    dve.tensor_tensor(m1, x, free(core.rope[:, t, 0, :], (0, 8), (1, HD1)), ALU.mult)
                    dve.tensor_tensor(m2[:, :, 0:32], x[:, :, 32:64], free(core.rope[:, t, 1, 0:32], (0, 8), (1, 32)), ALU.mult)
                    dve.tensor_tensor(m2[:, :, 32:64], x[:, :, 0:32], free(core.rope[:, t, 1, 32:64], (0, 8), (1, 32)),
                                      ALU.mult).then_inc(roped, 1)

            def turned_scores_rest(it, g):
                n = base[it] + g
                dve.wait_ge(th, n + 1)
                rest(dve, TL[n % 2], ps[2][:, :], TH[n % 2]).then_inc(tev, 1)

            def add_refined(it, g):
                n = base[it] + g
                dve.wait_ge(l2, n + 1)
                dve.wait_ge(kf, n + 1)
                c = SC[:, g * JG:(g + 1) * JG, :]
                dve.tensor_tensor(c, ps[5][:, :].rearrange("p (j h) -> p j h", h=H1), c, ALU.add).then_inc(fa, 1)
                dve.wait_ge(fa, n + 1)
                dve.tensor_reduce(MG[:, g, :], c.rearrange("p j h -> p h j"), AX.X, ALU.max).then_inc(gm, 1)

            for it in range(TT):
                w = (it + 1) * P
                turned_scores_rest(it, 0)
                for g in range(last_group(it) + 1):
                    if g < last_group(it):
                        turned_scores_rest(it, g + 1)
                    n = base[it] + g
                    for hf in range(2):
                        z = 2 * n + hf
                        dve.wait_ge(h1, z + 1)
                        if z >= 2:
                            dve.wait_ge(gl, z - 1)
                        dve.tensor_tensor(HS[:, z % 2, :].rearrange("p (c i) -> p c i", c=4),
                                          ps[3 + hf][:, :].rearrange("p (c i) -> p c i", c=4), table(it, g, hf),
                                          ALU.add).then_inc(hs, 1)
                    if g >= 1:
                        add_refined(it, g - 1)
                add_refined(it, last_group(it))
                dve.wait_ge(gm, base[it + 1])
                dve.tensor_reduce(NM[:, H1 * it:H1 * (it + 1)],
                                  MG[:, 0:last_group(it) + 1, :].rearrange("p g h -> p h g"), AX.X, ALU.max,
                                  negate=True).then_inc(mx, 1)
                if it >= 1:
                    dve.wait_ge(y, it)
                    norm.stats(dve, it - 1, ps[3][:, 0:D])
                for h in range(H1):
                    n = H1 * it + h
                    dve.wait_ge(tr, n + 1)
                    if n >= 3:
                        dve.wait_ge(pv, n - 2)
                    dve.tensor_copy(PTS[n % 3][:, 0:w], ps[n % 3][:, 0:w]).then_inc(pt, 1)
                dve.wait_ge(ex, H1 * (it + 1))
                inverse = RD[:, H1 * it:H1 * (it + 1)]
                own(dve, dve.reciprocal(inverse, DEN[:, H1 * it:H1 * (it + 1)]))
                dve.tensor_copy(RX.rearrange("p (h d) -> p h d", h=H1), free(inverse, (1, H1), (0, HD1))).then_inc(rd, 1)
                dve.wait_ge(pv, H1 * (it + 1))
                dve.wait_ge(bcc, it + 1)
                for k in range(2):
                    last = dve.tensor_tensor(OT[:, 4 * k:4 * k + 4, :], ps[6 + k][:, :].rearrange("p (c t) -> p c t", c=4),
                                             HG[:, k, :].rearrange("p (c t) -> p c t", c=4), ALU.mult)
                last.then_inc(otr, 1)
            dve.wait_ge(y, TT)
            norm.stats(dve, TT - 1, ps[3][:, 0:D])
            for t in range(TT):
                norm.apply(dve, t)



def decoder(nc, dram):
    with ExitStack() as ctx:
        core = Core(nc, ctx, dram)
        with core.semaphores():
            setup(core)
        with nc.Fori(0, B) as b:
            with core.semaphores():
                layer0(core, b)
            with core.semaphores():
                layer1(core, b)
        with nc.Block() as block:
            @block.sync
            def _(sp):
                sp.wait_ge(core.stored, 16 * TT * (B + 1))


def layer0(core, b):
    weights_in = [core.sem(f"c_weights_loaded{i}") for i in range(2)]
    qkv_in = core.sem("d_weights_loaded")

    def first_experts(sp):
        for s in range(2):
            sp.dma_start(raw0(core)[s], core.dram["w_e0"][s]).then_inc(weights_in[s], 16)

    def qkv(sp):
        sp.dma_start(core.work[:, WQKV_AT:WQKV_AT + DC * 3072].rearrange("p (c n) -> p c n", c=DC),
                     core.dram["w_qkv"].rearrange("(c p) n -> p c n", p=P)).then_inc(qkv_in, 16)
        sp.wait_ge(qkv_in, 16)

    phase_attention(core, b)
    mlstm(core, 0, "b", 1e-6, first_experts)
    silu_experts(core, weights_in, qkv)


def layer1(core, b):
    weights_in = [core.sem(f"f_weights_loaded{i}") for i in range(4)]

    def first_experts(sp):
        for k in range(4):
            sp.dma_start(raw1(core)[k], core.dram["w_e1"][0][:, 2 * k * C1:2 * (k + 1) * C1]).then_inc(weights_in[k], 16)

    rope_attention(core)
    mlstm(core, 1, "e", 1e-5, first_experts)
    relu_experts(core, weights_in, b)


def _constants():
    i = np.arange(P)
    mask = np.where(i[None, :] > i[:, None], np.float32(NEG), np.float32(0)).astype(np.float32)
    c = {"ident": np.eye(P, dtype=np.float32), "mask": mask}
    c["maskT"] = mask.T
    sel = np.zeros((NH, NH, P), np.float32)
    for h in range(NH):
        sel[h, h] = 1.0
    c["sel"] = sel
    e = np.arange(8)
    c["tri"] = np.broadcast_to((e[None, :] < e[:, None]).astype(np.float32), (P, 8, 8)).copy()
    inv = (1.0 / np.float32(10000.0) ** (np.arange(0, HD1, 2, dtype=np.float32) / np.float32(HD1))).astype(np.float32)
    f = np.outer(np.arange(S, dtype=np.float32), inv).astype(np.float32)
    cos, sin = np.cos(f), np.sin(f)
    rope = np.stack([np.concatenate([cos, cos], 1), np.concatenate([-sin, sin], 1)], 1)
    c["rope"] = np.ascontiguousarray(rope.reshape(TT, P, 2, HD1).transpose(1, 0, 2, 3)).astype(np.float32)
    jj = np.repeat(np.arange(4), H1)
    c["dist_c"] = np.abs(np.arange(640)[None, :] - P - jj[:, None]).astype(np.float32)
    c["dist_r"] = np.abs(i[:, None] - np.arange(S)[None, :] + (S - P)).astype(np.float32)
    return c


def _block_diagonal(w, n):
    k, m = w.shape
    out = np.zeros((n * k, n * m), w.dtype)
    for i in range(n):
        out[i * k:(i + 1) * k, i * m:(i + 1) * m] = w
    return out


def _gate_columns(ig, fg):
    out = np.zeros((ig.shape[0], FG_ROW + NH), ig.dtype)
    out[:, 0:NH], out[:, FG_ROW:] = ig, fg
    return out


def _arrays(i):
    g = {k: np.asarray(v) for k, v in i.items()}
    a = dict(_constants())
    a["x"], a["ctx"] = np.concatenate([g["x"], g["x"][:1]], 0), g["ctx_1024"]
    a["wa"] = np.concatenate([g["L0_attn_" + n] for n in ("Wq", "Wk", "Wqp", "Wkp", "Wv")], 1)
    a["woa"] = g["L0_attn_Wo"]
    a["lambda"] = g["L0_attn_lambda_raw"]
    a["gate0"] = _gate_columns(g["L0_xattn_ig_kernel"], g["L0_xattn_fg_kernel"])
    a["gate_bias0"] = np.stack([g["L0_xattn_ig_bias"], g["L0_xattn_fg_bias"]], 1)
    a["norm_w0"] = g["L0_xattn_outnorm_weight"].reshape(-1)
    a["gate1"] = _gate_columns(g["L1_xattn_w_igate"].T, g["L1_xattn_w_fgate"].T)
    a["gate_bias1"] = np.stack([g["L1_xattn_b_igate"], g["L1_xattn_b_fgate"]], 1)
    a["norm_w1"] = g["L1_xattn_ln_weight"]
    a["wr0"] = g["L0_ffn_gate_w"].T
    a["rb0"] = g["L0_ffn_gate_b"]

    w1 = np.concatenate([g["L0_ffn_w1"], g["L0_ffn_ws1"].reshape(2, I0, D)], 0)
    w3 = np.concatenate([g["L0_ffn_w3"], g["L0_ffn_ws3"].reshape(2, I0, D)], 0)
    w2 = np.concatenate([g["L0_ffn_w2"], g["L0_ffn_ws2"].reshape(D, 2, I0).transpose(1, 0, 2)], 0)
    b1 = np.concatenate([g["L0_ffn_b1"], g["L0_ffn_bs1"].reshape(2, I0)], 0)
    b3 = np.concatenate([g["L0_ffn_b3"], g["L0_ffn_bs3"].reshape(2, I0)], 0)
    def columns(w, m):
        return w[:, m * P:(m + 1) * P].reshape(DC, P, P).transpose(1, 0, 2).reshape(P, -1)
    a["w_e0"] = np.stack([np.concatenate([x for m in range(I0 // P) for x in (
        columns(w1[e].T, m), columns(w3[e].T, m), w2[e].T[m * P:(m + 1) * P])], 1) for e in range(E0A)])
    a["b_e0"] = np.stack([np.concatenate([b1[e].reshape(2, P).T, b3[e].reshape(2, P).T], 1) for e in range(E0A)])
    a["b2"] = np.concatenate([g["L0_ffn_b2"], g["L0_ffn_bs2"][None], np.zeros((1, D), np.float32)], 0)
    a["w_qkv"] = g["L1_attn_w_qkv"]
    a["wo1"] = g["L1_attn_w_o"]
    a["log_p"], a["log_a"] = g["L1_attn_log_p"].reshape(-1), g["L1_attn_log_a"].reshape(-1)
    a["b2a"] = g["L1_attn_b2"]
    a["pa_col"] = np.stack([np.tile(a["log_p"], 4), np.tile(a["log_a"], 4)], 1)
    a["b1_col"] = np.tile(g["L1_attn_b1"], 4)[:, None]
    w1 = g["L1_attn_w1"]
    big = _block_diagonal(w1[0:H1], 8)
    a["w1s"] = np.stack([big[:, 0:P], big[:, P:2 * P]], 1)
    a["w1k"] = _block_diagonal(w1[H1:], 4)
    a["w2b"] = _block_diagonal(g["L1_attn_w2"], 4)
    a["wr1"] = g["L1_ffn_Wr"]
    a["w_e1"] = np.stack([np.concatenate([x for m in range(F1 // P) for x in (
        columns(g["L1_ffn_W1"][e], m), g["L1_ffn_W2"][e][m * P:(m + 1) * P])], 1) for e in range(E1)])
    return {k: np.ascontiguousarray(v) for k, v in a.items()}


def kernel(**inputs):
    import concourse.bacc as bacc
    from concourse.bass_utils import run_bass_kernel_spmd

    nc, arrays = _build(bacc, inputs)
    r = run_bass_kernel_spmd(nc, [arrays], core_ids=[0])
    return r.results[0]["out_dram"]


def _build(bacc, inputs):
    nc = bacc.Bacc("TRN2", target_bir_lowering=False, num_devices=1)
    arrays, dram = {}, {}
    for name, x in _arrays(inputs).items():
        arrays[f"in_{name}_dram"] = x
        dram[name] = nc.dram_tensor(f"in_{name}_dram", x.shape, mybir.dt.from_np(x.dtype), kind="ExternalInput").ap()
    dram["gates0"] = nc.dram_tensor("gates0_dram", (E0A, S), F32, kind="Internal").ap()
    dram["gates1"] = nc.dram_tensor("gates1_dram", (E1, S), F32, kind="Internal").ap()
    dram["out"] = nc.dram_tensor("out_dram", (B, S, D), F32, kind="ExternalOutput").ap()
    decoder(nc, dram)
    return nc, arrays
```
